# Optimizing a Trainium2 kernel written in Bass

```python
import numpy as np
import jax
import jax.numpy as jnp

def _softmax(x, axis=-1):
    return jax.nn.softmax(x, axis=axis)

def _gelu(x):
    return jax.nn.gelu(x, approximate=True)

def _silu(x):
    return jax.nn.silu(x)

def _sigmoid(x):
    return jax.nn.sigmoid(x)

def _layernorm(x, axis=-1, eps=1e-05):
    m = jnp.mean(x, axis=axis, keepdims=True)
    v = jnp.var(x, axis=axis, keepdims=True)
    return (x - m) / jnp.sqrt(v + eps)

def _scatter_add(tgt, idx, src, axis=0):
    return tgt.at[idx].add(src)

def _segment_sum(src, seg, n):
    return jax.ops.segment_sum(src, seg, n)
kernel_name = 'mk_seq_preln_d1_jaxref_r4_fee550'

def setup_inputs(seed: int=0):
    np.random.seed(seed)
    _w = jnp.asarray

    def _L0_attn_setup():
        import jax, jax.numpy as jnp
        import numpy as np
        B, N, D = (2, 256, 256)
        H = 4
        KD = 128
        VD = 256
        DK = KD // H
        DV = VD // H
        LR = 16
        GLN = 16.0
        EPS = 1e-05

        def _split_heads(t, h):
            b, n, hd = t.shape
            return t.reshape(b, n, h, hd // h).transpose(0, 2, 1, 3)

        def _gla_scan(q, k, v, g):
            b, h, n, dk = q.shape
            dv = v.shape[-1]
            qT = jnp.moveaxis(q, 2, 0)
            kT = jnp.moveaxis(k, 2, 0)
            vT = jnp.moveaxis(v, 2, 0)
            gT = jnp.moveaxis(g, 2, 0)

            def step(S, inp):
                qt, kt, vt, gt = inp
                S = S * jnp.exp(gt)[..., None] + kt[..., None] * vt[..., None, :]
                ot = jnp.einsum('bhk,bhkv->bhv', qt, S)
                return (S, ot)
            S0 = jnp.zeros((b, h, dk, dv), q.dtype)
            _, o = jax.lax.scan(step, S0, (qT, kT, vT, gT))
            return jnp.moveaxis(o, 0, 2)
        key = jax.random.key(seed)
        ks = jax.random.split(key, 10)
        s = 0.02
        return {'x': jax.random.normal(ks[0], (B, N, D), jnp.float32), 'Wq': jax.random.normal(ks[1], (D, KD), jnp.float32) * s, 'Wk': jax.random.normal(ks[2], (D, KD), jnp.float32) * s, 'Wv': jax.random.normal(ks[3], (D, VD), jnp.float32) * s, 'Wg': jax.random.normal(ks[4], (D, VD), jnp.float32) * s, 'Wgk1': jax.random.normal(ks[5], (D, LR), jnp.float32) * s, 'Wgk2': jax.random.normal(ks[6], (LR, KD), jnp.float32) * s, 'bgk2': jax.random.normal(ks[7], (KD,), jnp.float32) * s, 'Wout': jax.random.normal(ks[8], (VD, D), jnp.float32) * s, 'rms_w': jnp.ones((DV,), jnp.float32)}
    _L0_attn_in = _L0_attn_setup()

    def _L0_ffn_setup():
        import jax, jax.numpy as jnp
        import numpy as np
        EPS = 1e-05
        TOP_K = 2

        def _rmsnorm(x, w):
            xf = x.astype(jnp.float32)
            rms = jax.lax.rsqrt(jnp.mean(xf * xf, axis=-1, keepdims=True) + EPS)
            return (xf * rms).astype(x.dtype) * w

        def _attention(x, wq, wk, wv, wo, num_heads=16):
            B, S, H = x.shape
            D = H // num_heads
            q = (x @ wq.T).reshape(B, S, num_heads, D)
            k = (x @ wk.T).reshape(B, S, num_heads, D)
            v = (x @ wv.T).reshape(B, S, num_heads, D)
            scale = 1.0 / jnp.sqrt(jnp.float32(D)).astype(x.dtype)
            scores = jnp.einsum('bqhd,bkhd->bhqk', q, k) * scale
            probs = jax.nn.softmax(scores, axis=-1)
            out = jnp.einsum('bhqk,bkhd->bqhd', probs, v).reshape(B, S, H)
            return out @ wo.T

        def _moe(x, gate_w, w1, w2, w3):
            B, S, H = x.shape
            xf = x.reshape(-1, H)
            logits = xf @ gate_w.T
            rw, sel = jax.lax.top_k(logits, TOP_K)
            rw = jax.nn.softmax(rw.astype(jnp.float32), axis=-1).astype(x.dtype)
            E = gate_w.shape[0]
            out = jnp.zeros_like(xf)
            for e in range(E):
                we = jnp.sum(jnp.where(sel == e, rw, 0.0), axis=-1)
                h = jax.nn.silu(xf @ w1[e].T) * (xf @ w3[e].T)
                out = out + h @ w2[e].T * we[:, None]
            return out.reshape(B, S, H)
        key = jax.random.key(seed)
        ks = jax.random.split(key, 10)
        H, I, E, NH = (256, 512, 8, 16)
        B, S = (2, 512)
        s = 0.02
        return {'x': jax.random.normal(ks[0], (B, S, H), jnp.float32), 'ln1_w': jnp.ones((H,), jnp.float32), 'ln2_w': jnp.ones((H,), jnp.float32), 'wq': jax.random.normal(ks[1], (H, H), jnp.float32) * s, 'wk': jax.random.normal(ks[2], (H, H), jnp.float32) * s, 'wv': jax.random.normal(ks[3], (H, H), jnp.float32) * s, 'wo': jax.random.normal(ks[4], (H, H), jnp.float32) * s, 'gate_w': jax.random.normal(ks[5], (E, H), jnp.float32) * s, 'w1': jax.random.normal(ks[6], (E, I, H), jnp.float32) * s, 'w2': jax.random.normal(ks[7], (E, H, I), jnp.float32) * s, 'w3': jax.random.normal(ks[8], (E, I, H), jnp.float32) * s}
    _L0_ffn_in = _L0_ffn_setup()
    _d = {'L0_attn_x': _L0_attn_in['x'], 'L0_attn_Wq': _L0_attn_in['Wq'], 'L0_attn_Wk': _L0_attn_in['Wk'], 'L0_attn_Wv': _L0_attn_in['Wv'], 'L0_attn_Wg': _L0_attn_in['Wg'], 'L0_attn_Wgk1': _L0_attn_in['Wgk1'], 'L0_attn_Wgk2': _L0_attn_in['Wgk2'], 'L0_attn_bgk2': _L0_attn_in['bgk2'], 'L0_attn_Wout': _L0_attn_in['Wout'], 'L0_attn_rms_w': _L0_attn_in['rms_w'], 'L0_ffn_ln1_w': _L0_ffn_in['ln1_w'], 'L0_ffn_ln2_w': _L0_ffn_in['ln2_w'], 'L0_ffn_wq': _L0_ffn_in['wq'], 'L0_ffn_wk': _L0_ffn_in['wk'], 'L0_ffn_wv': _L0_ffn_in['wv'], 'L0_ffn_wo': _L0_ffn_in['wo'], 'L0_ffn_gate_w': _L0_ffn_in['gate_w'], 'L0_ffn_w1': _L0_ffn_in['w1'], 'L0_ffn_w2': _L0_ffn_in['w2'], 'L0_ffn_w3': _L0_ffn_in['w3']}
    _x0 = _d['L0_attn_x']
    _d['L0_attn_x'] = jax.random.normal(jax.random.fold_in(jax.random.key(seed), 1), (8, 1024, 256), dtype=_x0.dtype)
    del _x0
    return _d

def reference(L0_attn_x, L0_attn_Wq, L0_attn_Wk, L0_attn_Wv, L0_attn_Wg, L0_attn_Wgk1, L0_attn_Wgk2, L0_attn_bgk2, L0_attn_Wout, L0_attn_rms_w, L0_ffn_ln1_w, L0_ffn_ln2_w, L0_ffn_wq, L0_ffn_wk, L0_ffn_wv, L0_ffn_wo, L0_ffn_gate_w, L0_ffn_w1, L0_ffn_w2, L0_ffn_w3):

    def _L0_attn_ref(x, Wq, Wk, Wv, Wg, Wgk1, Wgk2, bgk2, Wout, rms_w):
        import jax, jax.numpy as jnp
        import numpy as np
        B, N, D = (2, 256, 256)
        H = 4
        KD = 128
        VD = 256
        DK = KD // H
        DV = VD // H
        LR = 16
        GLN = 16.0
        EPS = 1e-05

        def _split_heads(t, h):
            b, n, hd = t.shape
            return t.reshape(b, n, h, hd // h).transpose(0, 2, 1, 3)

        def _gla_scan(q, k, v, g):
            b, h, n, dk = q.shape
            dv = v.shape[-1]
            qT = jnp.moveaxis(q, 2, 0)
            kT = jnp.moveaxis(k, 2, 0)
            vT = jnp.moveaxis(v, 2, 0)
            gT = jnp.moveaxis(g, 2, 0)

            def step(S, inp):
                qt, kt, vt, gt = inp
                S = S * jnp.exp(gt)[..., None] + kt[..., None] * vt[..., None, :]
                ot = jnp.einsum('bhk,bhkv->bhv', qt, S)
                return (S, ot)
            S0 = jnp.zeros((b, h, dk, dv), q.dtype)
            _, o = jax.lax.scan(step, S0, (qT, kT, vT, gT))
            return jnp.moveaxis(o, 0, 2)
        q = _split_heads(x @ Wq, H)
        k = _split_heads(x @ Wk, H)
        v = _split_heads(x @ Wv, H)
        g = jax.nn.log_sigmoid(x @ Wgk1 @ Wgk2 + bgk2) / GLN
        g = jnp.maximum(g, -3.0)
        g = _split_heads(g, H)
        o = _gla_scan(q, k, v, g)
        o = o.transpose(0, 2, 1, 3)
        o = o * jax.lax.rsqrt(jnp.mean(o * o, axis=-1, keepdims=True) + EPS) * rms_w
        o = o.reshape(o.shape[0], o.shape[1], VD)
        o = o * jax.nn.silu(x @ Wg)
        return o @ Wout

    def _L0_ffn_ref(x, ln1_w, ln2_w, wq, wk, wv, wo, gate_w, w1, w2, w3):
        import jax, jax.numpy as jnp
        import numpy as np
        EPS = 1e-05
        TOP_K = 2

        def _rmsnorm(x, w):
            xf = x.astype(jnp.float32)
            rms = jax.lax.rsqrt(jnp.mean(xf * xf, axis=-1, keepdims=True) + EPS)
            return (xf * rms).astype(x.dtype) * w

        def _attention(x, wq, wk, wv, wo, num_heads=16):
            B, S, H = x.shape
            D = H // num_heads
            q = (x @ wq.T).reshape(B, S, num_heads, D)
            k = (x @ wk.T).reshape(B, S, num_heads, D)
            v = (x @ wv.T).reshape(B, S, num_heads, D)
            scale = 1.0 / jnp.sqrt(jnp.float32(D)).astype(x.dtype)
            scores = jnp.einsum('bqhd,bkhd->bhqk', q, k) * scale
            probs = jax.nn.softmax(scores, axis=-1)
            out = jnp.einsum('bhqk,bkhd->bqhd', probs, v).reshape(B, S, H)
            return out @ wo.T

        def _moe(x, gate_w, w1, w2, w3):
            B, S, H = x.shape
            xf = x.reshape(-1, H)
            logits = xf @ gate_w.T
            rw, sel = jax.lax.top_k(logits, TOP_K)
            rw = jax.nn.softmax(rw.astype(jnp.float32), axis=-1).astype(x.dtype)
            E = gate_w.shape[0]
            out = jnp.zeros_like(xf)
            for e in range(E):
                we = jnp.sum(jnp.where(sel == e, rw, 0.0), axis=-1)
                h = jax.nn.silu(xf @ w1[e].T) * (xf @ w3[e].T)
                out = out + h @ w2[e].T * we[:, None]
            return out.reshape(B, S, H)
        h = x + _attention(_rmsnorm(x, ln1_w), wq, wk, wv, wo)
        h = h + _moe(_rmsnorm(h, ln2_w), gate_w, w1, w2, w3)
        return h
    x = L0_attn_x
    x = x + _L0_attn_ref(_layernorm(x, axis=-1), L0_attn_Wq, L0_attn_Wk, L0_attn_Wv, L0_attn_Wg, L0_attn_Wgk1, L0_attn_Wgk2, L0_attn_bgk2, L0_attn_Wout, L0_attn_rms_w)
    x = x + _L0_ffn_ref(_layernorm(x, axis=-1), L0_ffn_ln1_w, L0_ffn_ln2_w, L0_ffn_wq, L0_ffn_wk, L0_ffn_wv, L0_ffn_wo, L0_ffn_gate_w, L0_ffn_w1, L0_ffn_w2, L0_ffn_w3)
    return x

_drawn_inputs = setup_inputs


def setup_inputs(seed=0):
    import zlib

    import numpy as np

    out = dict(_drawn_inputs(seed))
    spreads = {'L0_attn_rms_w': (1.0, 0.6), 'L0_ffn_ln1_w': (1.0, 0.6), 'L0_ffn_ln2_w': (1.0, 0.6)}
    factors = {'L0_attn_Wgk1': 8.0,
     'L0_attn_Wgk2': 8.0,
     'L0_attn_bgk2': 8.0,
     'L0_ffn_wq': 8.0,
     'L0_ffn_wk': 8.0,
     'L0_ffn_wv': 8.0,
     'L0_ffn_wo': 8.0,
     'L0_ffn_gate_w': 6.671,
     'L0_ffn_w1': 5.972,
     'L0_ffn_w2': 5.893,
     'L0_ffn_w3': 5.899}
    for name, (base, spread) in spreads.items():
        noise = np.random.default_rng([zlib.crc32(name.encode()), seed]).standard_normal(out[name].shape)
        drawn = base * np.exp(spread * noise) if base else spread * noise
        out[name] = jnp.asarray(drawn.astype(out[name].dtype))
    for name, factor in factors.items():
        out[name] = (out[name] * factor).astype(out[name].dtype)
    return out
```

```python
from contextlib import ExitStack

import concourse.bass as bass
from concourse import mybir


def stage_semaphore(nc, stage, name):
    sem = nc.alloc_semaphore(name)
    stage.semaphores.append(sem)
    return sem


class Stage(ExitStack):

    def __init__(self, nc):
        super().__init__()
        self.nc, self.semaphores = nc, []

    def __exit__(self, *error):
        ended = super().__exit__(*error)
        self.nc.all_engine_barrier()
        self.nc.clear_and_free_semaphores(self.semaphores)
        self.nc.all_engine_barrier()
        return ended


def gla_and_projections(nc, ctx, x, Wq, Wk, Wv, Wg, Wgk1, Wgk2, bgk2, Wout, rms_w,
                        ln1_w, wq, wk, wv, x1y_d, qk_d, v_d, n_batches=8):
    P, D, T = 128, 256, 4
    HT = P * T
    C = 32
    NC = HT // C
    H, DK, DV = 4, 32, 64
    EPS = 1e-5
    f32, f32r = mybir.dt.float32, mybir.dt.float32r
    ALU, ACT, AX = mybir.AluOpType, mybir.ActivationFunctionType, mybir.AxisListType

    def sb(name, shape, dt=f32):
        return ctx.enter_context(nc.sbuf_tensor("a_" + name, shape, dt))

    Wq_s, Wk_s = sb("Wq_s", [P, 2, 128]), sb("Wk_s", [P, 2, 128])
    Wvg_s = sb("Wvg_s", [P, 2, 512])
    Wgk1_s, Wgk2_s, bgk_s = sb("Wgk1_s", [P, 2, 16]), sb("Wgk2_s", [16, 128]), sb("bgk_s", [P, 1])
    Wout_s = sb("Wout_s", [P, 2, D])
    rmsw_s, ln1w_s = sb("rmsw_s", [P, 1]), sb("ln1w_s", [P, 2])
    w_raw = sb("w_raw", [P, 3, 2, D])
    wT = sb("wT", [P, 3, 2, D])
    ident, ones = sb("ident", [P, P]), sb("ones", [P, P])
    mask = sb("mask", [P, HT])
    maski = sb("maski", [P, HT], mybir.dt.int32)
    keep = sb("keep", [P, HT])
    xin = sb("xin", [P, 2, T, D])
    st6, mv = sb("st6", [P, T, 6]), sb("mv", [P, T, 2])
    rstd = sb("rstd", [P, T])
    xn = sb("xn", [P, T, D])
    xT = sb("xT", [P, 2, HT])
    q_s, k_s = sb("q_s", [P, HT]), sb("k_s", [P, HT])
    gk1 = sb("gk1", [16, HT])
    za, zm, cum = sb("za", [P, HT]), sb("zm", [P, HT]), sb("cum", [P, HT])
    rel, tail = sb("rel", [P, HT]), sb("tail", [P, HT])
    e_in, e_out, e_cum, e_tail = (sb(f"e_{n}", [P, HT]) for n in ("in", "out", "cum", "tail"))
    decay = sb("decay", [P, NC])
    qt, kt, qh, kh = (sb(n, [P, HT]) for n in ("qt", "kt", "qh", "kh"))
    khat = sb("khat", [P, T, P])
    V, G = sb("V", [P, T, D]), sb("G", [P, T, D])
    eg = sb("eg", [P, T, D])
    AT = sb("AT", [P, H, HT])
    S = sb("S", [P, NC + 1, DV])
    Sbd = sb("Sbd", [P, NC, D])
    o_s, o2 = sb("o_s", [P, T, D]), sb("o2", [P, T, D])
    ss, rs = sb("ss", [P, T * H]), sb("rs", [P, T * H])
    ogT = sb("ogT", [P, 2, HT])
    x1y = sb("x1y", [P, T, 2, D])
    st6b, mvb, rstdb = sb("st6b", [P, T, 6]), sb("mvb", [P, T, 2]), sb("rstdb", [P, T])
    sq, ssy, ry = sb("sq", [P, D]), sb("ssy", [P, T]), sb("ry", [P, T])
    xr = sb("xr", [P, T, D])
    xrT = sb("xrT", [P, 2, HT])
    hi, lo = sb("hi", [P, 4, HT], f32r), sb("lo", [P, 4, HT], f32r)
    v_s = sb("v_s", [P, 8, T, 64])
    mhalf = sb("mhalf", [P, T * H])
    p_tr = ctx.enter_context(nc.psum_tensor("a_p_tr", [P, 2, 512], f32))
    p_a = ctx.enter_context(nc.psum_tensor("a_p_a", [P, 4, 512], f32))
    p_b = ctx.enter_context(nc.psum_tensor("a_p_b", [P, 2, 512], f32))

    names = ("w_in", "consts0", "consts", "wT_ps", "wT_done", "x_in0", "x_in1", "x_free", "st_done", "mv_done", "rstd_done",
             "xn_done", "xT_ps", "xT_done", "qkg_ps", "gk1_done", "qk_done", "z_ps", "za_done", "e_z", "l_z", "zm_done",
             "g0", "g1", "cum_done", "rel_done", "tail_done", "exps", "qtkt", "hats", "khT_ps", "khat_done", "vg_ps",
             "vg_taken", "eg0", "eg1", "eg2", "sg_done", "AT_ps", "AT_done", "inc_ps", "S_step", "S_carry", "Sbd_done", "o_ps",
             "o_s_done", "o2_done", "ss_done", "rs0", "rs_done", "on_done", "og_done", "ogT_ps", "ogT_done", "wout_ps",
             "x1_done", "stb_done", "mvb_done", "rstdb_done", "y_done", "sq_done", "ry_done", "xr_done", "xrT_ps", "xrT_done",
             "qk2_ps", "hi_done", "lo_done", "v2_ps", "v_done", "rstd_eps", "rs_eps", "rstdb_eps", "ry_eps", "stored", "store_free", "zero",
             "dve_turn", "pe_turn", "pool_turn")
    s = {n: stage_semaphore(nc, ctx, "a_" + n) for n in names}

    x_v = x.rearrange("(n t p) d -> n p t d", p=P, t=T)
    x1y_v = x1y_d.rearrange("(n t p) e d -> n p t e d", p=P, t=T)
    qk_v = qk_d.rearrange("w c (b m p) t -> w c b p m t", m=2, p=P)

    block = ctx.enter_context(nc.Block())

    @block.sync
    def _(sp):
        two = lambda w: w.rearrange("(k p) n -> p k n", p=P)
        loads = [(Wq_s[:], two(Wq)), (Wk_s[:], two(Wk)), (Wvg_s[:, :, 0:D], two(Wv)), (Wvg_s[:, :, D:2 * D], two(Wg)),
                 (Wgk1_s[:], two(Wgk1)), (Wgk2_s[:], Wgk2), (bgk_s[:], bgk2.rearrange("(p o) -> p o", o=1)),
                 (Wout_s[:], two(Wout)), (rmsw_s[0:64, :], rms_w.rearrange("(p o) -> p o", o=1)),
                 (rmsw_s[64:128, :], rms_w.rearrange("(p o) -> p o", o=1)),
                 (w_raw[:, 0], two(wq)), (w_raw[:, 1], two(wk)), (w_raw[:, 2], two(wv))]
        for dst, src in loads:
            sp.dma_start(dst, src).then_inc(s["w_in"], 16)
        with nc.allow_non_contiguous_dma("256 weights, once"):
            sp.dma_start(ln1w_s[:], ln1_w.rearrange("(k p) -> p k", p=P)).then_inc(s["w_in"], 16)
        with sp.Fori(0, n_batches) as b:
            for half in (0, 1):
                n = b * 2 + half
                sp.wait_ge(s["x1_done"], n + 1)
                sp.dma_start(xin[:, half], x_v[n]).then_inc(s[f"x_in{half}"], 16)

    @block.scalar
    def _(act):
        with act.Fori(0, n_batches) as b:
            for half in (0, 1):
                n = b * 2 + half
                n1 = n + 1
                act.wait_ge(s["xT_ps"], n1)
                nc.scalar.copy(xT[:], p_tr[:]).then_inc(s["xT_done"], 1)
                act.wait_ge(s["qkg_ps"], n1)
                nc.scalar.copy(gk1[:], p_a[0:16, 2, :]).then_inc(s["gk1_done"], 1)
                nc.scalar.copy(q_s[:], p_a[:, 0, :])
                nc.scalar.copy(k_s[:], p_a[:, 1, :]).then_inc(s["qk_done"], 1)
                for t in range(T):
                    act.wait_ge(s["vg_ps"], n * T + (t + 1))
                    nc.scalar.copy(V[:, t], p_b[:, t % 2, 0:D])
                    nc.scalar.copy(G[:, t], p_b[:, t % 2, D:2 * D]).then_inc(s["vg_taken"], 1)
                act.wait_ge(s["z_ps"], n1)
                nc.scalar.activation(za[:], p_a[:, 3, :], ACT.Abs, bias=bgk_s[:, 0:1]).then_inc(s["za_done"], 1)
                act.wait_ge(s["za_done"], n1)
                nc.scalar.activation(e_in[:], za[:], ACT.Exp, scale=-1.0).then_inc(s["e_z"], 1)
                act.wait_ge(s["e_z"], n1)
                nc.scalar.activation(za[:], e_in[:], ACT.Ln, bias=ones[:, 0:1]).then_inc(s["l_z"], 1)
                act.wait_ge(s["vg_taken"], n * T + T)
                nc.scalar.activation(eg[:], G[:], ACT.Exp, scale=-1.0).then_inc(s["eg0"], 1)
                act.wait_ge(s["tail_done"], n1)
                nc.scalar.activation(e_in[:], rel[:], ACT.Exp)
                nc.scalar.activation(e_out[:], rel[:], ACT.Exp, scale=-1.0)
                nc.scalar.activation(e_cum[:], cum[:], ACT.Exp)
                nc.scalar.activation(e_tail[:], tail[:], ACT.Exp)
                nc.scalar.activation(decay[:], cum[:].rearrange("p (c j) -> p c j", j=C)[:, :, C - 1], ACT.Exp).then_inc(s["exps"], 1)
                act.wait_ge(s["khT_ps"], n1)
                nc.scalar.copy(khat[:], p_tr[:, 0].rearrange("p (t c) -> p t c", t=T)).then_inc(s["khat_done"], 1)
                act.wait_ge(s["S_step"], n * NC + NC)
                for h in range(H):
                    i = nc.scalar.copy(Sbd[h * DK:(h + 1) * DK, :, h * DV:(h + 1) * DV], S[h * DK:(h + 1) * DK, 0:NC, :])
                i.then_inc(s["Sbd_done"], 1)
                act.wait_ge(s["o_ps"], n1)
                nc.scalar.copy(o_s[:].rearrange("p t d -> p (t d)"), p_b[:].rearrange("p a c -> p (a c)")).then_inc(s["o_s_done"], 1)
                nc.scalar.activation(o2[:].rearrange("p t d -> p (t d)"), p_b[:].rearrange("p a c -> p (a c)"), ACT.Square, scale=DV ** -0.5).then_inc(s["o2_done"], 1)
                act.wait_ge(s["ogT_ps"], n1)
                nc.scalar.mul(ogT[:], p_tr[:], rmsw_s[:, 0:1]).then_inc(s["ogT_done"], 1)
                act.wait_ge(s["y_done"], n1)
                for t in range(T):
                    act.wait_ge(s["sq_done"], n * T + (t + 1))
                    nc.scalar.activation(sq[:], x1y[:, t, 1], ACT.Square, scale=D ** -0.5, accum_out=ssy[:, t:t + 1]).then_inc(s["sq_done"], 1)
                act.wait_ge(s["xrT_ps"], n1)
                nc.scalar.mul(xrT[:, 0], p_tr[:, 0], ln1w_s[:, 0:1])
                nc.scalar.mul(xrT[:, 1], p_tr[:, 1], ln1w_s[:, 1:2]).then_inc(s["xrT_done"], 1)
                act.wait_ge(s["store_free"], n1)
                for j in range(4):
                    act.wait_ge(s["qk2_ps"], n * 4 + (j + 1))
                    nc.scalar.copy(hi[:, j], p_a[:, j]).then_inc(s["hi_done"], 1)
                act.wait_ge(s["v2_ps"], n1)
                for t in range(T):
                    i = nc.scalar.copy(v_s[:, :, t, :].rearrange("p a (h e) -> p a h e", h=2)[:, :, :, 0:16],
                                       p_b[:, t // 2, (t % 2) * D:(t % 2 + 1) * D].rearrange("p (a h e) -> p a h e", a=8, h=2))
                i.then_inc(s["v_done"], 1)

    @block.vector
    def _(dve):
        V_ = nc.vector
        V_.memset(ones[:], 1.0)
        V_.memset(v_s[:], 1.0)
        V_.memset(AT[:], 0.0)
        V_.memset(Sbd[:], 0.0)
        V_.memset(keep[:], 1.0).then_inc(s["consts0"], 1)
        dve.wait_ge(s["consts0"], 2)
        V_.memset(keep[:].rearrange("p (c j) -> p c j", j=C)[:, :, 0:1], 0.0)
        V_.tensor_copy(maski[:], mask[:]).then_inc(s["consts"], 1)
        dve.wait_ge(s["consts"], 1)
        for j in range(3):
            dve.wait_ge(s["wT_ps"], j + 1)
            V_.tensor_copy(wT[:, j].rearrange("p k m -> p (k m)"), p_a[:, j]).then_inc(s["wT_done"], 1)
        dve.sem_inc(s["x1_done"], 2)
        dve.sem_inc(s["sq_done"], 1)
        dve.sem_inc(s["store_free"], 1)
        dve.sem_inc(s["lo_done"], 1)
        dve.sem_inc(s["v_done"], 1)
        with dve.Fori(0, n_batches) as b:
            for half in (0, 1):
                n = b * 2 + half
                n1 = n + 1
                dve.wait_ge(s[f"x_in{half}"], b * 16 + 16)
                for t in range(T):
                    i = V_.bn_stats(st6[:, t], xin[:, half, t])
                i.then_inc(s["st_done"], 1)
                dve.wait_ge(s["st_done"], n1)
                dve.sem_inc(s["dve_turn"], 1)
                for t in range(T):
                    i = V_.bn_aggr(mv[:, t], st6[:, t])
                i.then_inc(s["mv_done"], 1)
                dve.wait_ge(s["rstd_done"], n1)
                for t in range(T):
                    i = V_.tensor_scalar(xn[:, t], xin[:, half, t], mv[:, t, 0:1], rstd[:, t:t + 1], ALU.subtract, ALU.mult)
                i.then_inc(s["xn_done"], 1)
                dve.wait_ge(s["z_ps"], n1)
                dve.wait_ge(s["za_done"], n1)
                V_.tensor_scalar(zm[:], p_a[:, 3, :], bgk_s[:, 0:1], 0.0, ALU.add, ALU.min).then_inc(s["zm_done"], 1)
                dve.wait_ge(s["l_z"], n1)
                dve.wait_ge(s["zm_done"], n1)
                V_.tensor_tensor(zm[:], zm[:], za[:], ALU.subtract).then_inc(s["g0"], 1)
                dve.wait_ge(s["g0"], n1)
                V_.tensor_scalar(zm[:], zm[:], 1.0 / 16.0, -3.0, ALU.mult, ALU.max).then_inc(s["g1"], 1)
                dve.wait_ge(s["g1"], n1)
                V_.tensor_tensor_scan(cum[:], keep[:], zm[:], 0.0, ALU.mult, ALU.add).then_inc(s["cum_done"], 1)
                dve.wait_ge(s["cum_done"], n1)
                cc = cum[:].rearrange("p (c j) -> p c j", j=C)
                V_.tensor_tensor(rel[:].rearrange("p (c j) -> p c j", j=C), cc,
                                 cc[:, :, C // 2 - 1:C // 2].to_broadcast([P, NC, C]), ALU.subtract)
                V_.tensor_tensor(tail[:].rearrange("p (c j) -> p c j", j=C),
                                 cc[:, :, C - 1:C].to_broadcast([P, NC, C]), cc, ALU.subtract).then_inc(s["tail_done"], 1)
                dve.wait_ge(s["eg0"], n1)
                V_.tensor_scalar(eg[:], eg[:], 1.0, None, ALU.add).then_inc(s["eg1"], 1)
                dve.wait_ge(s["eg1"], n1)
                V_.reciprocal(eg[:], eg[:]).then_inc(s["eg2"], 1)
                dve.wait_ge(s["qk_done"], n1)
                dve.wait_ge(s["exps"], n1)
                V_.tensor_tensor(qt[:], q_s[:], e_in[:], ALU.mult)
                V_.tensor_tensor(kt[:], k_s[:], e_out[:], ALU.mult).then_inc(s["qtkt"], 1)
                dve.wait_ge(s["eg2"], n1)
                V_.tensor_tensor(G[:], G[:], eg[:], ALU.mult).then_inc(s["sg_done"], 1)
                dve.wait_ge(s["AT_ps"], n1)
                dve.sem_inc(s["dve_turn"], 1)
                for h in range(H):
                    i = V_.copy_predicated(AT[:, h], maski[:], p_a[:, h])
                i.then_inc(s["AT_done"], 1)
                dve.wait_ge(s["inc_ps"], n1)
                for c in range(NC):
                    if c > 0:
                        dve.wait_ge(s["S_step"], n * NC + c)
                    elif half == 1:
                        dve.wait_ge(s["S_carry"], n1)
                    else:
                        V_.memset(S[:, 0], 0.0).then_inc(s["S_carry"], 1)
                        dve.wait_ge(s["S_carry"], n1)
                    V_.scalar_tensor_tensor(S[:, c + 1], S[:, c], decay[:, c:c + 1], p_a[:, c % 4, (c // 4) * DV:(c // 4 + 1) * DV],
                                            ALU.mult, ALU.add).then_inc(s["S_step"], 1)
                dve.wait_ge(s["S_step"], n * NC + NC)
                dve.wait_ge(s["Sbd_done"], n1)
                if half == 0:
                    V_.tensor_copy(S[:, 0], S[:, NC]).then_inc(s["S_carry"], 1)
                dve.wait_ge(s["o2_done"], n1)
                V_.reduce_sum(ss[:], o2[:].rearrange("p t (h v) -> p (t h) v", h=H), AX.X).then_inc(s["ss_done"], 1)
                dve.wait_ge(s["rs_done"], n1)
                ov = o_s[:].rearrange("p t (h v) -> p (t h) v", h=H)
                V_.tensor_tensor(ov, ov, rs[:].rearrange("p (a o) -> p a o", o=1).to_broadcast([P, T * H, DV]), ALU.mult).then_inc(s["on_done"], 1)
                dve.wait_ge(s["on_done"], n1)
                V_.tensor_tensor(o_s[:], o_s[:], G[:], ALU.mult).then_inc(s["og_done"], 1)
                dve.wait_ge(s["wout_ps"], n1)
                dve.wait_ge(s["store_free"], n1)
                V_.tensor_tensor(x1y[:, :, 0], p_b[:].rearrange("p a (e c) -> p (a e) c", e=2), xin[:, half], ALU.add).then_inc(s["x1_done"], 1)
                dve.wait_ge(s["x1_done"], n + 3)
                for t in range(T):
                    i = V_.bn_stats(st6b[:, t], x1y[:, t, 0])
                i.then_inc(s["stb_done"], 1)
                dve.wait_ge(s["stb_done"], n1)
                dve.sem_inc(s["dve_turn"], 1)
                for t in range(T):
                    i = V_.bn_aggr(mvb[:, t], st6b[:, t])
                i.then_inc(s["mvb_done"], 1)
                dve.wait_ge(s["rstdb_done"], n1)
                for t in range(T):
                    i = V_.tensor_scalar(x1y[:, t, 1], x1y[:, t, 0], mvb[:, t, 0:1], rstdb[:, t:t + 1], ALU.subtract, ALU.mult)
                i.then_inc(s["y_done"], 1)
                dve.wait_ge(s["ry_done"], n1)
                for t in range(T):
                    i = V_.tensor_scalar(xr[:, t], x1y[:, t, 1], ry[:, t:t + 1], None, ALU.mult)
                i.then_inc(s["xr_done"], 1)
                for j in range(4):
                    dve.wait_ge(s["hi_done"], n * 4 + (j + 1))
                    V_.tensor_tensor(lo[:, j], p_a[:, j], hi[:, j].bitcast(f32), ALU.subtract).then_inc(s["lo_done"], 1)

    @block.gpsimd
    def _(pool):
        g = nc.gpsimd
        g.memset(ident[:], 0.0)
        g.memset(mhalf[:], -0.5)
        g.memset(mask[:], 1.0).then_inc(s["zero"], 1)
        pool.wait_ge(s["zero"], 1)
        g.affine_select(out=ident[:], in_=ident[:], compare_op=ALU.not_equal, fill=1.0, base=0, pattern=[[-1, P]], channel_multiplier=1)
        m4 = mask[:].rearrange("p (t c j) -> p t c j", c=4, j=C)
        g.affine_select(out=m4, in_=m4, compare_op=ALU.is_ge, fill=0.0, base=0, pattern=[[0, T], [-C, 4], [0, C]], channel_multiplier=1).then_inc(s["zero"], 1)
        pool.wait_ge(s["zero"], 2)
        g.affine_select(out=m4, in_=m4, compare_op=ALU.is_ge, fill=0.0, base=0, pattern=[[0, T], [C, 4], [1, C]], channel_multiplier=-1).then_inc(s["consts0"], 1)
        with pool.Fori(0, n_batches) as b:
            for half in (0, 1):
                n = b * 2 + half
                n1 = n + 1
                pool.wait_ge(s["mv_done"], n1)
                pool.sem_inc(s["pool_turn"], 1)
                g.tensor_scalar(rstd[:], mv[:, :, 1], EPS, None, ALU.add).then_inc(s["rstd_eps"], 1)
                pool.wait_ge(s["rstd_eps"], n1)
                g.tensor_tensor(rstd[:], rstd[:], mhalf[:, 0:T], ALU.pow).then_inc(s["rstd_done"], 1)
                pool.wait_ge(s["qk_done"], n1)
                pool.wait_ge(s["exps"], n1)
                g.tensor_tensor(kh[:], k_s[:], e_tail[:], ALU.mult)
                g.tensor_tensor(qh[:], q_s[:], e_cum[:], ALU.mult).then_inc(s["hats"], 1)
                pool.wait_ge(s["ss_done"], n1)
                pool.sem_inc(s["pool_turn"], 1)
                g.tensor_scalar(rs[:], ss[:], EPS, None, ALU.add).then_inc(s["rs_eps"], 1)
                pool.wait_ge(s["rs_eps"], n1)
                g.tensor_tensor(rs[:], rs[:], mhalf[:, 0:T * H], ALU.pow).then_inc(s["rs_done"], 1)
                pool.wait_ge(s["mvb_done"], n1)
                pool.sem_inc(s["pool_turn"], 1)
                g.tensor_scalar(rstdb[:], mvb[:, :, 1], EPS, None, ALU.add).then_inc(s["rstdb_eps"], 1)
                pool.wait_ge(s["rstdb_eps"], n1)
                g.tensor_tensor(rstdb[:], rstdb[:], mhalf[:, 0:T], ALU.pow).then_inc(s["rstdb_done"], 1)
                pool.wait_ge(s["sq_done"], n * T + (T + 1))
                pool.sem_inc(s["pool_turn"], 1)
                g.tensor_scalar(ry[:], ssy[:], EPS, None, ALU.add).then_inc(s["ry_eps"], 1)
                pool.wait_ge(s["ry_eps"], n1)
                g.tensor_tensor(ry[:], ry[:], mhalf[:, 0:T], ALU.pow).then_inc(s["ry_done"], 1)
                pool.wait_ge(s["y_done"], n1)
                g.dma_start(x1y_v[n], x1y[:]).then_inc(s["stored"], 16)
                pool.wait_ge(s["v_done"], n + 2)
                g.dma_start(v_d[b, :, :, half * T:(half + 1) * T, :].rearrange("a p t e -> p a (t e)"), v_s[:].rearrange("p a t e -> p a (t e)")).then_inc(s["stored"], 16)
                pool.wait_ge(s["lo_done"], n * 4 + 5)
                for part, buf in ((0, hi), (1, lo)):
                    for which in (0, 1):
                        g.dma_start(qk_v[which, part, b, :, :, half * HT:(half + 1) * HT],
                                    buf[:, 2 * which:2 * which + 2, :].bitcast(f32)).then_inc(s["stored"], 16)
                pool.wait_ge(s["stored"], n * 96 + 96)
                pool.sem_inc(s["store_free"], 1)

    @block.tensor
    def _(pe):
        mm, tr = nc.tensor.matmul, nc.tensor.transpose
        pe.wait_ge(s["w_in"], 14 * 16)
        pe.wait_ge(s["consts"], 1)
        for j in range(3):
            for k in range(2):
                for m in range(2):
                    i = tr(p_a[:, j, k * D + m * P:k * D + (m + 1) * P], w_raw[:, j, m, k * P:(k + 1) * P], ident[:])
            i.then_inc(s["wT_ps"], 1)
        pe.wait_ge(s["wT_done"], 3)
        with pe.Fori(0, n_batches) as b:
            for half in (0, 1):
                n = b * 2 + half
                n1 = n + 1

                def transposes(src, done):
                    for t in range(T):
                        for k in range(2):
                            i = tr(p_tr[:, k, t * P:(t + 1) * P], src[:, t, k * P:(k + 1) * P], ident[:])
                    i.then_inc(done, 1)

                pe.wait_ge(s["xn_done"], n1)
                transposes(xn, s["xT_ps"])
                pe.wait_ge(s["xT_done"], n1)
                pe.wait_ge(s["lo_done"], n * 4 + 1)
                for bank, w, m in ((2, Wgk1_s, 16), (0, Wq_s, P), (1, Wk_s, P)):
                    for k in range(2):
                        i = mm(p_a[0:m, bank, :], w[:, k, :], xT[:, k, :], start=(k == 0), stop=(k == 1))
                i.then_inc(s["qkg_ps"], 1)
                for t in range(T):
                    if t >= 2:
                        pe.wait_ge(s["vg_taken"], n * T + (t - 1))
                    elif t == 0:
                        pe.wait_ge(s["v_done"], n1)
                    for k in range(2):
                        i = mm(p_b[:, t % 2, :], xT[:, k, t * P:(t + 1) * P], Wvg_s[:, k, :], start=(k == 0), stop=(k == 1))
                    i.then_inc(s["vg_ps"], 1)
                pe.wait_ge(s["gk1_done"], n1)
                mm(p_a[:, 3, :], Wgk2_s[:], gk1[:], start=True, stop=True).then_inc(s["z_ps"], 1)
                pe.wait_ge(s["qtkt"], n1)
                for h in range(H):
                    r = slice(h * DK, (h + 1) * DK)
                    for t in range(T):
                        i = mm(p_a[:, h, t * P:(t + 1) * P], kt[r, t * P:(t + 1) * P], qt[r, t * P:(t + 1) * P], start=True, stop=True)
                i.then_inc(s["AT_ps"], 1)
                pe.wait_ge(s["hats"], n1)
                for t in range(T):
                    i = tr(p_tr[:, 0, t * P:(t + 1) * P], kh[:, t * P:(t + 1) * P], ident[:])
                i.then_inc(s["khT_ps"], 1)
                pe.wait_ge(s["AT_done"], n1)
                pe.wait_ge(s["khat_done"], n1)
                pe.sem_inc(s["pe_turn"], 1)
                for t in range(T):
                    for c in range(4):
                        for h in range(H):
                            r = slice(c * C, (c + 1) * C)
                            i = mm(p_a[h * DK:(h + 1) * DK, c, t * DV:(t + 1) * DV], khat[r, t, h * DK:(h + 1) * DK],
                                   V[r, t, h * DV:(h + 1) * DV], start=True, stop=True)
                i.then_inc(s["inc_ps"], 1)
                pe.wait_ge(s["Sbd_done"], n1)
                pe.wait_ge(s["vg_taken"], n * T + T)
                for t in range(T):
                    bank, at = t // 2, (t % 2) * D
                    for c in range(4):
                        mm(p_b[c * C:(c + 1) * C, bank, at:at + D], qh[:, t * P + c * C:t * P + (c + 1) * C], Sbd[:, t * 4 + c, :],
                           start=True, stop=False, skip_group_check=True)
                    for h in range(H):
                        i = mm(p_b[:, bank, at + h * DV:at + (h + 1) * DV], AT[:, h, t * P:(t + 1) * P], V[:, t, h * DV:(h + 1) * DV],
                               start=False, stop=True, skip_group_check=True)
                i.then_inc(s["o_ps"], 1)
                pe.wait_ge(s["og_done"], n1)
                transposes(o_s, s["ogT_ps"])
                pe.wait_ge(s["ogT_done"], n1)
                for t in range(T):
                    bank, at = t // 2, (t % 2) * D
                    for k in range(2):
                        i = mm(p_b[:, bank, at:at + D], ogT[:, k, t * P:(t + 1) * P], Wout_s[:, k, :], start=(k == 0), stop=(k == 1))
                i.then_inc(s["wout_ps"], 1)
                pe.wait_ge(s["xr_done"], n1)
                transposes(xr, s["xrT_ps"])
                pe.wait_ge(s["xrT_done"], n1)
                for j in range(4):
                    for k in range(2):
                        i = mm(p_a[:, j, :], wT[:, j // 2, k, (j % 2) * P:(j % 2 + 1) * P], xrT[:, k, :], start=(k == 0), stop=(k == 1))
                    i.then_inc(s["qk2_ps"], 1)
                for t in range(T):
                    bank, at = t // 2, (t % 2) * D
                    for k in range(2):
                        i = mm(p_b[:, bank, at:at + D], xrT[:, k, t * P:(t + 1) * P], wT[:, 2, k, :], start=(k == 0), stop=(k == 1))
                i.then_inc(s["v2_ps"], 1)


def softmax_attention(nc, ctx, qk_d, v_d, o_d, n_batches=8):
    P, N, KT = 128, 1024, 8
    R = 64
    RING = 4
    PAIRS = 8 * n_batches
    f32, f32r = mybir.dt.float32, mybir.dt.float32r
    ALU, ACT, AX = mybir.AluOpType, mybir.ActivationFunctionType, mybir.AxisListType
    SCALE = 0.25

    def sb(name, shape, dt=f32):
        return ctx.enter_context(nc.sbuf_tensor("b_" + name, shape, dt))

    def sem(name):
        return stage_semaphore(nc, ctx, "b_" + name)

    qst = [sb(f"qst{r}", [P, N], f32r) for r in range(RING)]
    kst = [[sb(f"kst{r}_{h}", [P, N], f32r) for h in range(2)] for r in range(RING)]
    vst = [sb(f"vst{r}", [P, KT, 2, 32]) for r in range(RING)]
    ones, zrow = sb("ones", [2, N]), sb("zrow", [2, N])
    ident = sb("ident", [P, P])
    mx, mxq = sb("mx", [P, 16, 2]), sb("mxq", [P, 16])
    nm_hi, nm_lo = [sb(f"nm_hi{r}", [16, P], f32r) for r in range(2)], [sb(f"nm_lo{r}", [16, P], f32r) for r in range(2)]
    probs = [sb(f"probs{r}", [P, N]) for r in range(4)]
    oT = sb("oT", [P, 512])
    rden = sb("rden", [P, 4, 4])
    o_s = [sb(f"o_s{r}", [P, KT, 2, 16]) for r in range(2)]
    p_e = [ctx.enter_context(nc.psum_tensor(f"b_p_e{r}", [P, N], f32)) for r in range(2)]
    p_m = [ctx.enter_context(nc.psum_tensor(f"b_p_m{r}", [P, 512], f32)) for r in range(2)]
    p_o = ctx.enter_context(nc.psum_tensor("b_p_o", [P, 512], f32))
    p_t = ctx.enter_context(nc.psum_tensor("b_p_t", [P, 4, P], f32))

    names = ("consts", "ident0", "id", "rows", "free", "m_ps", "m_red", "mxq_done", "mT_ps", "mT_read", "nm_done",
             "e_ps", "e_done", "pv_done", "oT_done", "oT_ps", "rden_done", "o_done", "o_stored", "o_free",
             *(f"q_in{r}" for r in range(RING)), *(f"m_in{r}" for r in range(RING)), "start")
    s = {n: sem(n) for n in names}
    q_rows = qk_d.rearrange("w c (g r) t -> g w c r t", r=32)
    v_rows = v_d.rearrange("b a p t e -> (b a) p (t e)")
    o_rows = o_d.rearrange("b a p t e -> (b a) p (t e)")
    LOADS = 15
    STEPS = PAIRS // RING

    def pairs(eng, body):
        with eng.Fori(0, STEPS - 1) as i:
            for r in range(RING):
                body(i * RING + r, i, r, True, True)
        for r in range(RING):
            body((STEPS - 1) * RING + r, STEPS - 1, r, r < RING - 2, r < RING - 3)

    def ahead(i, r):
        return (i + 1, r - 2) if r >= 2 else (i, r + 2)

    block = ctx.enter_context(nc.Block())

    @block.sync
    def _(sp):
        sp.wait_ge(s["consts"], 1)
        for r in range(RING):
            for h in range(2):
                sp.dma_start(kst[r][h][R * h + 48:R * h + 50, :].bitcast(f32), ones[:]).then_inc(s["rows"], 16)

        def load(pair, r):
            for h in range(2):
                at, row = R * h, 16 * h
                sp.dma_start(qst[r][at:at + 16, :].bitcast(f32), q_rows[pair, 0, 0, row:row + 16, :]).then_inc(s[f"q_in{r}"], 16)
                sp.dma_start(qst[r][at + 16:at + 32, :].bitcast(f32), q_rows[pair, 0, 1, row:row + 16, :]).then_inc(s[f"q_in{r}"], 16)
                sp.dma_start(qst[r][at + 32:at + 48, :].bitcast(f32), q_rows[pair, 0, 0, row:row + 16, :]).then_inc(s[f"q_in{r}"], 16)
                sp.dma_start(kst[r][h][at:at + 16, :].bitcast(f32), q_rows[pair, 1, 0, row:row + 16, :]).then_inc(s[f"q_in{r}"], 16)
                sp.dma_start(kst[r][h][at + 16:at + 32, :].bitcast(f32), q_rows[pair, 1, 0, row:row + 16, :]).then_inc(s[f"q_in{r}"], 16)
                sp.dma_start(kst[r][h][at + 32:at + 48, :].bitcast(f32), q_rows[pair, 1, 1, row:row + 16, :]).then_inc(s[f"q_in{r}"], 16)
                sp.dma_start(qst[r][at + 48:at + 50, :].bitcast(f32), zrow[:]).then_inc(s[f"q_in{r}"], 16)
            sp.dma_start(vst[r][:].rearrange("p t h e -> p (t h e)"), v_rows[pair]).then_inc(s[f"q_in{r}"], 16)

        def maxima(pair, half, r):
            sp.wait_ge(s["nm_done"], (pair + 1) * 1)
            for h in range(2):
                for k, nm in enumerate((nm_hi[half], nm_lo[half])):
                    sp.dma_start(qst[r][R * h + 48 + k:R * h + 49 + k, :].bitcast(f32).rearrange("o (c j) -> o c j", c=8),
                                 nm[8 * h:8 * h + 8, :].bitcast(f32)).then_inc(s[f"m_in{r}"], 16)

        for r in range(3):
            load(r, r)
        maxima(0, 0, 0)
        maxima(1, 1, 1)

        def body(pair, i, r, more, more3):
            if more3:
                sp.wait_ge(s["pv_done"], pair * KT + 2)
                load(pair + 3, (r + 3) % RING)
            if more:
                maxima(pair + 2, r % 2, (r + 2) % RING)
        pairs(sp, body)

    @block.scalar
    def _(act):
        def negated(pair, half):
            act.wait_ge(s["mT_ps"], pair + 1)
            nc.scalar.mul(nm_hi[half][:], p_t[0:16, 0, :], -1.0).then_inc(s["mT_read"], 1)

        negated(0, 0)
        negated(1, 1)

        def body(pair, i, r, more, more3):
            for e in range(2 * KT):
                act.wait_ge(s["e_ps"], pair * 16 + (e + 1))
                act.wait_ge(s["pv_done"], pair * KT + (e // 2 + 1))
                nc.scalar.activation(probs[e % 4][:], p_e[e % 2][:], ACT.Exp, scale=SCALE).then_inc(s["e_done"], 1)
            if more:
                negated(pair + 2, r % 2)
        pairs(act, body)

    @block.gpsimd
    def _(pool):
        g = nc.gpsimd
        g.memset(ident[:], 0.0).then_inc(s["ident0"], 1)
        pool.wait_ge(s["ident0"], 1)
        g.affine_select(out=ident[:], in_=ident[:], compare_op=ALU.not_equal, fill=1.0, base=0, pattern=[[-1, P]], channel_multiplier=1).then_inc(s["id"], 1)

        def body(pair, i, r, more, more3):
            pool.wait_ge(s["o_done"], pair + 2)
            g.dma_start(o_rows[pair], o_s[r % 2][:].rearrange("p t h e -> p (t h e)")).then_inc(s["o_stored"], 16)
            pool.wait_ge(s["o_stored"], pair * 16 + 16)
            pool.sem_inc(s["o_free"], 1)
        pairs(pool, body)

    @block.vector
    def _(dve):
        V_ = nc.vector
        V_.memset(ones[:], 1.0)
        V_.memset(zrow[:], 0.0)
        for r in range(RING):
            V_.memset(qst[r][:].bitcast(f32), 0.0)
            for h in range(2):
                i = V_.memset(kst[r][h][:].bitcast(f32), 0.0)
        i.then_inc(s["consts"], 1)
        V_.memset(oT[:], 1.0).then_inc(s["start"], 1)
        dve.sem_inc(s["pv_done"], 2)
        dve.sem_inc(s["e_done"], 2)
        dve.sem_inc(s["m_red"], 2)
        dve.sem_inc(s["oT_done"], 1)
        dve.sem_inc(s["o_free"], 3)

        def reduce(pair, j):
            dve.wait_ge(s["m_ps"], pair * 32 + (j + 1))
            V_.reduce_max(mx[:, j // 2, j % 2:j % 2 + 1], p_m[j % 2][:], AX.X).then_inc(s["m_red"], 1)

        def combine(pair):
            dve.wait_ge(s["m_red"], pair * 32 + 34)
            V_.tensor_tensor(mxq[:], mx[:, :, 0], mx[:, :, 1], ALU.max).then_inc(s["mxq_done"], 1)

        def low_part(pair, half):
            dve.wait_ge(s["mT_read"], pair + 1)
            V_.scalar_tensor_tensor(nm_lo[half][:], p_t[0:16, 0, :], -1.0, nm_hi[half][:].bitcast(f32), ALU.mult, ALU.subtract).then_inc(s["nm_done"], 1)

        for pair in range(2):
            for j in range(32):
                reduce(pair, j)
            combine(pair)
            low_part(pair, pair)

        def normalise(n, half):
            dve.wait_ge(s["oT_ps"], n + 1)
            ot = p_t[:].rearrange("p q (h a e) -> p q h a e", h=2, a=2)
            V_.reciprocal(rden[:].rearrange("p q (h a) -> p q h a", h=2), ot[:, :, :, :, 16]).then_inc(s["rden_done"], 1)
            dve.wait_ge(s["rden_done"], n + 1)
            dve.wait_ge(s["o_free"], n + 1)
            for a in range(2):
                last = V_.tensor_tensor(o_s[half][:, a * 4:a * 4 + 4], ot[:, :, :, a, 0:16],
                                        rden[:].rearrange("p q (h a o) -> p q h a o", h=2, o=1)[:, :, :, a].to_broadcast([P, 4, 2, 16]), ALU.mult)
            last.then_inc(s["o_done"], 1)

        def body(pair, i, r, more, more3):
            if more:
                for j in range(8):
                    reduce(pair + 2, j)
            normalise(pair, (r + 1) % 2)
            if more:
                for j in range(8, 32):
                    reduce(pair + 2, j)
                combine(pair + 2)
            dve.wait_ge(s["pv_done"], pair * KT + (KT + 2))
            V_.tensor_copy(oT[:], p_o[:]).then_inc(s["oT_done"], 1)
            if more:
                low_part(pair + 2, r % 2)
        pairs(dve, body)
        normalise(PAIRS, 1)

    @block.tensor
    def _(pe):
        mm, tr = nc.tensor.matmul, nc.tensor.transpose
        pe.wait_ge(s["id"], 1)
        pe.wait_ge(s["start"], 1)
        pe.wait_ge(s["rows"], 16 * 2 * RING)

        def max_scores(pair, r, j):
            h, qt, kh = j // 16, j // 2 % 8, j % 2
            pe.wait_ge(s["m_red"], pair * 32 + (j + 1))
            mm(p_m[j % 2][:], qst[r][:, qt * P:(qt + 1) * P], kst[r][h][:, kh * 512:(kh + 1) * 512], start=True, stop=True).then_inc(s["m_ps"], 1)

        def max_transpose(pair):
            pe.wait_ge(s["mxq_done"], pair + 1)
            tr(p_t[0:16, 0, :], mxq[:], ident[:]).then_inc(s["mT_ps"], 1)

        def output_transpose(n):
            pe.wait_ge(s["nm_done"], n + 2 if not isinstance(n, int) else min(n + 2, PAIRS))
            pe.wait_ge(s["oT_done"], n + 1)
            if isinstance(n, int):
                pe.wait_ge(s["o_done"], n) if n else None
            for q in range(4):
                last = tr(p_t[:, q, :], oT[:, q * P:(q + 1) * P], ident[:])
            last.then_inc(s["oT_ps"], 1)

        def loaded(r, i):
            pe.wait_ge(s[f"q_in{r}"], i * (16 * LOADS) + 16 * LOADS)

        for pair in range(2):
            loaded(pair, 0)
            for j in range(32):
                max_scores(pair, pair, j)
            max_transpose(pair)
            pe.wait_ge(s["nm_done"], pair + 1)

        def body(pair, i, r, more, more3):
            i2, r2 = ahead(i, r)
            pe.wait_ge(s[f"m_in{r}"], i * 64 + 64)

            def values(kt):
                pe.wait_ge(s["e_done"], pair * 16 + (2 * kt + 4))
                for h in range(2):
                    for a in range(2):
                        last = mm(p_o[32 * (2 * h + a):32 * (2 * h + a) + 32, :], vst[r][:, kt, h, :],
                                  probs[(2 * kt + h) % 4][:, a * 512:(a + 1) * 512], start=(kt == 0), stop=(kt == KT - 1))
                last.then_inc(s["pv_done"], 1)

            if more:
                loaded(r2, i2)
            for kt in range(KT):
                for h in range(2):
                    pe.wait_ge(s["e_done"], pair * 16 + (2 * kt + h + 1))
                    for a in range(2):
                        last = mm(p_e[h][:, a * 512:(a + 1) * 512], kst[r][h][:, kt * P:(kt + 1) * P], qst[r][:, a * 512:(a + 1) * 512], start=True, stop=True)
                    last.then_inc(s["e_ps"], 1)
                    if more:
                        max_scores(pair + 2, r2, 4 * kt + h)
                if kt == 0:
                    pe.wait_ge(s["oT_done"], pair + 1)
                if kt > 0:
                    values(kt - 1)
                if more:
                    max_scores(pair + 2, r2, 4 * kt + 2)
                if kt == 1:
                    output_transpose(pair)
                if more:
                    max_scores(pair + 2, r2, 4 * kt + 3)
            values(KT - 1)
            if more:
                pe.wait_ge(s["o_done"], pair + 1)
                max_transpose(pair + 2)
        pairs(pe, body)
        output_transpose(PAIRS)


def output_projection_and_gate(nc, ctx, o_d, x1y_d, wo, gate_w, ln2_w, base_d, xg_d, chosen, share, n_batches=8):
    P, D, T, NE = 128, 256, 4, 8
    HT = P * T
    EPS = 1e-5
    f32 = mybir.dt.float32
    ALU, ACT, AX = mybir.AluOpType, mybir.ActivationFunctionType, mybir.AxisListType

    def sb(name, shape, dt=f32):
        return ctx.enter_context(nc.sbuf_tensor("c_" + name, shape, dt))

    wo_raw, woT = sb("wo_raw", [P, 2, D]), sb("woT", [P, 2, D])
    gw_raw, gwT = sb("gw_raw", [NE, D]), sb("gwT", [P, 2, NE])
    ln2 = sb("ln2", [P, 2])
    ident, mhalf = sb("ident", [P, P]), sb("mhalf", [P, T])
    oin, xy = [sb(f"oin{r}", [P, 8, T, 32]) for r in range(2)], [sb(f"xy{r}", [P, T, 2, D]) for r in range(2)]
    orow = [sb(f"orow{r}", [P, T, 8, 32]) for r in range(2)]
    oT, xgT = sb("oT", [P, 2, HT]), sb("xgT", [P, 2, HT])
    h = sb("h", [P, T, D])
    base, xg = [sb(f"base{r}", [P, T, D]) for r in range(2)], [sb(f"xg{r}", [P, T, D]) for r in range(2)]
    sq, ms, r_s = sb("sq", [P, D]), sb("ms", [P, T]), sb("r_s", [P, T])
    lg, top, tidx = sb("lg", [P, T, NE]), sb("top", [P, T, 8]), sb("tidx", [P, T, 8], mybir.dt.uint32)
    diff, ed, den = sb("diff", [P, T]), sb("ed", [P, T]), sb("den", [P, T])
    sh = sb("sh", [P, T, 2])
    p1, p2, p3 = (ctx.enter_context(nc.psum_tensor(f"c_p{i}", [P, 2, 512], f32)) for i in (1, 2, 3))
    p4 = ctx.enter_context(nc.psum_tensor("c_p4", [P, T, NE], f32))
    names = ("w_in", "zero", "consts", "wT_ps", "wT_done", "in0", "in1", "orow_done", "in_free", "oT_ps", "oT_done", "h_ps", "h_done", "ms_done",
             "ms_eps", "r_done", "xg_done", "base_done", "st0", "st1", "st_free", "xgT_ps", "xgT_done", "lg_ps", "lg_done", "top_done", "tidx_done",
             "diff_done", "ed_done", "den_done", "rec_done", "sh_done", "copied", "dve_turn", "pool_turn")
    s = {n: stage_semaphore(nc, ctx, "c_" + n) for n in names}
    x1y_v = x1y_d.rearrange("(n t p) e d -> n p t e d", p=P, t=T)
    base_v, xg_v = (d.rearrange("(n t p) d -> n p t d", p=P, t=T) for d in (base_d, xg_d))
    block = ctx.enter_context(nc.Block())

    def halves(eng, body):
        with eng.Fori(0, n_batches) as b:
            for half in (0, 1):
                body(b, half, b * 2 + half, b * 2 + (half + 1))

    @block.sync
    def _(sp):
        sp.dma_start(wo_raw[:], wo.rearrange("(k p) n -> p k n", p=P)).then_inc(s["w_in"], 16)
        sp.dma_start(gw_raw[:], gate_w).then_inc(s["w_in"], 16)
        with nc.allow_non_contiguous_dma("256 weights, once"):
            sp.dma_start(ln2[:], ln2_w.rearrange("(k p) -> p k", p=P)).then_inc(s["w_in"], 16)

        def body(b, half, n, n1):
            sp.wait_ge(s["in_free"], n1)
            sp.dma_start(oin[half][:].rearrange("p a t e -> p a (t e)"),
                         o_d[b, :, :, half * T:(half + 1) * T, :].rearrange("a p t e -> p a (t e)")).then_inc(s[f"in{half}"], 16)
            sp.dma_start(xy[half][:], x1y_v[n]).then_inc(s[f"in{half}"], 16)
        halves(sp, body)

    @block.gpsimd
    def _(pool):
        g = nc.gpsimd
        g.memset(ident[:], 0.0)
        g.memset(mhalf[:], -0.5).then_inc(s["zero"], 1)
        pool.wait_ge(s["zero"], 1)
        g.affine_select(out=ident[:], in_=ident[:], compare_op=ALU.not_equal, fill=1.0, base=0, pattern=[[-1, P]], channel_multiplier=1).then_inc(s["consts"], 1)

        def body(b, half, n, n1):
            pool.wait_ge(s[f"in{half}"], b * 32 + 32)
            pool.sem_inc(s["pool_turn"], 1)
            g.tensor_copy(orow[half][:].rearrange("p t a e -> p a t e"), oin[half][:]).then_inc(s["orow_done"], 1)
            pool.wait_ge(s["ms_done"], n * T + (T + 1))
            pool.sem_inc(s["pool_turn"], 1)
            g.tensor_scalar(r_s[:], ms[:], EPS, None, ALU.add).then_inc(s["ms_eps"], 1)
            pool.wait_ge(s["ms_eps"], n1)
            g.tensor_tensor(r_s[:], r_s[:], mhalf[:], ALU.pow).then_inc(s["r_done"], 1)
            pool.wait_ge(s["base_done"], n1)
            g.dma_start(base_v[n], base[half][:]).then_inc(s[f"st{half}"], 16)
            pool.wait_ge(s["xg_done"], n1)
            pool.sem_inc(s["pool_turn"], 1)
            g.dma_start(xg_v[n], xg[half][:]).then_inc(s[f"st{half}"], 16)
            pool.wait_ge(s[f"st{half}"], b * 32 + 32)
            pool.sem_inc(s["st_free"], 1)
        halves(pool, body)

    @block.scalar
    def _(act):
        act.wait_ge(s["w_in"], 48)

        def body(b, half, n, n1):
            act.wait_ge(s["oT_ps"], n1)
            nc.scalar.copy(oT[:], p1[:]).then_inc(s["oT_done"], 1)
            act.wait_ge(s["h_done"], n1)
            for t in range(T):
                act.wait_ge(s["ms_done"], n * T + (t + 1))
                nc.scalar.activation(sq[:], h[:, t], ACT.Square, scale=D ** -0.5, accum_out=ms[:, t:t + 1]).then_inc(s["ms_done"], 1)
            act.wait_ge(s["xgT_ps"], n1)
            nc.scalar.mul(xgT[:, 0], p3[:, 0], ln2[:, 0:1])
            nc.scalar.mul(xgT[:, 1], p3[:, 1], ln2[:, 1:2]).then_inc(s["xgT_done"], 1)
            act.wait_ge(s["diff_done"], n1)
            nc.scalar.activation(ed[:], diff[:], ACT.Exp).then_inc(s["ed_done"], 1)
        halves(act, body)

    @block.vector
    def _(dve):
        V_ = nc.vector
        for n, c in (("in_free", 2), ("ms_done", 1), ("st_free", 2)):
            dve.sem_inc(s[n], c)
        dve.wait_ge(s["wT_ps"], 1)
        V_.tensor_copy(woT[:].rearrange("p k m -> p (k m)"), p1[:, 0])
        V_.tensor_copy(gwT[:].rearrange("p k m -> p (k m)"), p1[:, 1, 0:2 * NE]).then_inc(s["wT_done"], 1)

        def body(b, half, n, n1):
            dve.wait_ge(s[f"in{half}"], b * 32 + 32)
            dve.wait_ge(s["h_ps"], n1)
            V_.tensor_tensor(h[:], p2[:].rearrange("p a (e c) -> p (a e) c", e=2), xy[half][:, :, 1], ALU.add).then_inc(s["h_done"], 1)
            dve.wait_ge(s["h_done"], n1)
            dve.wait_ge(s["st_free"], n1)
            V_.tensor_tensor(base[half][:], h[:], xy[half][:, :, 0], ALU.add).then_inc(s["base_done"], 1)
            dve.wait_ge(s["base_done"], n1)
            dve.sem_inc(s["in_free"], 1)
            dve.wait_ge(s["r_done"], n1)
            for t in range(T):
                i = V_.tensor_scalar(xg[half][:, t], h[:, t], r_s[:, t:t + 1], None, ALU.mult)
            i.then_inc(s["xg_done"], 1)
            dve.wait_ge(s["lg_ps"], n1)
            V_.tensor_copy(lg[:], p4[:]).then_inc(s["lg_done"], 1)
            dve.wait_ge(s["lg_done"], n1)
            dve.sem_inc(s["dve_turn"], 1)
            for t in range(T):
                i = V_.max(top[:, t], lg[:, t])
            i.then_inc(s["top_done"], 1)
            dve.wait_ge(s["top_done"], n1)
            V_.tensor_tensor(diff[:], top[:, :, 1], top[:, :, 0], ALU.subtract).then_inc(s["diff_done"], 1)
            for t in range(T):
                i = V_.max_index(tidx[:, t], top[:, t], lg[:, t])
            i.then_inc(s["tidx_done"], 1)
            dve.wait_ge(s["tidx_done"], n1)
            V_.tensor_copy(chosen[:, bass.ds(n * T, T), :], tidx[:, :, 0:2])
            dve.wait_ge(s["ed_done"], n1)
            V_.tensor_scalar(den[:], ed[:], 1.0, None, ALU.add).then_inc(s["den_done"], 1)
            dve.wait_ge(s["den_done"], n1)
            V_.reciprocal(sh[:, :, 0], den[:]).then_inc(s["rec_done"], 1)
            dve.wait_ge(s["rec_done"], n1)
            V_.tensor_tensor(sh[:, :, 1], ed[:], sh[:, :, 0], ALU.mult).then_inc(s["sh_done"], 1)
            dve.wait_ge(s["sh_done"], n1)
            V_.tensor_copy(share[:, bass.ds(n * T, T), :], sh[:]).then_inc(s["copied"], 1)
        halves(dve, body)

    @block.tensor
    def _(pe):
        mm, tr = nc.tensor.matmul, nc.tensor.transpose
        pe.wait_ge(s["w_in"], 48)
        pe.wait_ge(s["consts"], 1)
        for k in range(2):
            for m in range(2):
                tr(p1[:, 0, k * D + m * P:k * D + (m + 1) * P], wo_raw[:, m, k * P:(k + 1) * P], ident[:])
            i = tr(p1[:, 1, k * NE:(k + 1) * NE], gw_raw[:, k * P:(k + 1) * P], ident[0:NE, 0:NE])
        i.then_inc(s["wT_ps"], 1)
        pe.wait_ge(s["wT_done"], 1)

        def body(b, half, n, n1):
            pe.wait_ge(s["orow_done"], n1)
            for t in range(T):
                for k in range(2):
                    i = tr(p1[:, k, t * P:(t + 1) * P], orow[half][:, t, 4 * k:4 * k + 4, :].rearrange("p a e -> p (a e)"), ident[:])
            i.then_inc(s["oT_ps"], 1)
            pe.wait_ge(s["oT_done"], n1)
            for t in range(T):
                for k in range(2):
                    i = mm(p2[:, t // 2, (t % 2) * D:(t % 2 + 1) * D], oT[:, k, t * P:(t + 1) * P], woT[:, k, :], start=(k == 0), stop=(k == 1))
            i.then_inc(s["h_ps"], 1)
            pe.wait_ge(s["xg_done"], n1)
            for t in range(T):
                for k in range(2):
                    i = tr(p3[:, k, t * P:(t + 1) * P], xg[half][:, t, k * P:(k + 1) * P], ident[:])
            i.then_inc(s["xgT_ps"], 1)
            pe.wait_ge(s["xgT_done"], n1)
            for t in range(T):
                for k in range(2):
                    i = mm(p4[:, t, :], xgT[:, k, t * P:(t + 1) * P], gwT[:, k, :], start=(k == 0), stop=(k == 1))
            i.then_inc(s["lg_ps"], 1)
        halves(pe, body)


def route(nc, ctx, chosen, token_of, code_of, expert_of, NT, TILES):
    P, NE = 128, 8
    C2 = 2 * NT
    f32, i32 = mybir.dt.float32, mybir.dt.int32
    ALU, AX = mybir.AluOpType, mybir.AxisListType

    def sb(name, shape, dt=f32):
        return ctx.enter_context(nc.sbuf_tensor("r_" + name, shape, dt))

    ones, before = sb("ones", [P, P]), sb("before", [P, P])
    WIDE = max(P, TILES)
    iota_i, iota = sb("iota_i", [P, WIDE], i32), sb("iota", [P, WIDE])
    lane_i, lane = sb("lane_i", [P, 1], i32), sb("lane", [P, 1])
    val_i, val = sb("val_i", [P, C2], i32), sb("val", [P, C2])
    E = sb("E", [P, C2, NE])
    tot, cum = sb("tot", [P, NE, C2]), sb("cum", [P, NE, C2])
    full, full_i, tiles, end = sb("full", [P, NE]), sb("full_i", [P, NE], i32), sb("tiles", [P, NE]), sb("end", [P, NE])
    begin = sb("begin", [P, NE])
    where = sb("where", [P, C2, NE])
    slot, slot_i = sb("slot", [P, C2]), sb("slot_i", [P, C2], i32)
    lo_i, hi_i, lo, hi = sb("lo_i", [P, C2], i32), sb("hi_i", [P, C2], i32), sb("lo", [P, C2]), sb("hi", [P, C2])
    cmp, ex = sb("cmp", [P, TILES, NE]), sb("ex", [P, TILES])
    is_lo = [sb(f"is_lo{r}", [P, P]) for r in range(4)]
    is_hi = [sb(f"is_hi{r}", [P, TILES]) for r in range(4)]
    inv, invm, empty = sb("inv", [P, TILES]), sb("invm", [P, TILES]), sb("empty", [P, TILES])
    inv_i = sb("inv_i", [P, TILES], i32)
    W = C2 * NE // 2
    p_before = ctx.enter_context(nc.psum_tensor("r_p_before", [P, 2, 512], f32))
    p_total = ctx.enter_context(nc.psum_tensor("r_p_total", [P, 2, 512], f32))
    p_inv = ctx.enter_context(nc.psum_tensor("r_p_inv", [P, TILES], f32))
    s = {n: stage_semaphore(nc, ctx, "r_" + n) for n in ("pool0", "pool", "dve", "E_done", "ps", "hot", "inv_ps")}
    block = ctx.enter_context(nc.Block())

    @block.gpsimd
    def _(pool):
        g = nc.gpsimd
        g.memset(before[:], 1.0)
        g.iota(iota_i[:], [[1, WIDE]], base=0, channel_multiplier=0)
        g.iota(lane_i[:], [[1, 1]], base=0, channel_multiplier=1)
        g.iota(val_i[:], [[2 * P, NT], [1, 2]], base=1, channel_multiplier=2).then_inc(s["pool0"], 1)
        pool.wait_ge(s["pool0"], 1)
        g.affine_select(out=before[:], in_=before[:], compare_op=ALU.is_gt, fill=0.0, base=0, pattern=[[1, P]], channel_multiplier=-1).then_inc(s["pool"], 1)

    @block.vector
    def _(dve):
        V_ = nc.vector
        count = [0]

        def then(ins):
            count[0] += 1
            ins.then_inc(s["dve"], 1)
            dve.wait_ge(s["dve"], count[0])

        dve.wait_ge(s["pool"], 1)
        V_.memset(ones[:], 1.0)
        V_.tensor_copy(iota[:], iota_i[:])
        V_.tensor_copy(lane[:], lane_i[:])
        then(V_.tensor_copy(val[:], val_i[:]))
        V_.tensor_tensor(E[:], chosen[:].rearrange("p j (k o) -> p (j k) o", o=1).to_broadcast([P, C2, NE]),
                         iota[:, 0:NE].rearrange("p (o e) -> p o e", o=1).to_broadcast([P, C2, NE]), ALU.is_equal).then_inc(s["E_done"], 1)
        dve.wait_ge(s["ps"], 1)
        for k in range(2):
            i = V_.tensor_copy(tot[:, :, k * NT:(k + 1) * NT], p_total[:, k, 0:W].rearrange("p (c e) -> p e c", e=NE))
        then(i)
        for e in range(NE):
            i = V_.tensor_tensor_scan(cum[:, e, :], ones[:, 0:C2], tot[:, e, :], 0.0, ALU.mult, ALU.add)
        then(i)
        then(V_.tensor_scalar(full[:], cum[:, :, C2 - 1], float(P - 1), None, ALU.add))
        then(V_.tensor_copy(full_i[:], full[:]))
        then(V_.tensor_scalar(full_i[:], full_i[:], 7, None, ALU.arith_shift_right))
        then(V_.tensor_copy(tiles[:], full_i[:]))
        then(V_.tensor_tensor_scan(end[:], ones[:, 0:NE], tiles[:], 0.0, ALU.mult, ALU.add))
        then(V_.tensor_tensor(begin[:], end[:], tiles[:], ALU.subtract))
        then(V_.tensor_scalar(begin[:], begin[:], float(P), None, ALU.mult))
        then(V_.tensor_tensor(cum[:], cum[:], tot[:], ALU.subtract))
        then(V_.tensor_tensor(cum[:], cum[:], begin[:].rearrange("p (e o) -> p e o", o=1).to_broadcast([P, NE, C2]), ALU.add))
        for k in range(2):
            i = V_.tensor_tensor(where[:, k * NT:(k + 1) * NT, :], p_before[:, k, 0:W].rearrange("p (c e) -> p c e", e=NE),
                                 cum[:, :, k * NT:(k + 1) * NT].rearrange("p e c -> p c e"), ALU.add)
        then(i)
        then(V_.tensor_tensor(where[:], where[:], E[:], ALU.mult))
        then(V_.reduce_sum(slot[:], where[:], AX.X))
        then(V_.tensor_copy(slot_i[:], slot[:]))
        V_.tensor_scalar(hi_i[:], slot_i[:], 7, None, ALU.arith_shift_right)
        then(V_.tensor_scalar(lo_i[:], slot_i[:], P - 1, None, ALU.bitwise_and))
        V_.tensor_copy(hi[:], hi_i[:])
        then(V_.tensor_copy(lo[:], lo_i[:]))
        with dve.Fori(0, C2 // 4) as i4:
            for r in range(4):
                c = i4 * 4 + r
                dve.wait_ge(s["inv_ps"], c + 1)
                V_.tensor_scalar(is_lo[r][:], iota[:, 0:P], lo[:, bass.ds(c, 1)], None, ALU.is_equal)
                V_.tensor_scalar(is_hi[r][:], iota[:, 0:TILES], hi[:, bass.ds(c, 1)], val[:, bass.ds(c, 1)], ALU.is_equal, ALU.mult).then_inc(s["hot"], 1)
        V_.tensor_tensor(cmp[:], iota[:, 0:TILES].rearrange("p (m o) -> p m o", o=1).to_broadcast([P, TILES, NE]),
                         end[:].rearrange("p (o e) -> p o e", o=1).to_broadcast([P, TILES, NE]), ALU.is_ge).then_inc(s["dve"], 1)
        count[0] += 1
        dve.wait_ge(s["dve"], count[0])
        then(V_.reduce_sum(ex[:], cmp[:], AX.X))
        then(V_.tensor_scalar(ex[:], ex[:], float(NE - 1), None, ALU.min))
        V_.memset(expert_of[:, 0:1], 0)
        V_.tensor_copy(expert_of[:, 1:TILES + 1], ex[0:1, :])
        dve.wait_ge(s["inv_ps"], C2 + 4)
        then(V_.tensor_copy(inv[:], p_inv[:]))
        V_.tensor_scalar(empty[:], inv[:], 0.0, float(2 * NT * P + 1), ALU.is_equal, ALU.mult)
        then(V_.tensor_scalar(invm[:], inv[:], -1.0, None, ALU.add))
        then(V_.tensor_tensor(inv[:], invm[:], empty[:], ALU.add))
        then(V_.tensor_scalar(empty[:], empty[:], 1.0 / (2 * NT * P + 1), lane[:, 0:1], ALU.mult, ALU.mult))
        then(V_.tensor_tensor(inv[:], inv[:], empty[:], ALU.add))
        V_.tensor_copy(code_of[:], inv[:])
        then(V_.tensor_scalar(invm[:], invm[:], 0.0, None, ALU.max))
        then(V_.tensor_copy(inv_i[:], invm[:]))
        then(V_.tensor_scalar(token_of[:], inv_i[:], 1, None, ALU.arith_shift_right))

    @block.tensor
    def _(pe):
        mm = nc.tensor.matmul
        pe.sem_inc(s["inv_ps"], 4)
        pe.wait_ge(s["E_done"], 1)
        for k in range(2):
            rhs = E[:, k * NT:(k + 1) * NT, :].rearrange("p c e -> p (c e)")
            mm(p_before[:, k, 0:W], before[:], rhs, start=True, stop=True)
            i = mm(p_total[:, k, 0:W], ones[:], rhs, start=True, stop=True)
        i.then_inc(s["ps"], 1)
        def column(c, r, start, stop):
            pe.wait_ge(s["hot"], c + 1)
            mm(p_inv[:], is_lo[r][:], is_hi[r][:], start=start, stop=stop, skip_group_check=True).then_inc(s["inv_ps"], 1)
        for r in range(4):
            column(r, r, r == 0, False)
        with pe.Fori(1, C2 // 4) as i4:
            for r in range(4):
                column(i4 * 4 + r, r, False, False)


def experts(nc, ctx, xg_d, w1, w3, w2, ln2_w, token_of, code_of, expert_of, ys_d, TILES):
    P, D, I, NE = 128, 256, 512, 8
    f32, i32 = mybir.dt.float32, mybir.dt.int32
    ALU, ACT, AX = mybir.AluOpType, mybir.ActivationFunctionType, mybir.AxisListType

    def sb(name, shape, dt=f32):
        return ctx.enter_context(nc.sbuf_tensor("d_" + name, shape, dt))

    w1T, w3T = sb("w1T", [P, NE, 2, I]), sb("w3T", [P, NE, 2, I])
    w2T = sb("w2T", [P, NE, 4, D])
    raw = [sb(f"raw{r}", [P, 3, 1024]) for r in range(2)]
    ln2, ident = sb("ln2", [P, 2]), sb("ident", [P, P])
    tok, code = [sb(f"tok{r}", [P, 1], i32) for r in range(4)], [sb(f"code{r}", [P, 1], i32) for r in range(2)]
    xs = [sb(f"xs{r}", [P, D]) for r in range(4)]
    xT = [sb(f"xT{r}", [P, 2, P]) for r in range(2)]
    act_s, h = [sb(f"act{r}", [P, I]) for r in range(2)], [sb(f"h{r}", [P, I]) for r in range(2)]
    hT = [sb(f"hT{r}", [P, 4, P]) for r in range(2)]
    y = [sb(f"y{r}", [P, D]) for r in range(2)]
    p_x = ctx.enter_context(nc.psum_tensor("d_p_x", [P, 4, P], f32))
    p_up = [ctx.enter_context(nc.psum_tensor(f"d_p_up{r}", [P, 2, I], f32)) for r in range(2)]
    p_h = ctx.enter_context(nc.psum_tensor("d_p_h", [P, 4, P], f32))
    p_y = ctx.enter_context(nc.psum_tensor("d_p_y", [P, 512], f32))
    names = ("raw_in0", "raw_in1", "zero", "id", "wT_ps", "wT_even", "wT_odd", "tok_done", "turn", *(f"x_in{r}" for r in range(4)), "xT_ps", "xT_done",
             "ln_in", "up_ps", "act_done", "h_done", "hT_ps", "hT_done", "y_ps", "y_done", "code_done", "y_out", "y_free", "start")
    s = {n: stage_semaphore(nc, ctx, "d_" + n) for n in names}
    block = ctx.enter_context(nc.Block())

    @block.sync
    def _(sp):
        with nc.allow_non_contiguous_dma("256 weights, once"):
            sp.dma_start(ln2[:], ln2_w.rearrange("(k p) -> p k", p=P)).then_inc(s["ln_in"], 16)
        for e in range(NE):
            if e >= 2:
                sp.wait_ge(s["wT_ps"], 6 * (e - 1))
            r = e % 2
            sp.dma_start(raw[r][:, 0].rearrange("p (a d) -> p a d", a=4), w1[e].rearrange("(a p) d -> p a d", p=P)).then_inc(s[f"raw_in{r}"], 16)
            sp.dma_start(raw[r][:, 1].rearrange("p (a d) -> p a d", a=4), w3[e].rearrange("(a p) d -> p a d", p=P)).then_inc(s[f"raw_in{r}"], 16)
            sp.dma_start(raw[r][:, 2].rearrange("p (a i) -> p a i", a=2), w2[e].rearrange("(a p) i -> p a i", p=P)).then_inc(s[f"raw_in{r}"], 16)

    def banks(e, j):
        n = e * 6 + j
        return p_up[n // 2 % 2][:, n % 2, :]

    @block.gpsimd
    def _(pool):
        g = nc.gpsimd
        g.memset(ident[:], 0.0).then_inc(s["zero"], 1)
        pool.wait_ge(s["zero"], 1)
        g.affine_select(out=ident[:], in_=ident[:], compare_op=ALU.not_equal, fill=1.0, base=0, pattern=[[-1, P]], channel_multiplier=1).then_inc(s["id"], 1)

        def gather(m, r):
            g.tensor_copy(tok[r][:], token_of[:, bass.ds(m, 1)]).then_inc(s["tok_done"], 1)
            pool.wait_ge(s["tok_done"], m + 1)
            pool.sem_inc(s["turn"], 1)
            g.indirect_dma_start(xs[r][:], None, xg_d, bass.IndirectOffsetOnAxis(ap=tok[r][:, 0:1], axis=0)).then_inc(s[f"x_in{r}"], 16)

        def scatter(m, r):
            g.tensor_copy(code[r][:], code_of[:, bass.ds(m, 1)]).then_inc(s["code_done"], 1)
            pool.wait_ge(s["code_done"], m + 1)
            pool.wait_ge(s["y_done"], m + 3)
            pool.sem_inc(s["turn"], 1)
            g.indirect_dma_start(ys_d, bass.IndirectOffsetOnAxis(ap=code[r][:, 0:1], axis=0), y[r][:], None).then_inc(s["y_out"], 16)
            pool.wait_ge(s["y_out"], m * 16 + 16)
            pool.sem_inc(s["y_free"], 1)

        for m in range(3):
            gather(m, m)
        with pool.Fori(0, TILES // 4 - 1) as i:
            for r in range(4):
                m = i * 4 + r
                pool.wait_ge(s["xT_ps"], m + 1)
                gather(m + 3, (r + 3) % 4)
                scatter(m, r % 2)
        for r in range(4):
            m = TILES - 4 + r
            if r == 0:
                pool.wait_ge(s["xT_ps"], m + 1)
                gather(m + 3, 3)
            scatter(m, r % 2)

    @block.scalar
    def _(act):
        act.wait_ge(s["ln_in"], 16)
        for e in range(NE):
            for j in (1, 3, 5):
                act.wait_ge(s["wT_ps"], e * 6 + j + 1)
                dst = (w1T[:, e, 1], w3T[:, e, 1], w2T[:, e, 2:4])[j // 2]
                nc.scalar.copy(dst.rearrange("p a n -> p (a n)") if j == 5 else dst, banks(e, j)).then_inc(s["wT_odd"], 1)

        def first(m, r):
            act.wait_ge(s["xT_ps"], m + 2)
            nc.scalar.mul(xT[r][:, 0], p_x[:, 0], ln2[:, 0:1])
            nc.scalar.mul(xT[r][:, 1], p_x[:, 1], ln2[:, 1:2]).then_inc(s["xT_done"], 1)
            act.wait_ge(s["up_ps"], 2 * m + 1)
            nc.scalar.activation(act_s[r][:], p_up[r][:, 0], ACT.Silu).then_inc(s["act_done"], 1)

        with act.Fori(0, TILES // 2) as i:
            for r in (0, 1):
                m = i * 2 + r
                first(m, r)
                act.wait_ge(s["hT_ps"], m + 1)
                nc.scalar.copy(hT[1 - r][:], p_h[:]).then_inc(s["hT_done"], 1)
        act.wait_ge(s["hT_ps"], TILES + 1)
        nc.scalar.copy(hT[1][:], p_h[:]).then_inc(s["hT_done"], 1)

    @block.vector
    def _(dve):
        V_ = nc.vector
        for r in (0, 1):
            V_.memset(h[r][:], 0.0)
        V_.memset(hT[1][:], 0.0).then_inc(s["start"], 1)
        dve.sem_inc(s["xT_ps"], 1)
        dve.sem_inc(s["y_free"], 3)
        dve.sem_inc(s["y_done"], 1)
        for e in range(NE):
            for j in (0, 2, 4):
                dve.wait_ge(s["wT_ps"], e * 6 + j + 1)
                dst = (w1T[:, e, 0], w3T[:, e, 0], w2T[:, e, 0:2])[j // 2]
                V_.tensor_copy(dst.rearrange("p a n -> p (a n)") if j == 4 else dst, banks(e, j)).then_inc(s["wT_even"], 1)

        with dve.Fori(0, TILES // 2) as i:
            for r in (0, 1):
                m = i * 2 + r
                dve.wait_ge(s["act_done"], m + 1)
                dve.wait_ge(s["up_ps"], 2 * m + 2)
                V_.tensor_tensor(h[r][:], act_s[r][:], p_up[r][:, 1], ALU.mult).then_inc(s["h_done"], 1)
                dve.wait_ge(s["y_ps"], m + 1)
                dve.wait_ge(s["y_free"], m + 1)
                V_.tensor_copy(y[1 - r][:], p_y[:, 0:D]).then_inc(s["y_done"], 1)
        dve.wait_ge(s["y_ps"], TILES + 1)
        dve.wait_ge(s["y_free"], TILES + 1)
        V_.tensor_copy(y[1][:], p_y[:, 0:D]).then_inc(s["y_done"], 1)

    @block.tensor
    def _(pe):
        mm, tr = nc.tensor.matmul, nc.tensor.transpose
        pe.wait_ge(s["id"], 1)
        pe.wait_ge(s["start"], 1)
        for e in range(NE):
            pe.wait_ge(s[f"raw_in{e % 2}"], 48 * (e // 2) + 48)
            for j in range(6):
                n = e * 6 + j
                if n >= 4:
                    pe.wait_ge(s[("wT_even", "wT_odd")[n % 2]], (n - 4) // 2 + 1)
                for i in range(4):
                    if j < 4:
                        src = raw[e % 2][:, j // 2].rearrange("p (a d) -> p a d", a=4)[:, i, (j % 2) * P:(j % 2 + 1) * P]
                    else:
                        src = raw[e % 2][:, 2].rearrange("p (a i) -> p a i", a=2)[:, i % 2, (2 * (j - 4) + i // 2) * P:(2 * (j - 4) + i // 2 + 1) * P]
                    last = tr(banks(e, j)[:, i * P:(i + 1) * P], src, ident[:])
                last.then_inc(s["wT_ps"], 1)
        pe.wait_ge(s["wT_even"], 3 * NE)
        pe.wait_ge(s["wT_odd"], 3 * NE)
        def last_product(m, r):
            e = pe.value_load(expert_of[0:1, bass.ds(m, 1)], min_val=0, max_val=NE - 1)
            for k in range(4):
                last = tr(p_h[:, k, :], h[r][:, k * P:(k + 1) * P], ident[:])
            last.then_inc(s["hT_ps"], 1)
            pe.wait_ge(s["hT_done"], m + 1)
            pe.wait_ge(s["y_done"], m + 1)
            for k in range(4):
                last = mm(p_y[:, 0:D], hT[r][:, k], w2T[:, bass.ds(e, 1), k, :].rearrange("p o n -> p (o n)"), start=(k == 0), stop=(k == 3))
            last.then_inc(s["y_ps"], 1)

        with pe.Fori(0, TILES // 4) as i:
            for q in range(4):
                m = i * 4 + q
                r = q % 2
                pe.wait_ge(s[f"x_in{q}"], i * 16 + 16)
                for k in range(2):
                    last = tr(p_x[:, k, :], xs[q][:, k * P:(k + 1) * P], ident[:])
                last.then_inc(s["xT_ps"], 1)
                e = pe.value_load(expert_of[0:1, bass.ds(m + 1, 1)], min_val=0, max_val=NE - 1)
                pe.wait_ge(s["xT_done"], m + 1)
                for u, w in ((0, w1T), (1, w3T)):
                    for k in range(2):
                        last = mm(p_up[r][:, u], xT[r][:, k], w[:, bass.ds(e, 1), k, :].rearrange("p o n -> p (o n)"), start=(k == 0), stop=(k == 1))
                    last.then_inc(s["up_ps"], 1)
                last_product(m, 1 - r)
                pe.wait_ge(s["h_done"], m + 1)
        last_product(TILES, 1)


def combine(nc, ctx, base_d, ys_d, share, out, NT):
    P, D, T = 128, 256, 4
    RING = 4
    f32 = mybir.dt.float32
    ALU = mybir.AluOpType
    base = [ctx.enter_context(nc.sbuf_tensor(f"e_base{r}", [P, T, D], f32)) for r in range(RING)]
    ys = [ctx.enter_context(nc.sbuf_tensor(f"e_ys{r}", [P, T, 2, D], f32)) for r in range(RING)]
    sh = [ctx.enter_context(nc.sbuf_tensor(f"e_sh{r}", [P, T, 2], f32)) for r in range(RING)]
    names = [f"in{r}" for r in range(RING)] + [f"out{r}" for r in range(RING)] + ["sh_done", "first", "sum"]
    s = {n: stage_semaphore(nc, ctx, "e_" + n) for n in names}
    base_v, out_v = (d.rearrange("(n t p) d -> n p t d", p=P, t=T) for d in (base_d, out))
    ys_v = ys_d[0:2 * NT * P, :].rearrange("(n t p k) d -> n p t k d", p=P, t=T, k=2)
    N = NT // T
    block = ctx.enter_context(nc.Block())

    @block.sync
    def _(sp):
        def load(n, r):
            sp.dma_start(base[r][:], base_v[n]).then_inc(s[f"in{r}"], 16)
            sp.dma_start(ys[r][:], ys_v[n]).then_inc(s[f"in{r}"], 16)
        for r in range(min(RING, N)):
            load(r, r)
        if N > RING:
            with sp.Fori(1, N // RING) as i:
                for r in range(RING):
                    sp.wait_ge(s[f"out{r}"], i * 16)
                    load(i * RING + r, r)

    @block.vector
    def _(dve):
        V_ = nc.vector
        with dve.Fori(0, (N + RING - 1) // RING) as i:
            for r in range(min(RING, N)):
                n = i * RING + r
                V_.tensor_copy(sh[r][:], share[:, bass.ds(n * T, T), :]).then_inc(s["sh_done"], 1)
                dve.wait_ge(s["sh_done"], n + 1)
                dve.wait_ge(s[f"in{r}"], i * 32 + 32)
                for k in range(2):
                    if k:
                        dve.wait_ge(s["first"], n + 1)
                    for t in range(T):
                        last = V_.scalar_tensor_tensor(base[r][:, t], ys[r][:, t, k], sh[r][:, t, k:k + 1], base[r][:, t], ALU.mult, ALU.add)
                    last.then_inc(s["first" if k == 0 else "sum"], 1)

    @block.scalar
    def _(act):
        with act.Fori(0, (N + RING - 1) // RING) as i:
            for r in range(min(RING, N)):
                n = i * RING + r
                act.wait_ge(s["sum"], n + 1)
                act.dma_start(out_v[n], base[r][:]).then_inc(s[f"out{r}"], 16)
        for r in range(min(RING, N)):
            act.wait_ge(s[f"out{r}"], 16 * ((N + RING - 1) // RING))


def layer_kernel(nc, x, Wq, Wk, Wv, Wg, Wgk1, Wgk2, bgk2, Wout, rms_w, ln1_w, ln2_w, wq, wk, wv, wo, gate_w, w1, w2, w3, out):
    B, N, D = x.shape
    P = 128
    NT = B * N // P
    NE = gate_w.shape[0]
    TILES = 2 * NT + NE
    f32, i32 = mybir.dt.float32, mybir.dt.int32
    flat = x.rearrange("b n d -> (b n) d")
    x1y_d = nc.dram_tensor("x1y_d", (B * N, 2, D), f32).ap()
    qk_d = nc.dram_tensor("qk_d", (2, 2, B * D, N), f32).ap()
    v_d = nc.dram_tensor("v_d", (B, 8, P, N // P, 64), f32).ap()
    o_d = nc.dram_tensor("o_d", (B, 8, P, N // P, 32), f32).ap()
    base_d = nc.dram_tensor("base_d", (B * N, D), f32).ap()
    xg_d = nc.dram_tensor("xg_d", (B * N, D), f32).ap()
    ys_d = nc.dram_tensor("ys_d", (2 * B * N + P, D), f32).ap()
    with ExitStack() as ctx:
        def sb(name, shape, dt=f32):
            return ctx.enter_context(nc.sbuf_tensor(name, shape, dt))
        chosen, share = sb("chosen", [P, NT, 2]), sb("share", [P, NT, 2])
        token_of, code_of = sb("token_of", [P, TILES], i32), sb("code_of", [P, TILES], i32)
        expert_of = sb("expert_of", [1, TILES + 1], i32)
        with Stage(nc) as stage:
            gla_and_projections(nc, stage, flat, Wq, Wk, Wv, Wg, Wgk1, Wgk2, bgk2, Wout, rms_w,
                                ln1_w, wq, wk, wv, x1y_d, qk_d, v_d, B)
        with Stage(nc) as stage:
            softmax_attention(nc, stage, qk_d, v_d, o_d, B)
        with Stage(nc) as stage:
            output_projection_and_gate(nc, stage, o_d, x1y_d, wo, gate_w, ln2_w, base_d, xg_d, chosen, share, B)
        with Stage(nc) as stage:
            route(nc, stage, chosen, token_of, code_of, expert_of, NT, TILES)
        with Stage(nc) as stage:
            experts(nc, stage, xg_d, w1, w3, w2, ln2_w, token_of, code_of, expert_of, ys_d, TILES)
        with Stage(nc) as stage:
            combine(nc, stage, base_d, ys_d, share, out.rearrange("b n d -> (b n) d"), NT)


_INS = ["L0_attn_x", "L0_attn_Wq", "L0_attn_Wk", "L0_attn_Wv", "L0_attn_Wg", "L0_attn_Wgk1", "L0_attn_Wgk2",
        "L0_attn_bgk2", "L0_attn_Wout", "L0_attn_rms_w", "L0_ffn_ln1_w", "L0_ffn_ln2_w", "L0_ffn_wq", "L0_ffn_wk",
        "L0_ffn_wv", "L0_ffn_wo", "L0_ffn_gate_w", "L0_ffn_w1", "L0_ffn_w2", "L0_ffn_w3"]
_OUTS = [((8, 1024, 256), "float32")]


def kernel(**inputs):
    import numpy as _np
    import concourse.bacc as _bacc
    from concourse import mybir as _mybir
    from concourse.bass_utils import run_bass_kernel_spmd as _run

    nc = _bacc.Bacc("TRN2", target_bir_lowering=False, num_devices=1)
    arrays, args = {}, []
    for name in _INS:
        a = _np.ascontiguousarray(inputs[name])
        arrays[f"in_{name}_dram"] = a
        args.append(nc.dram_tensor(f"in_{name}_dram", a.shape, _mybir.dt.from_np(a.dtype), kind="ExternalInput").ap())
    for i, (shape, dtype) in enumerate(_OUTS):
        dt = _mybir.dt.from_np(_np.dtype(dtype))
        args.append(nc.dram_tensor(f"out_{i}_dram", shape, dt, kind="ExternalOutput").ap())
    layer_kernel(nc, *args)
    r = _run(nc, [arrays], core_ids=[0])
    got = tuple(r.results[0][f"out_{i}_dram"] for i in range(len(_OUTS)))
    return got[0]
```

```python
from contextlib import ExitStack

import concourse.bass as bass
from concourse import mybir


def stage_semaphore(nc, stage, name):
    sem = nc.alloc_semaphore(name)
    stage.semaphores.append(sem)
    return sem


class Stage(ExitStack):

    def __init__(self, nc):
        super().__init__()
        self.nc, self.semaphores = nc, []

    def __exit__(self, *error):
        ended = super().__exit__(*error)
        self.nc.all_engine_barrier()
        self.nc.clear_and_free_semaphores(self.semaphores)
        self.nc.all_engine_barrier()
        return ended


def gla_and_projections(nc, ctx, x, Wq, Wk, Wv, Wg, Wgk1, Wgk2, bgk2, Wout, rms_w,
                        ln1_w, wq, wk, wv, x1y_d, qk_d, v_d, n_batches=8):
    P, D, T = 128, 256, 4
    HT = P * T
    C = 32
    NC = HT // C
    H, DK, DV = 4, 32, 64
    EPS = 1e-5
    f32, f32r = mybir.dt.float32, mybir.dt.float32r
    ALU, ACT, AX = mybir.AluOpType, mybir.ActivationFunctionType, mybir.AxisListType

    def sb(name, shape, dt=f32):
        return ctx.enter_context(nc.sbuf_tensor("a_" + name, shape, dt))

    Wq_s, Wk_s = sb("Wq_s", [P, 2, 128]), sb("Wk_s", [P, 2, 128])
    Wvg_s = sb("Wvg_s", [P, 2, 512])
    Wgk1_s, Wgk2_s, bgk_s = sb("Wgk1_s", [P, 2, 16]), sb("Wgk2_s", [16, 128]), sb("bgk_s", [P, 1])
    Wout_s = sb("Wout_s", [P, 2, D])
    rmsw_s, ln1w_s = sb("rmsw_s", [P, 1]), sb("ln1w_s", [P, 2])
    w_raw = sb("w_raw", [P, 3, 2, D])
    wT = sb("wT", [P, 3, 2, D])
    ident, ones = sb("ident", [P, P]), sb("ones", [P, P])
    mask = sb("mask", [P, HT])
    maski = sb("maski", [P, HT], mybir.dt.int32)
    keep = sb("keep", [P, HT])
    xin = sb("xin", [P, 2, T, D])
    st6, mv = sb("st6", [P, T, 6]), sb("mv", [P, T, 2])
    rstd = sb("rstd", [P, T])
    xn = sb("xn", [P, T, D])
    xT = sb("xT", [P, 2, HT])
    q_s, k_s = sb("q_s", [P, HT]), sb("k_s", [P, HT])
    gk1 = sb("gk1", [16, HT])
    za, zm, cum = sb("za", [P, HT]), sb("zm", [P, HT]), sb("cum", [P, HT])
    rel, tail = sb("rel", [P, HT]), sb("tail", [P, HT])
    e_in, e_out, e_cum, e_tail = (sb(f"e_{n}", [P, HT]) for n in ("in", "out", "cum", "tail"))
    decay = sb("decay", [P, NC])
    kt, qh, kh = (sb(n, [P, HT]) for n in ("kt", "qh", "kh"))
    qz = sb("qz", [P, T, H, P])
    khat = sb("khat", [P, T, P])
    V, G = sb("V", [P, T, D]), [sb(f"G{r}", [P, T, D]) for r in range(2)]
    AT = sb("AT", [P, T, H, P])
    S = sb("S", [P, NC + 1, DV])
    Sbd = sb("Sbd", [P, NC, D])
    o_s, o2 = sb("o_s", [P, T, D]), sb("o2", [P, T, D])
    ss, rs = sb("ss", [P, T * H]), sb("rs", [P, T * H])
    ogT = sb("ogT", [P, 2, HT])
    x1y = sb("x1y", [P, T, 2, D])
    st6b, mvb, rstdb = sb("st6b", [P, T, 6]), sb("mvb", [P, T, 2]), sb("rstdb", [P, T])
    sq, ssy, ry = sb("sq", [P, D]), sb("ssy", [P, T]), sb("ry", [P, T])
    xr = sb("xr", [P, T, D])
    xrT = sb("xrT", [P, 2, HT])
    hi, lo = sb("hi", [P, 4, HT], f32r), sb("lo", [P, 4, HT], f32r)
    v_s = sb("v_s", [P, 8, T, 64])
    mhalf = sb("mhalf", [P, T * H])
    p_f = ctx.enter_context(nc.psum_tensor("a_p_f", [P, 4, 512], f32))
    p_g = ctx.enter_context(nc.psum_tensor("a_p_g", [P, 4, 512], f32))

    names = ("w_in", "consts0", "consts", "wT_ps", "wT_done", "x_in0", "x_in1", "st_done", "mv_done", "rstd_done",
             "xn_done", "xT_ps", "xT_done", "gk1_ps", "gk1_done", "z_ps", "za_done", "e_z", "l_z", "zm_done", "q_ps", "k_ps", "q_done", "k_done",
             "g0", "g1", "cum_done", "rel_done", "tail_done", "exps", "qtkt", "hats", "khT_ps", "khat_done", "vg_ps",
             "vg_taken", "AT_ps", "AT_done", "inc_ps", "S_step", "S_carry", "Sbd_done", "o_ps",
             "o_s_done", "o2_done", "ss_done", "rs_done", "on_done", "og_done", "ogT_ps", "ogT_done", "wout_ps",
             "x1_done", "stb_done", "mvb_done", "rstdb_done", "y_done", "sq_done", "ry_done", "xr_done", "xrT_ps", "xrT_done",
             "qk2_ps", "hi_done", "lo_done", "v2_ps", "v_done", "rstd_eps", "rs_eps", "rstdb_eps", "ry_eps", "stored", "store_free", "zero",
             "dve_turn", "pe_turn", "pool_turn")
    s = {n: stage_semaphore(nc, ctx, "a_" + n) for n in names}

    x_v = x.rearrange("(n t p) d -> n p t d", p=P, t=T)
    x1y_v = x1y_d.rearrange("(n t p) e d -> n p t e d", p=P, t=T)
    qk_v = qk_d.rearrange("w c (b m p) t -> w c b p m t", m=2, p=P)

    N_HALVES = 2 * n_batches
    block = ctx.enter_context(nc.Block())

    def rounds(eng, body):
        if n_batches > 1:
            with eng.Fori(0, n_batches - 1) as b:
                body(b * 2, 0, b, b, True, True)
                body(b * 2 + 1, 1, b, b + 1, True, True)
        b = n_batches - 1
        body(b * 2, 0, b, b, True, False)
        body(b * 2 + 1, 1, b, b + 1, False, False)

    @block.sync
    def _(sp):
        two = lambda w: w.rearrange("(k p) n -> p k n", p=P)
        loads = [(Wgk1_s[:], two(Wgk1)), (Wgk2_s[:], Wgk2), (bgk_s[:], bgk2.rearrange("(p o) -> p o", o=1)),
                 (Wq_s[:], two(Wq)), (Wk_s[:], two(Wk)), (Wvg_s[:, :, 0:D], two(Wv)), (Wvg_s[:, :, D:2 * D], two(Wg)),
                 (Wout_s[:], two(Wout)), (rmsw_s[0:64, :], rms_w.rearrange("(p o) -> p o", o=1)),
                 (rmsw_s[64:128, :], rms_w.rearrange("(p o) -> p o", o=1)),
                 (w_raw[:, 0], two(wq)), (w_raw[:, 1], two(wk)), (w_raw[:, 2], two(wv))]
        for half in (0, 1):
            sp.dma_start(xin[:, half], x_v[half]).then_inc(s[f"x_in{half}"], 16)
        for dst, src in loads:
            sp.dma_start(dst, src).then_inc(s["w_in"], 16)
        with nc.allow_non_contiguous_dma("256 weights, once"):
            sp.dma_start(ln1w_s[:], ln1_w.rearrange("(k p) -> p k", p=P)).then_inc(s["w_in"], 16)

        def body(n, half, b, b_next, more, more2):
            if more2:
                sp.wait_ge(s["x1_done"], n + 1)
                sp.dma_start(xin[:, half], x_v[n + 2]).then_inc(s[f"x_in{half}"], 16)
            sp.wait_ge(s["y_done"], n + 1)
            sp.dma_start(x1y_v[n], x1y[:]).then_inc(s["stored"], 16)
            sp.wait_ge(s["lo_done"], n * 4 + 5)
            for part, buf in ((0, hi), (1, lo)):
                for which in (0, 1):
                    sp.dma_start(qk_v[which, part, b, :, :, half * HT:(half + 1) * HT],
                                 buf[:, 2 * which:2 * which + 2, :].bitcast(f32)).then_inc(s["stored"], 16)
            sp.wait_ge(s["v_done"], n + 2)
            sp.dma_start(v_d[b, :, :, half * T:(half + 1) * T, :].rearrange("a p t e -> p a (t e)"), v_s[:].rearrange("p a t e -> p a (t e)")).then_inc(s["stored"], 16)
            sp.wait_ge(s["stored"], n * 96 + 96)
            sp.sem_inc(s["store_free"], 1)
        rounds(sp, body)

    @block.scalar
    def _(act):
        A = nc.scalar

        def gate_and_values(f, r):
            act.wait_ge(s["xT_ps"], f + 1)
            A.copy(xT[:], p_f[:, 0:2]).then_inc(s["xT_done"], 1)
            act.wait_ge(s["gk1_ps"], f + 1)
            A.copy(gk1[:], p_f[0:16, 3, :]).then_inc(s["gk1_done"], 1)
            act.wait_ge(s["q_ps"], f + 1)
            A.copy(q_s[:], p_f[:, 0, :]).then_inc(s["q_done"], 1)
            act.wait_ge(s["z_ps"], f + 1)
            A.activation(za[:], p_f[:, 2, :], ACT.Abs, bias=bgk_s[:, 0:1]).then_inc(s["za_done"], 1)
            act.wait_ge(s["za_done"], f + 1)
            A.activation(e_in[:], za[:], ACT.Exp, scale=-1.0).then_inc(s["e_z"], 1)
            act.wait_ge(s["e_z"], f + 1)
            A.activation(za[:], e_in[:], ACT.Ln, bias=ones[:, 0:1]).then_inc(s["l_z"], 1)
            act.wait_ge(s["k_ps"], f + 1)
            A.copy(k_s[:], p_f[:, 1, :]).then_inc(s["k_done"], 1)
            for t in range(T):
                act.wait_ge(s["vg_ps"], f * T + (t + 1))
                A.copy(V[:, t], p_f[:, (3, 0)[t % 2], 0:D])
                A.activation(G[r][:, t], p_f[:, (3, 0)[t % 2], D:2 * D], ACT.Silu).then_inc(s["vg_taken"], 1)

        def decays(f):
            act.wait_ge(s["tail_done"], f + 1)
            A.activation(e_in[:], rel[:], ACT.Exp)
            A.activation(e_out[:], rel[:], ACT.Exp, scale=-1.0)
            A.activation(e_tail[:], tail[:], ACT.Exp)
            A.activation(e_cum[:], cum[:], ACT.Exp)
            A.activation(decay[:], cum[:].rearrange("p (c j) -> p c j", j=C)[:, :, C - 1], ACT.Exp).then_inc(s["exps"], 1)

        def keys(f):
            act.wait_ge(s["khT_ps"], f + 1)
            A.copy(khat[:], p_f[:, 3].rearrange("p (t c) -> p t c", t=T)).then_inc(s["khat_done"], 1)

        def states(f):
            act.wait_ge(s["S_step"], f * NC + NC)
            for h in range(H):
                last = A.copy(Sbd[h * DK:(h + 1) * DK, :, h * DV:(h + 1) * DV], S[h * DK:(h + 1) * DK, 0:NC, :])
            last.then_inc(s["Sbd_done"], 1)

        gate_and_values(0, 0)
        decays(0)
        keys(0)
        states(0)

        def body(n, half, b, b_next, more, more2):
            n1 = n + 1
            act.wait_ge(s["o_ps"], n1)
            A.copy(o_s[:].rearrange("p t d -> p (t d)"), p_g[:, 0:2].rearrange("p a c -> p (a c)")).then_inc(s["o_s_done"], 1)
            A.activation(o2[:].rearrange("p t d -> p (t d)"), p_g[:, 0:2].rearrange("p a c -> p (a c)"), ACT.Square, scale=DV ** -0.5).then_inc(s["o2_done"], 1)
            if more:
                gate_and_values(n + 1, 1 - half)
            act.wait_ge(s["ogT_ps"], n1)
            A.mul(ogT[:], p_g[:, 2:4], rmsw_s[:, 0:1]).then_inc(s["ogT_done"], 1)
            if more:
                decays(n + 1)
                keys(n + 1)
            act.wait_ge(s["y_done"], n1)
            for t in range(T):
                act.wait_ge(s["sq_done"], n * T + (t + 1))
                A.activation(sq[:], x1y[:, t, 1], ACT.Square, scale=D ** -0.5, accum_out=ssy[:, t:t + 1]).then_inc(s["sq_done"], 1)
            act.wait_ge(s["xrT_ps"], n1)
            A.mul(xrT[:, 0], p_g[:, 2], ln1w_s[:, 0:1])
            A.mul(xrT[:, 1], p_g[:, 3], ln1w_s[:, 1:2]).then_inc(s["xrT_done"], 1)
            act.wait_ge(s["store_free"], n1)
            for j in range(4):
                act.wait_ge(s["qk2_ps"], n * 4 + (j + 1))
                A.copy(hi[:, j], p_g[:, j]).then_inc(s["hi_done"], 1)
                if j == 1 and more:
                    states(n + 1)
            act.wait_ge(s["v2_ps"], n1)
            for t in range(T):
                last = A.copy(v_s[:, :, t, :].rearrange("p a (h e) -> p a h e", h=2)[:, :, :, 0:16],
                              p_g[:, t // 2, (t % 2) * D:(t % 2 + 1) * D].rearrange("p (a h e) -> p a h e", a=8, h=2))
            last.then_inc(s["v_done"], 1)
        rounds(act, body)

    @block.vector
    def _(dve):
        V_ = nc.vector
        V_.memset(ones[:], 1.0)
        V_.memset(v_s[:], 1.0)
        V_.memset(AT[:], 0.0)
        V_.memset(qz[:], 0.0)
        V_.memset(Sbd[:], 0.0)
        V_.memset(keep[:], 1.0).then_inc(s["consts0"], 1)
        dve.wait_ge(s["consts0"], 2)
        V_.memset(keep[:].rearrange("p (c j) -> p c j", j=C)[:, :, 0:1], 0.0)
        V_.tensor_copy(maski[:], mask[:]).then_inc(s["consts"], 1)
        dve.wait_ge(s["consts"], 1)
        for j in range(3):
            dve.wait_ge(s["wT_ps"], j + 1)
            V_.tensor_copy(wT[:, j].rearrange("p k m -> p (k m)"), p_g[:, j]).then_inc(s["wT_done"], 1)
        dve.sem_inc(s["sq_done"], 1)
        dve.sem_inc(s["store_free"], 1)
        dve.sem_inc(s["lo_done"], 1)
        dve.sem_inc(s["v_done"], 1)

        def statistics(f, r, b):
            dve.wait_ge(s[f"x_in{r}"], b * 16 + 16)
            for t in range(T):
                last = V_.bn_stats(st6[:, t], xin[:, r, t])
            last.then_inc(s["st_done"], 1)
            dve.wait_ge(s["st_done"], f + 1)
            dve.sem_inc(s["dve_turn"], 1)
            for t in range(T):
                last = V_.bn_aggr(mv[:, t], st6[:, t])
            last.then_inc(s["mv_done"], 1)

        def normalise(f, r):
            dve.wait_ge(s["rstd_done"], f + 1)
            for t in range(T):
                last = V_.tensor_scalar(xn[:, t], xin[:, r, t], mv[:, t, 0:1], rstd[:, t:t + 1], ALU.subtract, ALU.mult)
            last.then_inc(s["xn_done"], 1)

        def running_sums(f):
            dve.wait_ge(s["z_ps"], f + 1)
            dve.wait_ge(s["za_done"], f + 1)
            V_.tensor_scalar(zm[:], p_f[:, 2, :], bgk_s[:, 0:1], 0.0, ALU.add, ALU.min).then_inc(s["zm_done"], 1)
            dve.wait_ge(s["l_z"], f + 1)
            dve.wait_ge(s["zm_done"], f + 1)
            V_.tensor_tensor(zm[:], zm[:], za[:], ALU.subtract).then_inc(s["g0"], 1)
            dve.wait_ge(s["g0"], f + 1)
            V_.tensor_scalar(zm[:], zm[:], 1.0 / 16.0, -3.0, ALU.mult, ALU.max).then_inc(s["g1"], 1)
            dve.wait_ge(s["g1"], f + 1)
            V_.tensor_tensor_scan(cum[:], keep[:], zm[:], 0.0, ALU.mult, ALU.add).then_inc(s["cum_done"], 1)
            dve.wait_ge(s["cum_done"], f + 1)
            cc = cum[:].rearrange("p (c j) -> p c j", j=C)
            V_.tensor_tensor(rel[:].rearrange("p (c j) -> p c j", j=C), cc,
                             cc[:, :, C // 2 - 1:C // 2].to_broadcast([P, NC, C]), ALU.subtract)
            V_.tensor_tensor(tail[:].rearrange("p (c j) -> p c j", j=C),
                             cc[:, :, C - 1:C].to_broadcast([P, NC, C]), cc, ALU.subtract).then_inc(s["tail_done"], 1)

        def decayed(f):
            dve.wait_ge(s["q_done"], f + 1)
            dve.wait_ge(s["k_done"], f + 1)
            dve.wait_ge(s["exps"], f + 1)
            V_.tensor_tensor(kt[:], k_s[:], e_out[:], ALU.mult)
            for h in range(H):
                rows = slice(h * DK, (h + 1) * DK)
                last = V_.tensor_tensor(qz[rows, :, h, :], q_s[rows, :].rearrange("p (t c) -> p t c", t=T),
                                        e_in[rows, :].rearrange("p (t c) -> p t c", t=T), ALU.mult)
            last.then_inc(s["qtkt"], 1)

        def within_chunks(f):
            for t in range(T):
                dve.wait_ge(s["AT_ps"], f * T + (t + 1))
                dve.sem_inc(s["dve_turn"], 1)
                V_.copy_predicated(AT[:, t].rearrange("p h c -> p (h c)"), maski[:], p_f[:, t]).then_inc(s["AT_done"], 1)

        def states(f, half):
            dve.wait_ge(s["inc_ps"], f + 1)
            for c in range(NC):
                if c > 0:
                    dve.wait_ge(s["S_step"], f * NC + c)
                elif half == 1:
                    dve.wait_ge(s["S_carry"], f + 1)
                else:
                    V_.memset(S[:, 0], 0.0).then_inc(s["S_carry"], 1)
                    dve.wait_ge(s["S_carry"], f + 1)
                V_.scalar_tensor_tensor(S[:, c + 1], S[:, c], decay[:, c:c + 1], p_f[:, c % 4, (c // 4) * DV:(c // 4 + 1) * DV],
                                        ALU.mult, ALU.add).then_inc(s["S_step"], 1)

        def carry(f, half):
            if half == 0:
                dve.wait_ge(s["Sbd_done"], f + 1)
                V_.tensor_copy(S[:, 0], S[:, NC]).then_inc(s["S_carry"], 1)

        statistics(0, 0, 0)
        normalise(0, 0)
        running_sums(0)
        statistics(1, 1, 0)
        decayed(0)
        within_chunks(0)
        states(0, 0)
        normalise(1, 1)
        carry(0, 0)

        def body(n, half, b, b_next, more, more2):
            n1 = n + 1
            dve.wait_ge(s["o2_done"], n1)
            V_.reduce_sum(ss[:], o2[:].rearrange("p t (h v) -> p (t h) v", h=H), AX.X).then_inc(s["ss_done"], 1)
            dve.wait_ge(s["rs_done"], n1)
            ov = o_s[:].rearrange("p t (h v) -> p (t h) v", h=H)
            V_.tensor_tensor(ov, ov, rs[:].rearrange("p (a o) -> p a o", o=1).to_broadcast([P, T * H, DV]), ALU.mult).then_inc(s["on_done"], 1)
            dve.wait_ge(s["on_done"], n1)
            V_.tensor_tensor(o_s[:], o_s[:], G[half][:], ALU.mult).then_inc(s["og_done"], 1)
            if more:
                running_sums(n + 1)
                decayed(n + 1)
            dve.wait_ge(s["wout_ps"], n1)
            dve.wait_ge(s["store_free"], n1)
            V_.tensor_tensor(x1y[:, :, 0], p_g[:, 0:2].rearrange("p a (e c) -> p (a e) c", e=2), xin[:, half], ALU.add).then_inc(s["x1_done"], 1)
            dve.wait_ge(s["x1_done"], n1)
            for t in range(T):
                last = V_.bn_stats(st6b[:, t], x1y[:, t, 0])
            last.then_inc(s["stb_done"], 1)
            dve.wait_ge(s["stb_done"], n1)
            dve.sem_inc(s["dve_turn"], 1)
            for t in range(T):
                last = V_.bn_aggr(mvb[:, t], st6b[:, t])
            last.then_inc(s["mvb_done"], 1)
            dve.wait_ge(s["rstdb_done"], n1)
            for t in range(T):
                last = V_.tensor_scalar(x1y[:, t, 1], x1y[:, t, 0], mvb[:, t, 0:1], rstdb[:, t:t + 1], ALU.subtract, ALU.mult)
            last.then_inc(s["y_done"], 1)
            if more:
                within_chunks(n + 1)
            dve.wait_ge(s["ry_done"], n1)
            for t in range(T):
                last = V_.tensor_scalar(xr[:, t], x1y[:, t, 1], ry[:, t:t + 1], None, ALU.mult)
            last.then_inc(s["xr_done"], 1)
            if more2:
                statistics(n + 2, half, b + 1)
            if more:
                states(n + 1, 1 - half)
            for j in range(4):
                dve.wait_ge(s["hi_done"], n * 4 + (j + 1))
                V_.tensor_tensor(lo[:, j], p_g[:, j], hi[:, j].bitcast(f32), ALU.subtract).then_inc(s["lo_done"], 1)
                if j == 0 and more2:
                    normalise(n + 2, half)
            if more:
                carry(n + 1, 1 - half)
        rounds(dve, body)

    @block.gpsimd
    def _(pool):
        g = nc.gpsimd
        g.memset(ident[:], 0.0)
        g.memset(mhalf[:], -0.5)
        g.memset(mask[:], 1.0).then_inc(s["zero"], 1)
        pool.wait_ge(s["zero"], 1)
        g.affine_select(out=ident[:], in_=ident[:], compare_op=ALU.not_equal, fill=1.0, base=0, pattern=[[-1, P]], channel_multiplier=1)
        m4 = mask[:].rearrange("p (t c j) -> p t c j", c=4, j=C)
        g.affine_select(out=m4, in_=m4, compare_op=ALU.is_ge, fill=0.0, base=0, pattern=[[0, T], [-C, 4], [0, C]], channel_multiplier=1).then_inc(s["zero"], 1)
        pool.wait_ge(s["zero"], 2)
        g.affine_select(out=m4, in_=m4, compare_op=ALU.is_ge, fill=0.0, base=0, pattern=[[0, T], [C, 4], [1, C]], channel_multiplier=-1).then_inc(s["consts0"], 1)

        def inverse_root(out, src, width, ready, count, eps_done, done, times):
            pool.wait_ge(s[ready], count)
            pool.sem_inc(s["pool_turn"], 1)
            g.tensor_scalar(out, src, EPS, None, ALU.add).then_inc(s[eps_done], 1)
            pool.wait_ge(s[eps_done], times)
            g.tensor_tensor(out, out, mhalf[:, 0:width], ALU.pow).then_inc(s[done], 1)

        def front_root(f):
            inverse_root(rstd[:], mv[:, :, 1], T, "mv_done", f + 1, "rstd_eps", "rstd_done", f + 1)

        def hats(f):
            pool.wait_ge(s["q_done"], f + 1)
            pool.wait_ge(s["k_done"], f + 1)
            pool.wait_ge(s["exps"], f + 1)
            g.tensor_tensor(kh[:], k_s[:], e_tail[:], ALU.mult).then_inc(s["hats"], 1)
            g.tensor_tensor(qh[:], q_s[:], e_cum[:], ALU.mult).then_inc(s["hats"], 1)

        front_root(0)
        front_root(1)
        hats(0)

        def body(n, half, b, b_next, more, more2):
            inverse_root(rs[:], ss[:], T * H, "ss_done", n + 1, "rs_eps", "rs_done", n + 1)
            if more:
                hats(n + 1)
            inverse_root(rstdb[:], mvb[:, :, 1], T, "mvb_done", n + 1, "rstdb_eps", "rstdb_done", n + 1)
            inverse_root(ry[:], ssy[:], T, "sq_done", n * T + (T + 1), "ry_eps", "ry_done", n + 1)
            if more2:
                front_root(n + 2)
        rounds(pool, body)

    @block.tensor
    def _(pe):
        mm, tr = nc.tensor.matmul, nc.tensor.transpose
        pe.wait_ge(s["w_in"], 14 * 16)
        pe.wait_ge(s["consts"], 1)
        for j in range(3):
            for k in range(2):
                for m in range(2):
                    last = tr(p_g[:, j, k * D + m * P:k * D + (m + 1) * P], w_raw[:, j, m, k * P:(k + 1) * P], ident[:])
            last.then_inc(s["wT_ps"], 1)
        pe.wait_ge(s["wT_done"], 3)

        def transposes(dst, src, done):
            for k in range(2):
                for t in range(T):
                    last = tr(dst[:, k, t * P:(t + 1) * P], src[:, t, k * P:(k + 1) * P], ident[:])
            last.then_inc(done, 1)

        def input_transposes(f):
            pe.wait_ge(s["xn_done"], f + 1)
            transposes(p_f[:, 0:2], xn, s["xT_ps"])

        def projections(f):
            pe.wait_ge(s["xT_done"], f + 1)
            for bank, w, m, done in ((3, Wgk1_s, 16, "gk1_ps"), (0, Wq_s, P, "q_ps")):
                for k in range(2):
                    last = mm(p_f[0:m, bank, :], w[:, k, :], xT[:, k, :], start=(k == 0), stop=(k == 1))
                last.then_inc(s[done], 1)
            pe.wait_ge(s["gk1_done"], f + 1)
            mm(p_f[:, 2, :], Wgk2_s[:], gk1[:], start=True, stop=True).then_inc(s["z_ps"], 1)
            for k in range(2):
                last = mm(p_f[:, 1, :], Wk_s[:, k, :], xT[:, k, :], start=(k == 0), stop=(k == 1))
            last.then_inc(s["k_ps"], 1)
            for t in range(T):
                if t == 1:
                    pe.wait_ge(s["q_done"], f + 1)
                elif t >= 2:
                    pe.wait_ge(s["vg_taken"], f * T + (t - 1))
                for k in range(2):
                    last = mm(p_f[:, (3, 0)[t % 2], :], xT[:, k, t * P:(t + 1) * P], Wvg_s[:, k, :], start=(k == 0), stop=(k == 1))
                last.then_inc(s["vg_ps"], 1)

        def chunks(f):
            pe.wait_ge(s["vg_taken"], f * T + T)
            pe.wait_ge(s["hats"], f * 2 + 1)
            for t in range(T):
                last = tr(p_f[:, 3, t * P:(t + 1) * P], kh[:, t * P:(t + 1) * P], ident[:])
            last.then_inc(s["khT_ps"], 1)
            pe.wait_ge(s["qtkt"], f + 1)
            for t in range(T):
                if t == 3:
                    pe.wait_ge(s["khat_done"], f + 1)
                mm(p_f[:, t], kt[:, t * P:(t + 1) * P], qz[:, t].rearrange("p h c -> p (h c)"), start=True, stop=True).then_inc(s["AT_ps"], 1)
            pe.wait_ge(s["AT_done"], f * T + T)
            pe.sem_inc(s["pe_turn"], 1)
            for t in range(T):
                for c in range(4):
                    for h in range(H):
                        rows = slice(c * C, (c + 1) * C)
                        last = mm(p_f[h * DK:(h + 1) * DK, c, t * DV:(t + 1) * DV], khat[rows, t, h * DK:(h + 1) * DK],
                                  V[rows, t, h * DV:(h + 1) * DV], start=True, stop=True)
            last.then_inc(s["inc_ps"], 1)

        input_transposes(0)
        projections(0)
        chunks(0)

        def body(n, half, b, b_next, more, more2):
            n1 = n + 1
            pe.wait_ge(s["Sbd_done"], n1)
            pe.wait_ge(s["hats"], n * 2 + 2)
            if more:
                input_transposes(n + 1)
            pe.wait_ge(s["v_done"], n1)
            for t in range(T):
                bank, at = t // 2, (t % 2) * D
                for c in range(4):
                    mm(p_g[c * C:(c + 1) * C, bank, at:at + D], qh[:, t * P + c * C:t * P + (c + 1) * C], Sbd[:, t * 4 + c, :],
                       start=True, stop=False, skip_group_check=True)
                for h in range(H):
                    last = mm(p_g[:, bank, at + h * DV:at + (h + 1) * DV], AT[:, t, h, :], V[:, t, h * DV:(h + 1) * DV],
                              start=False, stop=True, skip_group_check=True)
            last.then_inc(s["o_ps"], 1)
            if more:
                projections(n + 1)
            pe.wait_ge(s["og_done"], n1)
            pe.wait_ge(s["lo_done"], n * 4 + 1)
            transposes(p_g[:, 2:4], o_s, s["ogT_ps"])
            pe.wait_ge(s["ogT_done"], n1)
            for t in range(T):
                bank, at = t // 2, (t % 2) * D
                for k in range(2):
                    last = mm(p_g[:, bank, at:at + D], ogT[:, k, t * P:(t + 1) * P], Wout_s[:, k, :], start=(k == 0), stop=(k == 1))
            last.then_inc(s["wout_ps"], 1)
            if more:
                chunks(n + 1)
            pe.wait_ge(s["xr_done"], n1)
            transposes(p_g[:, 2:4], xr, s["xrT_ps"])
            pe.wait_ge(s["xrT_done"], n1)
            for j in range(4):
                for k in range(2):
                    last = mm(p_g[:, j, :], wT[:, j // 2, k, (j % 2) * P:(j % 2 + 1) * P], xrT[:, k, :], start=(k == 0), stop=(k == 1))
                last.then_inc(s["qk2_ps"], 1)
            pe.wait_ge(s["lo_done"], n * 4 + 3)
            for t in range(T):
                bank, at = t // 2, (t % 2) * D
                for k in range(2):
                    last = mm(p_g[:, bank, at:at + D], xrT[:, k, t * P:(t + 1) * P], wT[:, 2, k, :], start=(k == 0), stop=(k == 1))
            last.then_inc(s["v2_ps"], 1)
        rounds(pe, body)


def softmax_attention(nc, ctx, qk_d, v_d, o_d, n_batches=8):
    P, N, KT = 128, 1024, 8
    R = 64
    RING = 4
    PAIRS = 8 * n_batches
    f32, f32r = mybir.dt.float32, mybir.dt.float32r
    ALU, ACT, AX = mybir.AluOpType, mybir.ActivationFunctionType, mybir.AxisListType
    SCALE = 0.25

    def sb(name, shape, dt=f32):
        return ctx.enter_context(nc.sbuf_tensor("b_" + name, shape, dt))

    def sem(name):
        return stage_semaphore(nc, ctx, "b_" + name)

    qst = [sb(f"qst{r}", [P, N], f32r) for r in range(RING)]
    kst = [[sb(f"kst{r}_{h}", [P, N], f32r) for h in range(2)] for r in range(RING)]
    vst = [sb(f"vst{r}", [P, KT, 2, 32]) for r in range(RING)]
    ones, zrow = sb("ones", [2, N]), sb("zrow", [2, N])
    ident = sb("ident", [P, P])
    mx, mxq = sb("mx", [P, 16, 2]), sb("mxq", [P, 16])
    nm_hi, nm_lo = [sb(f"nm_hi{r}", [16, P], f32r) for r in range(2)], [sb(f"nm_lo{r}", [16, P], f32r) for r in range(2)]
    probs = [sb(f"probs{r}", [P, N]) for r in range(4)]
    oT = sb("oT", [P, 512])
    rden = sb("rden", [P, 4, 4])
    o_s = [sb(f"o_s{r}", [P, KT, 2, 16]) for r in range(2)]
    p_e = [ctx.enter_context(nc.psum_tensor(f"b_p_e{r}", [P, N], f32)) for r in range(2)]
    p_m = [ctx.enter_context(nc.psum_tensor(f"b_p_m{r}", [P, 512], f32)) for r in range(2)]
    p_o = ctx.enter_context(nc.psum_tensor("b_p_o", [P, 512], f32))
    p_t = ctx.enter_context(nc.psum_tensor("b_p_t", [P, 4, P], f32))

    names = ("consts", "ident0", "id", "rows", "free", "m_ps", "m_red", "mxq_done", "mT_ps", "mT_read", "nm_done",
             "e_ps", "e_done", "pv_done", "oT_done", "oT_ps", "rden_done", "o_done", "o_stored", "o_free",
             *(f"q_in{r}" for r in range(RING)), *(f"m_in{r}" for r in range(RING)), "start")
    s = {n: sem(n) for n in names}
    q_rows = qk_d.rearrange("w c (g r) t -> g w c r t", r=32)
    v_rows = v_d.rearrange("b a p t e -> (b a) p (t e)")
    o_rows = o_d.rearrange("b a p t e -> (b a) p (t e)")
    LOADS = 15
    STEPS = PAIRS // RING

    def pairs(eng, body):
        with eng.Fori(0, STEPS - 1) as i:
            for r in range(RING):
                body(i * RING + r, i, r, True, True)
        for r in range(RING):
            body((STEPS - 1) * RING + r, STEPS - 1, r, r < RING - 2, r < RING - 3)

    def ahead(i, r):
        return (i + 1, r - 2) if r >= 2 else (i, r + 2)

    block = ctx.enter_context(nc.Block())

    @block.sync
    def _(sp):
        sp.wait_ge(s["consts"], 1)
        for r in range(RING):
            for h in range(2):
                sp.dma_start(kst[r][h][R * h + 48:R * h + 50, :].bitcast(f32), ones[:]).then_inc(s["rows"], 16)

        def load(pair, r):
            for h in range(2):
                at, row = R * h, 16 * h
                sp.dma_start(qst[r][at:at + 16, :].bitcast(f32), q_rows[pair, 0, 0, row:row + 16, :]).then_inc(s[f"q_in{r}"], 16)
                sp.dma_start(qst[r][at + 16:at + 32, :].bitcast(f32), q_rows[pair, 0, 1, row:row + 16, :]).then_inc(s[f"q_in{r}"], 16)
                sp.dma_start(qst[r][at + 32:at + 48, :].bitcast(f32), q_rows[pair, 0, 0, row:row + 16, :]).then_inc(s[f"q_in{r}"], 16)
                sp.dma_start(kst[r][h][at:at + 16, :].bitcast(f32), q_rows[pair, 1, 0, row:row + 16, :]).then_inc(s[f"q_in{r}"], 16)
                sp.dma_start(kst[r][h][at + 16:at + 32, :].bitcast(f32), q_rows[pair, 1, 0, row:row + 16, :]).then_inc(s[f"q_in{r}"], 16)
                sp.dma_start(kst[r][h][at + 32:at + 48, :].bitcast(f32), q_rows[pair, 1, 1, row:row + 16, :]).then_inc(s[f"q_in{r}"], 16)
                sp.dma_start(qst[r][at + 48:at + 50, :].bitcast(f32), zrow[:]).then_inc(s[f"q_in{r}"], 16)
            sp.dma_start(vst[r][:].rearrange("p t h e -> p (t h e)"), v_rows[pair]).then_inc(s[f"q_in{r}"], 16)

        def maxima(pair, half, r):
            sp.wait_ge(s["nm_done"], (pair + 1) * 1)
            for h in range(2):
                for k, nm in enumerate((nm_hi[half], nm_lo[half])):
                    sp.dma_start(qst[r][R * h + 48 + k:R * h + 49 + k, :].bitcast(f32).rearrange("o (c j) -> o c j", c=8),
                                 nm[8 * h:8 * h + 8, :].bitcast(f32)).then_inc(s[f"m_in{r}"], 16)

        for r in range(3):
            load(r, r)
        maxima(0, 0, 0)
        maxima(1, 1, 1)

        def body(pair, i, r, more, more3):
            if more3:
                sp.wait_ge(s["pv_done"], pair * KT + 2)
                load(pair + 3, (r + 3) % RING)
            if more:
                maxima(pair + 2, r % 2, (r + 2) % RING)
        pairs(sp, body)

    @block.scalar
    def _(act):
        def negated(pair, half):
            act.wait_ge(s["mT_ps"], pair + 1)
            nc.scalar.mul(nm_hi[half][:], p_t[0:16, 0, :], -1.0).then_inc(s["mT_read"], 1)

        negated(0, 0)
        negated(1, 1)

        def body(pair, i, r, more, more3):
            for e in range(2 * KT):
                act.wait_ge(s["e_ps"], pair * 16 + (e + 1))
                act.wait_ge(s["pv_done"], pair * KT + (e // 2 + 1))
                nc.scalar.activation(probs[e % 4][:], p_e[e % 2][:], ACT.Exp, scale=SCALE).then_inc(s["e_done"], 1)
            if more:
                negated(pair + 2, r % 2)
        pairs(act, body)

    @block.gpsimd
    def _(pool):
        g = nc.gpsimd
        g.memset(ident[:], 0.0).then_inc(s["ident0"], 1)
        pool.wait_ge(s["ident0"], 1)
        g.affine_select(out=ident[:], in_=ident[:], compare_op=ALU.not_equal, fill=1.0, base=0, pattern=[[-1, P]], channel_multiplier=1).then_inc(s["id"], 1)

        def body(pair, i, r, more, more3):
            pool.wait_ge(s["o_done"], pair + 2)
            g.dma_start(o_rows[pair], o_s[r % 2][:].rearrange("p t h e -> p (t h e)")).then_inc(s["o_stored"], 16)
            pool.wait_ge(s["o_stored"], pair * 16 + 16)
            pool.sem_inc(s["o_free"], 1)
        pairs(pool, body)

    @block.vector
    def _(dve):
        V_ = nc.vector
        V_.memset(ones[:], 1.0)
        V_.memset(zrow[:], 0.0)
        for r in range(RING):
            V_.memset(qst[r][:].bitcast(f32), 0.0)
            for h in range(2):
                i = V_.memset(kst[r][h][:].bitcast(f32), 0.0)
        i.then_inc(s["consts"], 1)
        V_.memset(oT[:], 1.0).then_inc(s["start"], 1)
        dve.sem_inc(s["pv_done"], 2)
        dve.sem_inc(s["e_done"], 2)
        dve.sem_inc(s["m_red"], 2)
        dve.sem_inc(s["oT_done"], 1)
        dve.sem_inc(s["o_free"], 3)

        def reduce(pair, j):
            dve.wait_ge(s["m_ps"], pair * 32 + (j + 1))
            V_.reduce_max(mx[:, j // 2, j % 2:j % 2 + 1], p_m[j % 2][:], AX.X).then_inc(s["m_red"], 1)

        def combine(pair):
            dve.wait_ge(s["m_red"], pair * 32 + 34)
            V_.tensor_tensor(mxq[:], mx[:, :, 0], mx[:, :, 1], ALU.max).then_inc(s["mxq_done"], 1)

        def low_part(pair, half):
            dve.wait_ge(s["mT_read"], pair + 1)
            V_.scalar_tensor_tensor(nm_lo[half][:], p_t[0:16, 0, :], -1.0, nm_hi[half][:].bitcast(f32), ALU.mult, ALU.subtract).then_inc(s["nm_done"], 1)

        for pair in range(2):
            for j in range(32):
                reduce(pair, j)
            combine(pair)
            low_part(pair, pair)

        def normalise(n, half):
            dve.wait_ge(s["oT_ps"], n + 1)
            ot = p_t[:].rearrange("p q (h a e) -> p q h a e", h=2, a=2)
            V_.reciprocal(rden[:].rearrange("p q (h a) -> p q h a", h=2), ot[:, :, :, :, 16]).then_inc(s["rden_done"], 1)
            dve.wait_ge(s["rden_done"], n + 1)
            dve.wait_ge(s["o_free"], n + 1)
            for a in range(2):
                last = V_.tensor_tensor(o_s[half][:, a * 4:a * 4 + 4], ot[:, :, :, a, 0:16],
                                        rden[:].rearrange("p q (h a o) -> p q h a o", h=2, o=1)[:, :, :, a].to_broadcast([P, 4, 2, 16]), ALU.mult)
            last.then_inc(s["o_done"], 1)

        def body(pair, i, r, more, more3):
            if more:
                for j in range(8):
                    reduce(pair + 2, j)
            normalise(pair, (r + 1) % 2)
            if more:
                for j in range(8, 32):
                    reduce(pair + 2, j)
                combine(pair + 2)
            dve.wait_ge(s["pv_done"], pair * KT + (KT + 2))
            V_.tensor_copy(oT[:], p_o[:]).then_inc(s["oT_done"], 1)
            if more:
                low_part(pair + 2, r % 2)
        pairs(dve, body)
        normalise(PAIRS, 1)

    @block.tensor
    def _(pe):
        mm, tr = nc.tensor.matmul, nc.tensor.transpose
        pe.wait_ge(s["id"], 1)
        pe.wait_ge(s["start"], 1)
        pe.wait_ge(s["rows"], 16 * 2 * RING)

        def max_scores(pair, r, j):
            h, qt, kh = j // 16, j // 2 % 8, j % 2
            pe.wait_ge(s["m_red"], pair * 32 + (j + 1))
            mm(p_m[j % 2][:], qst[r][:, qt * P:(qt + 1) * P], kst[r][h][:, kh * 512:(kh + 1) * 512], start=True, stop=True).then_inc(s["m_ps"], 1)

        def max_transpose(pair):
            pe.wait_ge(s["mxq_done"], pair + 1)
            tr(p_t[0:16, 0, :], mxq[:], ident[:]).then_inc(s["mT_ps"], 1)

        def output_transpose(n):
            pe.wait_ge(s["nm_done"], n + 2 if not isinstance(n, int) else min(n + 2, PAIRS))
            pe.wait_ge(s["oT_done"], n + 1)
            if isinstance(n, int):
                pe.wait_ge(s["o_done"], n) if n else None
            for q in range(4):
                last = tr(p_t[:, q, :], oT[:, q * P:(q + 1) * P], ident[:])
            last.then_inc(s["oT_ps"], 1)

        def loaded(r, i):
            pe.wait_ge(s[f"q_in{r}"], i * (16 * LOADS) + 16 * LOADS)

        for pair in range(2):
            loaded(pair, 0)
            for j in range(32):
                max_scores(pair, pair, j)
            max_transpose(pair)
            pe.wait_ge(s["nm_done"], pair + 1)

        def body(pair, i, r, more, more3):
            i2, r2 = ahead(i, r)
            pe.wait_ge(s[f"m_in{r}"], i * 64 + 64)

            def values(kt):
                pe.wait_ge(s["e_done"], pair * 16 + (2 * kt + 4))
                for h in range(2):
                    for a in range(2):
                        last = mm(p_o[32 * (2 * h + a):32 * (2 * h + a) + 32, :], vst[r][:, kt, h, :],
                                  probs[(2 * kt + h) % 4][:, a * 512:(a + 1) * 512], start=(kt == 0), stop=(kt == KT - 1))
                last.then_inc(s["pv_done"], 1)

            if more:
                loaded(r2, i2)
            for kt in range(KT):
                for h in range(2):
                    pe.wait_ge(s["e_done"], pair * 16 + (2 * kt + h + 1))
                    for a in range(2):
                        last = mm(p_e[h][:, a * 512:(a + 1) * 512], kst[r][h][:, kt * P:(kt + 1) * P], qst[r][:, a * 512:(a + 1) * 512], start=True, stop=True)
                    last.then_inc(s["e_ps"], 1)
                    if more:
                        max_scores(pair + 2, r2, 4 * kt + h)
                if kt == 0:
                    pe.wait_ge(s["oT_done"], pair + 1)
                if kt > 0:
                    values(kt - 1)
                if more:
                    max_scores(pair + 2, r2, 4 * kt + 2)
                if kt == 1:
                    output_transpose(pair)
                if more:
                    max_scores(pair + 2, r2, 4 * kt + 3)
            values(KT - 1)
            if more:
                pe.wait_ge(s["o_done"], pair + 1)
                max_transpose(pair + 2)
        pairs(pe, body)
        output_transpose(PAIRS)


def output_projection_and_gate(nc, ctx, o_d, x1y_d, wo, gate_w, ln2_w, base_d, xg_d, chosen, share, n_batches=8):
    P, D, T, NE = 128, 256, 4, 8
    HT = P * T
    EPS = 1e-5
    f32 = mybir.dt.float32
    ALU, ACT, AX = mybir.AluOpType, mybir.ActivationFunctionType, mybir.AxisListType

    def sb(name, shape, dt=f32):
        return ctx.enter_context(nc.sbuf_tensor("c_" + name, shape, dt))

    wo_raw, woT = sb("wo_raw", [P, 2, D]), sb("woT", [P, 2, D])
    gw_raw, gwT = sb("gw_raw", [NE, D]), sb("gwT", [P, 2, NE])
    ln2 = sb("ln2", [P, 2])
    ident, mhalf = sb("ident", [P, P]), sb("mhalf", [P, T])
    oin, xy = [sb(f"oin{r}", [P, 8, T, 32]) for r in range(2)], [sb(f"xy{r}", [P, T, 2, D]) for r in range(2)]
    orow = [sb(f"orow{r}", [P, T, 8, 32]) for r in range(2)]
    oT, xgT = sb("oT", [P, 2, HT]), sb("xgT", [P, 2, HT])
    h = sb("h", [P, T, D])
    base, xg = [sb(f"base{r}", [P, T, D]) for r in range(2)], [sb(f"xg{r}", [P, T, D]) for r in range(2)]
    sq, ms, r_s = sb("sq", [P, D]), sb("ms", [P, T]), sb("r_s", [P, T])
    lg, top, tidx = sb("lg", [P, T, NE]), sb("top", [P, T, 8]), sb("tidx", [P, T, 8], mybir.dt.uint32)
    diff, ed, den = sb("diff", [P, T]), sb("ed", [P, T]), sb("den", [P, T])
    sh = sb("sh", [P, T, 2])
    p1, p2, p3 = (ctx.enter_context(nc.psum_tensor(f"c_p{i}", [P, 2, 512], f32)) for i in (1, 2, 3))
    p4 = ctx.enter_context(nc.psum_tensor("c_p4", [P, T, NE], f32))
    names = ("w_in", "zero", "consts", "wT_ps", "wT_done", "in0", "in1", "orow_done", "in_free", "oT_ps", "oT_done", "h_ps", "h_done", "ms_done",
             "ms_eps", "r_done", "xg_done", "base_done", "st0", "st1", "st_free", "xgT_ps", "xgT_done", "lg_ps", "lg_done", "top_done", "tidx_done",
             "diff_done", "ed_done", "den_done", "rec_done", "sh_done", "copied", "dve_turn", "pool_turn")
    s = {n: stage_semaphore(nc, ctx, "c_" + n) for n in names}
    x1y_v = x1y_d.rearrange("(n t p) e d -> n p t e d", p=P, t=T)
    base_v, xg_v = (d.rearrange("(n t p) d -> n p t d", p=P, t=T) for d in (base_d, xg_d))
    block = ctx.enter_context(nc.Block())

    def halves(eng, body):
        with eng.Fori(0, n_batches) as b:
            for half in (0, 1):
                body(b, half, b * 2 + half, b * 2 + (half + 1))

    @block.sync
    def _(sp):
        sp.dma_start(wo_raw[:], wo.rearrange("(k p) n -> p k n", p=P)).then_inc(s["w_in"], 16)
        sp.dma_start(gw_raw[:], gate_w).then_inc(s["w_in"], 16)
        with nc.allow_non_contiguous_dma("256 weights, once"):
            sp.dma_start(ln2[:], ln2_w.rearrange("(k p) -> p k", p=P)).then_inc(s["w_in"], 16)

        def body(b, half, n, n1):
            sp.wait_ge(s["in_free"], n1)
            sp.dma_start(oin[half][:].rearrange("p a t e -> p a (t e)"),
                         o_d[b, :, :, half * T:(half + 1) * T, :].rearrange("a p t e -> p a (t e)")).then_inc(s[f"in{half}"], 16)
            sp.dma_start(xy[half][:], x1y_v[n]).then_inc(s[f"in{half}"], 16)
        halves(sp, body)

    @block.gpsimd
    def _(pool):
        g = nc.gpsimd
        g.memset(ident[:], 0.0)
        g.memset(mhalf[:], -0.5).then_inc(s["zero"], 1)
        pool.wait_ge(s["zero"], 1)
        g.affine_select(out=ident[:], in_=ident[:], compare_op=ALU.not_equal, fill=1.0, base=0, pattern=[[-1, P]], channel_multiplier=1).then_inc(s["consts"], 1)

        def body(b, half, n, n1):
            pool.wait_ge(s[f"in{half}"], b * 32 + 32)
            pool.sem_inc(s["pool_turn"], 1)
            g.tensor_copy(orow[half][:].rearrange("p t a e -> p a t e"), oin[half][:]).then_inc(s["orow_done"], 1)
            pool.wait_ge(s["ms_done"], n * T + (T + 1))
            pool.sem_inc(s["pool_turn"], 1)
            g.tensor_scalar(r_s[:], ms[:], EPS, None, ALU.add).then_inc(s["ms_eps"], 1)
            pool.wait_ge(s["ms_eps"], n1)
            g.tensor_tensor(r_s[:], r_s[:], mhalf[:], ALU.pow).then_inc(s["r_done"], 1)
            pool.wait_ge(s["base_done"], n1)
            g.dma_start(base_v[n], base[half][:]).then_inc(s[f"st{half}"], 16)
            pool.wait_ge(s["xg_done"], n1)
            pool.sem_inc(s["pool_turn"], 1)
            g.dma_start(xg_v[n], xg[half][:]).then_inc(s[f"st{half}"], 16)
            pool.wait_ge(s[f"st{half}"], b * 32 + 32)
            pool.sem_inc(s["st_free"], 1)
        halves(pool, body)

    @block.scalar
    def _(act):
        act.wait_ge(s["w_in"], 48)

        def body(b, half, n, n1):
            act.wait_ge(s["oT_ps"], n1)
            nc.scalar.copy(oT[:], p1[:]).then_inc(s["oT_done"], 1)
            act.wait_ge(s["h_done"], n1)
            for t in range(T):
                act.wait_ge(s["ms_done"], n * T + (t + 1))
                nc.scalar.activation(sq[:], h[:, t], ACT.Square, scale=D ** -0.5, accum_out=ms[:, t:t + 1]).then_inc(s["ms_done"], 1)
            act.wait_ge(s["xgT_ps"], n1)
            nc.scalar.mul(xgT[:, 0], p3[:, 0], ln2[:, 0:1])
            nc.scalar.mul(xgT[:, 1], p3[:, 1], ln2[:, 1:2]).then_inc(s["xgT_done"], 1)
            act.wait_ge(s["diff_done"], n1)
            nc.scalar.activation(ed[:], diff[:], ACT.Exp).then_inc(s["ed_done"], 1)
        halves(act, body)

    @block.vector
    def _(dve):
        V_ = nc.vector
        for n, c in (("in_free", 2), ("ms_done", 1), ("st_free", 2)):
            dve.sem_inc(s[n], c)
        dve.wait_ge(s["wT_ps"], 1)
        V_.tensor_copy(woT[:].rearrange("p k m -> p (k m)"), p1[:, 0])
        V_.tensor_copy(gwT[:].rearrange("p k m -> p (k m)"), p1[:, 1, 0:2 * NE]).then_inc(s["wT_done"], 1)

        def body(b, half, n, n1):
            dve.wait_ge(s[f"in{half}"], b * 32 + 32)
            dve.wait_ge(s["h_ps"], n1)
            V_.tensor_tensor(h[:], p2[:].rearrange("p a (e c) -> p (a e) c", e=2), xy[half][:, :, 1], ALU.add).then_inc(s["h_done"], 1)
            dve.wait_ge(s["h_done"], n1)
            dve.wait_ge(s["st_free"], n1)
            V_.tensor_tensor(base[half][:], h[:], xy[half][:, :, 0], ALU.add).then_inc(s["base_done"], 1)
            dve.wait_ge(s["base_done"], n1)
            dve.sem_inc(s["in_free"], 1)
            dve.wait_ge(s["r_done"], n1)
            for t in range(T):
                i = V_.tensor_scalar(xg[half][:, t], h[:, t], r_s[:, t:t + 1], None, ALU.mult)
            i.then_inc(s["xg_done"], 1)
            dve.wait_ge(s["lg_ps"], n1)
            V_.tensor_copy(lg[:], p4[:]).then_inc(s["lg_done"], 1)
            dve.wait_ge(s["lg_done"], n1)
            dve.sem_inc(s["dve_turn"], 1)
            for t in range(T):
                i = V_.max(top[:, t], lg[:, t])
            i.then_inc(s["top_done"], 1)
            dve.wait_ge(s["top_done"], n1)
            V_.tensor_tensor(diff[:], top[:, :, 1], top[:, :, 0], ALU.subtract).then_inc(s["diff_done"], 1)
            for t in range(T):
                i = V_.max_index(tidx[:, t], top[:, t], lg[:, t])
            i.then_inc(s["tidx_done"], 1)
            dve.wait_ge(s["tidx_done"], n1)
            V_.tensor_copy(chosen[:, bass.ds(n * T, T), :], tidx[:, :, 0:2])
            dve.wait_ge(s["ed_done"], n1)
            V_.tensor_scalar(den[:], ed[:], 1.0, None, ALU.add).then_inc(s["den_done"], 1)
            dve.wait_ge(s["den_done"], n1)
            V_.reciprocal(sh[:, :, 0], den[:]).then_inc(s["rec_done"], 1)
            dve.wait_ge(s["rec_done"], n1)
            V_.tensor_tensor(sh[:, :, 1], ed[:], sh[:, :, 0], ALU.mult).then_inc(s["sh_done"], 1)
            dve.wait_ge(s["sh_done"], n1)
            V_.tensor_copy(share[:, bass.ds(n * T, T), :], sh[:]).then_inc(s["copied"], 1)
        halves(dve, body)

    @block.tensor
    def _(pe):
        mm, tr = nc.tensor.matmul, nc.tensor.transpose
        pe.wait_ge(s["w_in"], 48)
        pe.wait_ge(s["consts"], 1)
        for k in range(2):
            for m in range(2):
                tr(p1[:, 0, k * D + m * P:k * D + (m + 1) * P], wo_raw[:, m, k * P:(k + 1) * P], ident[:])
            i = tr(p1[:, 1, k * NE:(k + 1) * NE], gw_raw[:, k * P:(k + 1) * P], ident[0:NE, 0:NE])
        i.then_inc(s["wT_ps"], 1)
        pe.wait_ge(s["wT_done"], 1)

        def body(b, half, n, n1):
            pe.wait_ge(s["orow_done"], n1)
            for t in range(T):
                for k in range(2):
                    i = tr(p1[:, k, t * P:(t + 1) * P], orow[half][:, t, 4 * k:4 * k + 4, :].rearrange("p a e -> p (a e)"), ident[:])
            i.then_inc(s["oT_ps"], 1)
            pe.wait_ge(s["oT_done"], n1)
            for t in range(T):
                for k in range(2):
                    i = mm(p2[:, t // 2, (t % 2) * D:(t % 2 + 1) * D], oT[:, k, t * P:(t + 1) * P], woT[:, k, :], start=(k == 0), stop=(k == 1))
            i.then_inc(s["h_ps"], 1)
            pe.wait_ge(s["xg_done"], n1)
            for t in range(T):
                for k in range(2):
                    i = tr(p3[:, k, t * P:(t + 1) * P], xg[half][:, t, k * P:(k + 1) * P], ident[:])
            i.then_inc(s["xgT_ps"], 1)
            pe.wait_ge(s["xgT_done"], n1)
            for t in range(T):
                for k in range(2):
                    i = mm(p4[:, t, :], xgT[:, k, t * P:(t + 1) * P], gwT[:, k, :], start=(k == 0), stop=(k == 1))
            i.then_inc(s["lg_ps"], 1)
        halves(pe, body)


def route(nc, ctx, chosen, token_of, code_of, expert_of, NT, TILES):
    P, NE = 128, 8
    C2 = 2 * NT
    f32, i32 = mybir.dt.float32, mybir.dt.int32
    ALU, AX = mybir.AluOpType, mybir.AxisListType

    def sb(name, shape, dt=f32):
        return ctx.enter_context(nc.sbuf_tensor("r_" + name, shape, dt))

    ones, before = sb("ones", [P, P]), sb("before", [P, P])
    WIDE = max(P, TILES)
    iota_i, iota = sb("iota_i", [P, WIDE], i32), sb("iota", [P, WIDE])
    lane_i, lane = sb("lane_i", [P, 1], i32), sb("lane", [P, 1])
    val_i, val = sb("val_i", [P, C2], i32), sb("val", [P, C2])
    E = sb("E", [P, C2, NE])
    tot, cum = sb("tot", [P, NE, C2]), sb("cum", [P, NE, C2])
    full, full_i, tiles, end = sb("full", [P, NE]), sb("full_i", [P, NE], i32), sb("tiles", [P, NE]), sb("end", [P, NE])
    begin = sb("begin", [P, NE])
    where = sb("where", [P, C2, NE])
    slot, slot_i = sb("slot", [P, C2]), sb("slot_i", [P, C2], i32)
    lo_i, hi_i, lo, hi = sb("lo_i", [P, C2], i32), sb("hi_i", [P, C2], i32), sb("lo", [P, C2]), sb("hi", [P, C2])
    cmp, ex = sb("cmp", [P, TILES, NE]), sb("ex", [P, TILES])
    is_lo = [sb(f"is_lo{r}", [P, P]) for r in range(4)]
    is_hi = [sb(f"is_hi{r}", [P, TILES]) for r in range(4)]
    inv, invm, empty = sb("inv", [P, TILES]), sb("invm", [P, TILES]), sb("empty", [P, TILES])
    inv_i = sb("inv_i", [P, TILES], i32)
    W = C2 * NE // 2
    p_before = ctx.enter_context(nc.psum_tensor("r_p_before", [P, 2, 512], f32))
    p_total = ctx.enter_context(nc.psum_tensor("r_p_total", [P, 2, 512], f32))
    p_inv = ctx.enter_context(nc.psum_tensor("r_p_inv", [P, TILES], f32))
    s = {n: stage_semaphore(nc, ctx, "r_" + n) for n in ("pool0", "pool", "dve", "E_done", "ps", "hot", "inv_ps")}
    block = ctx.enter_context(nc.Block())

    @block.gpsimd
    def _(pool):
        g = nc.gpsimd
        g.memset(before[:], 1.0)
        g.iota(iota_i[:], [[1, WIDE]], base=0, channel_multiplier=0)
        g.iota(lane_i[:], [[1, 1]], base=0, channel_multiplier=1)
        g.iota(val_i[:], [[2 * P, NT], [1, 2]], base=1, channel_multiplier=2).then_inc(s["pool0"], 1)
        pool.wait_ge(s["pool0"], 1)
        g.affine_select(out=before[:], in_=before[:], compare_op=ALU.is_gt, fill=0.0, base=0, pattern=[[1, P]], channel_multiplier=-1).then_inc(s["pool"], 1)

    @block.vector
    def _(dve):
        V_ = nc.vector
        count = [0]

        def then(ins):
            count[0] += 1
            ins.then_inc(s["dve"], 1)
            dve.wait_ge(s["dve"], count[0])

        dve.wait_ge(s["pool"], 1)
        V_.memset(ones[:], 1.0)
        V_.tensor_copy(iota[:], iota_i[:])
        V_.tensor_copy(lane[:], lane_i[:])
        then(V_.tensor_copy(val[:], val_i[:]))
        V_.tensor_tensor(E[:], chosen[:].rearrange("p j (k o) -> p (j k) o", o=1).to_broadcast([P, C2, NE]),
                         iota[:, 0:NE].rearrange("p (o e) -> p o e", o=1).to_broadcast([P, C2, NE]), ALU.is_equal).then_inc(s["E_done"], 1)
        dve.wait_ge(s["ps"], 1)
        for k in range(2):
            i = V_.tensor_copy(tot[:, :, k * NT:(k + 1) * NT], p_total[:, k, 0:W].rearrange("p (c e) -> p e c", e=NE))
        then(i)
        for e in range(NE):
            i = V_.tensor_tensor_scan(cum[:, e, :], ones[:, 0:C2], tot[:, e, :], 0.0, ALU.mult, ALU.add)
        then(i)
        then(V_.tensor_scalar(full[:], cum[:, :, C2 - 1], float(P - 1), None, ALU.add))
        then(V_.tensor_copy(full_i[:], full[:]))
        then(V_.tensor_scalar(full_i[:], full_i[:], 7, None, ALU.arith_shift_right))
        then(V_.tensor_copy(tiles[:], full_i[:]))
        then(V_.tensor_tensor_scan(end[:], ones[:, 0:NE], tiles[:], 0.0, ALU.mult, ALU.add))
        then(V_.tensor_tensor(begin[:], end[:], tiles[:], ALU.subtract))
        then(V_.tensor_scalar(begin[:], begin[:], float(P), None, ALU.mult))
        then(V_.tensor_tensor(cum[:], cum[:], tot[:], ALU.subtract))
        then(V_.tensor_tensor(cum[:], cum[:], begin[:].rearrange("p (e o) -> p e o", o=1).to_broadcast([P, NE, C2]), ALU.add))
        for k in range(2):
            i = V_.tensor_tensor(where[:, k * NT:(k + 1) * NT, :], p_before[:, k, 0:W].rearrange("p (c e) -> p c e", e=NE),
                                 cum[:, :, k * NT:(k + 1) * NT].rearrange("p e c -> p c e"), ALU.add)
        then(i)
        then(V_.tensor_tensor(where[:], where[:], E[:], ALU.mult))
        then(V_.reduce_sum(slot[:], where[:], AX.X))
        then(V_.tensor_copy(slot_i[:], slot[:]))
        V_.tensor_scalar(hi_i[:], slot_i[:], 7, None, ALU.arith_shift_right)
        then(V_.tensor_scalar(lo_i[:], slot_i[:], P - 1, None, ALU.bitwise_and))
        V_.tensor_copy(hi[:], hi_i[:])
        then(V_.tensor_copy(lo[:], lo_i[:]))
        with dve.Fori(0, C2 // 4) as i4:
            for r in range(4):
                c = i4 * 4 + r
                dve.wait_ge(s["inv_ps"], c + 1)
                V_.tensor_scalar(is_lo[r][:], iota[:, 0:P], lo[:, bass.ds(c, 1)], None, ALU.is_equal)
                V_.tensor_scalar(is_hi[r][:], iota[:, 0:TILES], hi[:, bass.ds(c, 1)], val[:, bass.ds(c, 1)], ALU.is_equal, ALU.mult).then_inc(s["hot"], 1)
        V_.tensor_tensor(cmp[:], iota[:, 0:TILES].rearrange("p (m o) -> p m o", o=1).to_broadcast([P, TILES, NE]),
                         end[:].rearrange("p (o e) -> p o e", o=1).to_broadcast([P, TILES, NE]), ALU.is_ge).then_inc(s["dve"], 1)
        count[0] += 1
        dve.wait_ge(s["dve"], count[0])
        then(V_.reduce_sum(ex[:], cmp[:], AX.X))
        then(V_.tensor_scalar(ex[:], ex[:], float(NE - 1), None, ALU.min))
        V_.memset(expert_of[:, 0:1], 0)
        V_.tensor_copy(expert_of[:, 1:TILES + 1], ex[0:1, :])
        dve.wait_ge(s["inv_ps"], C2 + 4)
        then(V_.tensor_copy(inv[:], p_inv[:]))
        V_.tensor_scalar(empty[:], inv[:], 0.0, float(2 * NT * P + 1), ALU.is_equal, ALU.mult)
        then(V_.tensor_scalar(invm[:], inv[:], -1.0, None, ALU.add))
        then(V_.tensor_tensor(inv[:], invm[:], empty[:], ALU.add))
        then(V_.tensor_scalar(empty[:], empty[:], 1.0 / (2 * NT * P + 1), lane[:, 0:1], ALU.mult, ALU.mult))
        then(V_.tensor_tensor(inv[:], inv[:], empty[:], ALU.add))
        V_.tensor_copy(code_of[:], inv[:])
        then(V_.tensor_scalar(invm[:], invm[:], 0.0, None, ALU.max))
        then(V_.tensor_copy(inv_i[:], invm[:]))
        then(V_.tensor_scalar(token_of[:], inv_i[:], 1, None, ALU.arith_shift_right))

    @block.tensor
    def _(pe):
        mm = nc.tensor.matmul
        pe.sem_inc(s["inv_ps"], 4)
        pe.wait_ge(s["E_done"], 1)
        for k in range(2):
            rhs = E[:, k * NT:(k + 1) * NT, :].rearrange("p c e -> p (c e)")
            mm(p_before[:, k, 0:W], before[:], rhs, start=True, stop=True)
            i = mm(p_total[:, k, 0:W], ones[:], rhs, start=True, stop=True)
        i.then_inc(s["ps"], 1)
        def column(c, r, start, stop):
            pe.wait_ge(s["hot"], c + 1)
            mm(p_inv[:], is_lo[r][:], is_hi[r][:], start=start, stop=stop, skip_group_check=True).then_inc(s["inv_ps"], 1)
        for r in range(4):
            column(r, r, r == 0, False)
        with pe.Fori(1, C2 // 4) as i4:
            for r in range(4):
                column(i4 * 4 + r, r, False, False)


def experts(nc, ctx, xg_d, w1, w3, w2, ln2_w, token_of, code_of, expert_of, ys_d, TILES):
    P, D, I, NE = 128, 256, 512, 8
    f32, i32 = mybir.dt.float32, mybir.dt.int32
    ALU, ACT, AX = mybir.AluOpType, mybir.ActivationFunctionType, mybir.AxisListType

    def sb(name, shape, dt=f32):
        return ctx.enter_context(nc.sbuf_tensor("d_" + name, shape, dt))

    w1T, w3T = sb("w1T", [P, NE, 2, I]), sb("w3T", [P, NE, 2, I])
    w2T = sb("w2T", [P, NE, 4, D])
    raw = [sb(f"raw{r}", [P, 3, 1024]) for r in range(2)]
    ln2, ident = sb("ln2", [P, 2]), sb("ident", [P, P])
    tok, code = [sb(f"tok{r}", [P, 1], i32) for r in range(4)], [sb(f"code{r}", [P, 1], i32) for r in range(2)]
    xs = [sb(f"xs{r}", [P, D]) for r in range(4)]
    xT = [sb(f"xT{r}", [P, 2, P]) for r in range(2)]
    act_s, h = [sb(f"act{r}", [P, I]) for r in range(2)], [sb(f"h{r}", [P, I]) for r in range(2)]
    hT = [sb(f"hT{r}", [P, 4, P]) for r in range(2)]
    y = [sb(f"y{r}", [P, D]) for r in range(2)]
    p_x = ctx.enter_context(nc.psum_tensor("d_p_x", [P, 4, P], f32))
    p_up = [ctx.enter_context(nc.psum_tensor(f"d_p_up{r}", [P, 2, I], f32)) for r in range(2)]
    p_h = ctx.enter_context(nc.psum_tensor("d_p_h", [P, 4, P], f32))
    p_y = ctx.enter_context(nc.psum_tensor("d_p_y", [P, 512], f32))
    names = ("raw_in0", "raw_in1", "zero", "id", "wT_ps", "wT_even", "wT_odd", "tok_done", "turn", *(f"x_in{r}" for r in range(4)), "xT_ps", "xT_done",
             "ln_in", "up_ps", "act_done", "h_done", "hT_ps", "hT_done", "y_ps", "y_done", "code_done", "y_out", "y_free", "start")
    s = {n: stage_semaphore(nc, ctx, "d_" + n) for n in names}
    block = ctx.enter_context(nc.Block())

    @block.sync
    def _(sp):
        with nc.allow_non_contiguous_dma("256 weights, once"):
            sp.dma_start(ln2[:], ln2_w.rearrange("(k p) -> p k", p=P)).then_inc(s["ln_in"], 16)
        for e in range(NE):
            if e >= 2:
                sp.wait_ge(s["wT_ps"], 6 * (e - 1))
            r = e % 2
            sp.dma_start(raw[r][:, 0].rearrange("p (a d) -> p a d", a=4), w1[e].rearrange("(a p) d -> p a d", p=P)).then_inc(s[f"raw_in{r}"], 16)
            sp.dma_start(raw[r][:, 1].rearrange("p (a d) -> p a d", a=4), w3[e].rearrange("(a p) d -> p a d", p=P)).then_inc(s[f"raw_in{r}"], 16)
            sp.dma_start(raw[r][:, 2].rearrange("p (a i) -> p a i", a=2), w2[e].rearrange("(a p) i -> p a i", p=P)).then_inc(s[f"raw_in{r}"], 16)

    def banks(e, j):
        n = e * 6 + j
        return p_up[n // 2 % 2][:, n % 2, :]

    @block.gpsimd
    def _(pool):
        g = nc.gpsimd
        g.memset(ident[:], 0.0).then_inc(s["zero"], 1)
        pool.wait_ge(s["zero"], 1)
        g.affine_select(out=ident[:], in_=ident[:], compare_op=ALU.not_equal, fill=1.0, base=0, pattern=[[-1, P]], channel_multiplier=1).then_inc(s["id"], 1)

        def gather(m, r):
            g.tensor_copy(tok[r][:], token_of[:, bass.ds(m, 1)]).then_inc(s["tok_done"], 1)
            pool.wait_ge(s["tok_done"], m + 1)
            pool.sem_inc(s["turn"], 1)
            g.indirect_dma_start(xs[r][:], None, xg_d, bass.IndirectOffsetOnAxis(ap=tok[r][:, 0:1], axis=0)).then_inc(s[f"x_in{r}"], 16)

        def scatter(m, r):
            g.tensor_copy(code[r][:], code_of[:, bass.ds(m, 1)]).then_inc(s["code_done"], 1)
            pool.wait_ge(s["code_done"], m + 1)
            pool.wait_ge(s["y_done"], m + 3)
            pool.sem_inc(s["turn"], 1)
            g.indirect_dma_start(ys_d, bass.IndirectOffsetOnAxis(ap=code[r][:, 0:1], axis=0), y[r][:], None).then_inc(s["y_out"], 16)
            pool.wait_ge(s["y_out"], m * 16 + 16)
            pool.sem_inc(s["y_free"], 1)

        for m in range(3):
            gather(m, m)
        with pool.Fori(0, TILES // 4 - 1) as i:
            for r in range(4):
                m = i * 4 + r
                pool.wait_ge(s["xT_ps"], m + 1)
                gather(m + 3, (r + 3) % 4)
                scatter(m, r % 2)
        for r in range(4):
            m = TILES - 4 + r
            if r == 0:
                pool.wait_ge(s["xT_ps"], m + 1)
                gather(m + 3, 3)
            scatter(m, r % 2)

    @block.scalar
    def _(act):
        act.wait_ge(s["ln_in"], 16)
        for e in range(NE):
            for j in (1, 3, 5):
                act.wait_ge(s["wT_ps"], e * 6 + j + 1)
                dst = (w1T[:, e, 1], w3T[:, e, 1], w2T[:, e, 2:4])[j // 2]
                nc.scalar.copy(dst.rearrange("p a n -> p (a n)") if j == 5 else dst, banks(e, j)).then_inc(s["wT_odd"], 1)

        def first(m, r):
            act.wait_ge(s["xT_ps"], m + 2)
            nc.scalar.mul(xT[r][:, 0], p_x[:, 0], ln2[:, 0:1])
            nc.scalar.mul(xT[r][:, 1], p_x[:, 1], ln2[:, 1:2]).then_inc(s["xT_done"], 1)
            act.wait_ge(s["up_ps"], 2 * m + 1)
            nc.scalar.activation(act_s[r][:], p_up[r][:, 0], ACT.Silu).then_inc(s["act_done"], 1)

        with act.Fori(0, TILES // 2) as i:
            for r in (0, 1):
                m = i * 2 + r
                first(m, r)
                act.wait_ge(s["hT_ps"], m + 1)
                nc.scalar.copy(hT[1 - r][:], p_h[:]).then_inc(s["hT_done"], 1)
        act.wait_ge(s["hT_ps"], TILES + 1)
        nc.scalar.copy(hT[1][:], p_h[:]).then_inc(s["hT_done"], 1)

    @block.vector
    def _(dve):
        V_ = nc.vector
        for r in (0, 1):
            V_.memset(h[r][:], 0.0)
        V_.memset(hT[1][:], 0.0).then_inc(s["start"], 1)
        dve.sem_inc(s["xT_ps"], 1)
        dve.sem_inc(s["y_free"], 3)
        dve.sem_inc(s["y_done"], 1)
        for e in range(NE):
            for j in (0, 2, 4):
                dve.wait_ge(s["wT_ps"], e * 6 + j + 1)
                dst = (w1T[:, e, 0], w3T[:, e, 0], w2T[:, e, 0:2])[j // 2]
                V_.tensor_copy(dst.rearrange("p a n -> p (a n)") if j == 4 else dst, banks(e, j)).then_inc(s["wT_even"], 1)

        with dve.Fori(0, TILES // 2) as i:
            for r in (0, 1):
                m = i * 2 + r
                dve.wait_ge(s["act_done"], m + 1)
                dve.wait_ge(s["up_ps"], 2 * m + 2)
                V_.tensor_tensor(h[r][:], act_s[r][:], p_up[r][:, 1], ALU.mult).then_inc(s["h_done"], 1)
                dve.wait_ge(s["y_ps"], m + 1)
                dve.wait_ge(s["y_free"], m + 1)
                V_.tensor_copy(y[1 - r][:], p_y[:, 0:D]).then_inc(s["y_done"], 1)
        dve.wait_ge(s["y_ps"], TILES + 1)
        dve.wait_ge(s["y_free"], TILES + 1)
        V_.tensor_copy(y[1][:], p_y[:, 0:D]).then_inc(s["y_done"], 1)

    @block.tensor
    def _(pe):
        mm, tr = nc.tensor.matmul, nc.tensor.transpose
        pe.wait_ge(s["id"], 1)
        pe.wait_ge(s["start"], 1)
        for e in range(NE):
            pe.wait_ge(s[f"raw_in{e % 2}"], 48 * (e // 2) + 48)
            for j in range(6):
                n = e * 6 + j
                if n >= 4:
                    pe.wait_ge(s[("wT_even", "wT_odd")[n % 2]], (n - 4) // 2 + 1)
                for i in range(4):
                    if j < 4:
                        src = raw[e % 2][:, j // 2].rearrange("p (a d) -> p a d", a=4)[:, i, (j % 2) * P:(j % 2 + 1) * P]
                    else:
                        src = raw[e % 2][:, 2].rearrange("p (a i) -> p a i", a=2)[:, i % 2, (2 * (j - 4) + i // 2) * P:(2 * (j - 4) + i // 2 + 1) * P]
                    last = tr(banks(e, j)[:, i * P:(i + 1) * P], src, ident[:])
                last.then_inc(s["wT_ps"], 1)
        pe.wait_ge(s["wT_even"], 3 * NE)
        pe.wait_ge(s["wT_odd"], 3 * NE)
        def last_product(m, r):
            e = pe.value_load(expert_of[0:1, bass.ds(m, 1)], min_val=0, max_val=NE - 1)
            for k in range(4):
                last = tr(p_h[:, k, :], h[r][:, k * P:(k + 1) * P], ident[:])
            last.then_inc(s["hT_ps"], 1)
            pe.wait_ge(s["hT_done"], m + 1)
            pe.wait_ge(s["y_done"], m + 1)
            for k in range(4):
                last = mm(p_y[:, 0:D], hT[r][:, k], w2T[:, bass.ds(e, 1), k, :].rearrange("p o n -> p (o n)"), start=(k == 0), stop=(k == 3))
            last.then_inc(s["y_ps"], 1)

        with pe.Fori(0, TILES // 4) as i:
            for q in range(4):
                m = i * 4 + q
                r = q % 2
                pe.wait_ge(s[f"x_in{q}"], i * 16 + 16)
                for k in range(2):
                    last = tr(p_x[:, k, :], xs[q][:, k * P:(k + 1) * P], ident[:])
                last.then_inc(s["xT_ps"], 1)
                e = pe.value_load(expert_of[0:1, bass.ds(m + 1, 1)], min_val=0, max_val=NE - 1)
                pe.wait_ge(s["xT_done"], m + 1)
                for u, w in ((0, w1T), (1, w3T)):
                    for k in range(2):
                        last = mm(p_up[r][:, u], xT[r][:, k], w[:, bass.ds(e, 1), k, :].rearrange("p o n -> p (o n)"), start=(k == 0), stop=(k == 1))
                    last.then_inc(s["up_ps"], 1)
                last_product(m, 1 - r)
                pe.wait_ge(s["h_done"], m + 1)
        last_product(TILES, 1)


def combine(nc, ctx, base_d, ys_d, share, out, NT):
    P, D, T = 128, 256, 4
    RING = 4
    f32 = mybir.dt.float32
    ALU = mybir.AluOpType
    base = [ctx.enter_context(nc.sbuf_tensor(f"e_base{r}", [P, T, D], f32)) for r in range(RING)]
    ys = [ctx.enter_context(nc.sbuf_tensor(f"e_ys{r}", [P, T, 2, D], f32)) for r in range(RING)]
    sh = [ctx.enter_context(nc.sbuf_tensor(f"e_sh{r}", [P, T, 2], f32)) for r in range(RING)]
    names = [f"in{r}" for r in range(RING)] + [f"out{r}" for r in range(RING)] + ["sh_done", "first", "sum"]
    s = {n: stage_semaphore(nc, ctx, "e_" + n) for n in names}
    base_v, out_v = (d.rearrange("(n t p) d -> n p t d", p=P, t=T) for d in (base_d, out))
    ys_v = ys_d[0:2 * NT * P, :].rearrange("(n t p k) d -> n p t k d", p=P, t=T, k=2)
    N = NT // T
    block = ctx.enter_context(nc.Block())

    @block.sync
    def _(sp):
        def load(n, r):
            sp.dma_start(base[r][:], base_v[n]).then_inc(s[f"in{r}"], 16)
            sp.dma_start(ys[r][:], ys_v[n]).then_inc(s[f"in{r}"], 16)
        for r in range(min(RING, N)):
            load(r, r)
        if N > RING:
            with sp.Fori(1, N // RING) as i:
                for r in range(RING):
                    sp.wait_ge(s[f"out{r}"], i * 16)
                    load(i * RING + r, r)

    @block.vector
    def _(dve):
        V_ = nc.vector
        with dve.Fori(0, (N + RING - 1) // RING) as i:
            for r in range(min(RING, N)):
                n = i * RING + r
                V_.tensor_copy(sh[r][:], share[:, bass.ds(n * T, T), :]).then_inc(s["sh_done"], 1)
                dve.wait_ge(s["sh_done"], n + 1)
                dve.wait_ge(s[f"in{r}"], i * 32 + 32)
                for k in range(2):
                    if k:
                        dve.wait_ge(s["first"], n + 1)
                    for t in range(T):
                        last = V_.scalar_tensor_tensor(base[r][:, t], ys[r][:, t, k], sh[r][:, t, k:k + 1], base[r][:, t], ALU.mult, ALU.add)
                    last.then_inc(s["first" if k == 0 else "sum"], 1)

    @block.scalar
    def _(act):
        with act.Fori(0, (N + RING - 1) // RING) as i:
            for r in range(min(RING, N)):
                n = i * RING + r
                act.wait_ge(s["sum"], n + 1)
                act.dma_start(out_v[n], base[r][:]).then_inc(s[f"out{r}"], 16)
        for r in range(min(RING, N)):
            act.wait_ge(s[f"out{r}"], 16 * ((N + RING - 1) // RING))


def layer_kernel(nc, x, Wq, Wk, Wv, Wg, Wgk1, Wgk2, bgk2, Wout, rms_w, ln1_w, ln2_w, wq, wk, wv, wo, gate_w, w1, w2, w3, out):
    B, N, D = x.shape
    P = 128
    NT = B * N // P
    NE = gate_w.shape[0]
    TILES = 2 * NT + NE
    f32, i32 = mybir.dt.float32, mybir.dt.int32
    flat = x.rearrange("b n d -> (b n) d")
    x1y_d = nc.dram_tensor("x1y_d", (B * N, 2, D), f32).ap()
    qk_d = nc.dram_tensor("qk_d", (2, 2, B * D, N), f32).ap()
    v_d = nc.dram_tensor("v_d", (B, 8, P, N // P, 64), f32).ap()
    o_d = nc.dram_tensor("o_d", (B, 8, P, N // P, 32), f32).ap()
    base_d = nc.dram_tensor("base_d", (B * N, D), f32).ap()
    xg_d = nc.dram_tensor("xg_d", (B * N, D), f32).ap()
    ys_d = nc.dram_tensor("ys_d", (2 * B * N + P, D), f32).ap()
    with ExitStack() as ctx:
        def sb(name, shape, dt=f32):
            return ctx.enter_context(nc.sbuf_tensor(name, shape, dt))
        chosen, share = sb("chosen", [P, NT, 2]), sb("share", [P, NT, 2])
        token_of, code_of = sb("token_of", [P, TILES], i32), sb("code_of", [P, TILES], i32)
        expert_of = sb("expert_of", [1, TILES + 1], i32)
        with Stage(nc) as stage:
            gla_and_projections(nc, stage, flat, Wq, Wk, Wv, Wg, Wgk1, Wgk2, bgk2, Wout, rms_w,
                                ln1_w, wq, wk, wv, x1y_d, qk_d, v_d, B)
        with Stage(nc) as stage:
            softmax_attention(nc, stage, qk_d, v_d, o_d, B)
        with Stage(nc) as stage:
            output_projection_and_gate(nc, stage, o_d, x1y_d, wo, gate_w, ln2_w, base_d, xg_d, chosen, share, B)
        with Stage(nc) as stage:
            route(nc, stage, chosen, token_of, code_of, expert_of, NT, TILES)
        with Stage(nc) as stage:
            experts(nc, stage, xg_d, w1, w3, w2, ln2_w, token_of, code_of, expert_of, ys_d, TILES)
        with Stage(nc) as stage:
            combine(nc, stage, base_d, ys_d, share, out.rearrange("b n d -> (b n) d"), NT)


_INS = ["L0_attn_x", "L0_attn_Wq", "L0_attn_Wk", "L0_attn_Wv", "L0_attn_Wg", "L0_attn_Wgk1", "L0_attn_Wgk2",
        "L0_attn_bgk2", "L0_attn_Wout", "L0_attn_rms_w", "L0_ffn_ln1_w", "L0_ffn_ln2_w", "L0_ffn_wq", "L0_ffn_wk",
        "L0_ffn_wv", "L0_ffn_wo", "L0_ffn_gate_w", "L0_ffn_w1", "L0_ffn_w2", "L0_ffn_w3"]
_OUTS = [((8, 1024, 256), "float32")]


def kernel(**inputs):
    import numpy as _np
    import concourse.bacc as _bacc
    from concourse import mybir as _mybir
    from concourse.bass_utils import run_bass_kernel_spmd as _run

    nc = _bacc.Bacc("TRN2", target_bir_lowering=False, num_devices=1)
    arrays, args = {}, []
    for name in _INS:
        a = _np.ascontiguousarray(inputs[name])
        arrays[f"in_{name}_dram"] = a
        args.append(nc.dram_tensor(f"in_{name}_dram", a.shape, _mybir.dt.from_np(a.dtype), kind="ExternalInput").ap())
    for i, (shape, dtype) in enumerate(_OUTS):
        dt = _mybir.dt.from_np(_np.dtype(dtype))
        args.append(nc.dram_tensor(f"out_{i}_dram", shape, dt, kind="ExternalOutput").ap())
    layer_kernel(nc, *args)
    r = _run(nc, [arrays], core_ids=[0])
    got = tuple(r.results[0][f"out_{i}_dram"] for i in range(len(_OUTS)))
    return got[0]
```

```python
from contextlib import ExitStack

import concourse.bass as bass
from concourse import mybir


def stage_semaphore(nc, stage, name):
    sem = nc.alloc_semaphore(name)
    stage.semaphores.append(sem)
    return sem


class Stage(ExitStack):

    def __init__(self, nc):
        super().__init__()
        self.nc, self.semaphores = nc, []

    def __exit__(self, *error):
        ended = super().__exit__(*error)
        self.nc.all_engine_barrier()
        self.nc.clear_and_free_semaphores(self.semaphores)
        self.nc.all_engine_barrier()
        return ended


def gla_and_projections(nc, ctx, x, Wq, Wk, Wv, Wg, Wgk1, Wgk2, bgk2, Wout, rms_w,
                        ln1_w, wq, wk, wv, x1y_d, qk_d, v_d, n_batches=8):
    P, D, T = 128, 256, 4
    HT = P * T
    C = 32
    NC = HT // C
    H, DK, DV = 4, 32, 64
    EPS = 1e-5
    f32, f32r = mybir.dt.float32, mybir.dt.float32r
    ALU, ACT, AX = mybir.AluOpType, mybir.ActivationFunctionType, mybir.AxisListType

    def sb(name, shape, dt=f32):
        return ctx.enter_context(nc.sbuf_tensor("a_" + name, shape, dt))

    W_f = [sb(f"W_f{part}", [P, 2, 896], f32r) for part in range(2)]
    COLUMNS = {"z": slice(0, 128), "q": slice(128, 256), "k": slice(256, 384), "vg": slice(384, 896)}
    Wgk1_s, Wgk2_s, bgk_s = sb("Wgk1_s", [P, 2, 16]), sb("Wgk2_s", [16, 128]), sb("bgk_s", [P, 1])
    Wgk1T = sb("Wgk1T", [16, D])
    Wout_s = sb("Wout_s", [P, 2, D])
    rmsw_s, ln1w_s = sb("rmsw_s", [P, 1]), sb("ln1w_s", [P, 2])
    wT = [sb(f"wT{part}", [P, 3, 2, D], f32r) for part in range(2)]
    ident, ones = sb("ident", [P, P]), sb("ones", [P, P])
    mask = sb("mask", [P, HT])
    maski = sb("maski", [P, HT], mybir.dt.int32)
    keep = sb("keep", [P, HT])
    xin = sb("xin", [P, 2, T, D])
    st6, mv = sb("st6", [P, T, 6]), sb("mv", [P, T, 2])
    rstd = sb("rstd", [P, T])
    xn = sb("xn", [P, T, D])
    xT, xTl = sb("xT", [P, 2, HT], f32r), sb("xTl", [P, 2, HT], f32r)
    q_s, k_s = sb("q_s", [P, HT]), sb("k_s", [P, HT])
    za, zm, cum = sb("za", [P, HT]), sb("zm", [P, HT]), sb("cum", [P, HT])
    rel, tail = sb("rel", [P, HT]), sb("tail", [P, HT])
    e_in, e_out, e_cum, e_tail = (sb(f"e_{n}", [P, HT]) for n in ("in", "out", "cum", "tail"))
    decay = sb("decay", [P, NC])
    kt, qh, kh = (sb(n, [P, HT]) for n in ("kt", "qh", "kh"))
    qz = sb("qz", [P, T, H, P])
    khat = sb("khat", [P, T, P])
    V, G = sb("V", [P, T, D]), [sb(f"G{r}", [P, T, D]) for r in range(2)]
    AT = sb("AT", [P, T, H, P])
    S = sb("S", [P, NC + 1, DV])
    Sbd = sb("Sbd", [P, NC, D])
    staged = Sbd[:].rearrange("p c d -> p (c d)")
    front_raw = staged[:, 0:2 * 896].rearrange("p (k n) -> p k n", k=2)
    w_raw = staged[:, 2 * 896:2 * 896 + 6 * D].rearrange("p (j k d) -> p j k d", j=3, k=2)
    o_s, o2 = sb("o_s", [P, T, D]), sb("o2", [P, T, D])
    ss, rs = sb("ss", [P, T * H]), sb("rs", [P, T * H])
    ogT = sb("ogT", [P, 2, HT])
    x1y = sb("x1y", [P, T, 2, D])
    st6b, mvb = sb("st6b", [P, T, 6]), sb("mvb", [P, T, 2])
    roots = sb("roots", [P, 2, T])
    xr = sb("xr", [P, T, D])
    xrT, xrTl = sb("xrT", [P, 2, HT], f32r), sb("xrTl", [P, 2, HT], f32r)
    hi, lo = sb("hi", [P, 4, HT], f32r), sb("lo", [P, 4, HT], f32r)
    v_s = sb("v_s", [P, 8, T, 64])
    mhalf = sb("mhalf", [P, T * H])
    p_f = ctx.enter_context(nc.psum_tensor("a_p_f", [P, 4, 512], f32))
    p_g = ctx.enter_context(nc.psum_tensor("a_p_g", [P, 4, 512], f32))

    names = ("w_in", "consts0", "consts", "filled", "wT_ps", "wT_done", "x_in0", "x_in1", "st_done", "mv_done", "rstd_done",
             "xn_done", "xT_ps", "xT_done", "xTl_done", "xrTl_done", "raw_done", "front_hi", "wT_hi", "front_done", "gk_ps", "gk1T_done", "z_ps", "za_done", "e_z", "l_z", "zm_done", "q_ps", "k_ps", "q_done", "k_done",
             "g0", "g1", "cum_done", "tail_done", "exps_rel", "exps_tail", "exps", "qtkt", "hats", "khT_ps", "khat_done", "vg_ps",
             "vg_taken", "AT_ps", "AT_done", "inc_ps", "S_step", "S_carry", "Sbd_done", "o_ps",
             "o_s_done", "o2_done", "ss_done", "rs_done", "on_done", "og_done", "ogT_ps", "ogT_done", "wout_ps",
             "x1_done", "stb_done", "mvb_done", "roots_done", "y_done", "xr_done", "xrT_ps", "xrT_done",
             "qk2_ps", "hi_done", "lo_done", "v2_ps", "v_done", "rstd_eps", "rs_eps", "roots_eps", "stored", "store_free", "zero",
             "dve_turn", "pe_turn", "pool_turn")
    s = {n: stage_semaphore(nc, ctx, "a_" + n) for n in names}

    x_v = x.rearrange("(n t p) d -> n p t d", p=P, t=T)
    x1y_v = x1y_d.rearrange("(n t p) e d -> n p t e d", p=P, t=T)
    qk_v = qk_d.rearrange("w c (b m p) t -> w c b p m t", m=2, p=P)

    VG_BANK = (3, 2, 0, 1)
    block = ctx.enter_context(nc.Block())

    def rounds(eng, body):
        if n_batches > 1:
            with eng.Fori(0, n_batches - 1) as b:
                body(b * 2, 0, b, b, True, True)
                body(b * 2 + 1, 1, b, b + 1, True, True)
        b = n_batches - 1
        body(b * 2, 0, b, b, True, False)
        body(b * 2 + 1, 1, b, b + 1, False, False)

    @block.sync
    def _(sp):
        two = lambda w: w.rearrange("(k p) n -> p k n", p=P)
        loads = [(Wgk1_s[:], two(Wgk1)), (Wgk2_s[:], Wgk2), (bgk_s[:], bgk2.rearrange("(p o) -> p o", o=1)),
                 (front_raw[:, :, 128:256], two(Wq)), (front_raw[:, :, 256:384], two(Wk)),
                 (front_raw[:, :, 384:640], two(Wv)), (front_raw[:, :, 640:896], two(Wg)),
                 (Wout_s[:], two(Wout)), (rmsw_s[0:64, :], rms_w.rearrange("(p o) -> p o", o=1)),
                 (rmsw_s[64:128, :], rms_w.rearrange("(p o) -> p o", o=1)),
                 (w_raw[:, 0], two(wq)), (w_raw[:, 1], two(wk)), (w_raw[:, 2], two(wv))]
        for half in (0, 1):
            sp.dma_start(xin[:, half], x_v[half]).then_inc(s[f"x_in{half}"], 16)
        for dst, src in loads:
            sp.dma_start(dst, src).then_inc(s["w_in"], 16)
        with nc.allow_non_contiguous_dma("256 weights, once"):
            sp.dma_start(ln1w_s[:], ln1_w.rearrange("(k p) -> p k", p=P)).then_inc(s["w_in"], 16)

        def body(n, half, b, b_next, more, more2):
            sp.wait_ge(s["x1_done"], n + 1)
            sp.dma_start(x1y_v[n][:, :, 0], x1y[:, :, 0]).then_inc(s["stored"], 16)
            if more2:
                sp.dma_start(xin[:, half], x_v[n + 2]).then_inc(s[f"x_in{half}"], 16)
            for which in (0, 1):
                sp.wait_ge(s["lo_done"], n * 4 + (3, 5)[which])
                for part, buf in ((0, hi), (1, lo)):
                    sp.dma_start(qk_v[which, part, b, :, :, half * HT:(half + 1) * HT],
                                 buf[:, 2 * which:2 * which + 2, :].bitcast(f32)).then_inc(s["stored"], 16)
            sp.wait_ge(s["y_done"], n + 1)
            sp.dma_start(x1y_v[n][:, :, 1], x1y[:, :, 1]).then_inc(s["stored"], 16)
            sp.wait_ge(s["v_done"], n + 2)
            sp.dma_start(v_d[b, :, :, half * T:(half + 1) * T, :].rearrange("a p t e -> p a (t e)"), v_s[:].rearrange("p a t e -> p a (t e)")).then_inc(s["stored"], 16)
            sp.wait_ge(s["stored"], n * 112 + 112)
            sp.sem_inc(s["store_free"], 1)
        rounds(sp, body)

    @block.scalar
    def _(act):
        A = nc.scalar

        def input(f):
            act.wait_ge(s["xT_ps"], f + 1)
            A.copy(xT[:], p_f[:, 0:2]).then_inc(s["xT_done"], 1)

        def gate_q_k(f):
            act.wait_ge(s["z_ps"], f + 1)
            A.activation(za[:], p_f[:, 2, :], ACT.Abs, bias=bgk_s[:, 0:1]).then_inc(s["za_done"], 1)
            act.wait_ge(s["za_done"], f + 1)
            A.activation(e_in[:], za[:], ACT.Exp, scale=-1.0).then_inc(s["e_z"], 1)
            act.wait_ge(s["e_z"], f + 1)
            A.activation(za[:], e_in[:], ACT.Ln, bias=ones[:, 0:1]).then_inc(s["l_z"], 1)
            act.wait_ge(s["q_ps"], f + 1)
            A.copy(q_s[:], p_f[:, 0, :]).then_inc(s["q_done"], 1)
            act.wait_ge(s["k_ps"], f + 1)
            A.copy(k_s[:], p_f[:, 1, :]).then_inc(s["k_done"], 1)

        def values_and_gate(f, r, tiles):
            for t in tiles:
                act.wait_ge(s["vg_ps"], f * T + (t + 1))
                A.copy(V[:, t], p_f[:, VG_BANK[t], 0:D])
                A.activation(G[r][:, t], p_f[:, VG_BANK[t], D:2 * D], ACT.Silu).then_inc(s["vg_taken"], 1)

        def decays(f):
            act.wait_ge(s["tail_done"], f + 1)
            A.activation(e_out[:], rel[:], ACT.Exp, scale=-1.0)
            A.activation(e_in[:], rel[:], ACT.Exp).then_inc(s["exps_rel"], 1)
            A.activation(e_tail[:], tail[:], ACT.Exp).then_inc(s["exps_tail"], 1)
            A.activation(e_cum[:], cum[:], ACT.Exp)
            A.activation(decay[:], cum[:].rearrange("p (c j) -> p c j", j=C)[:, :, C - 1], ACT.Exp).then_inc(s["exps"], 1)

        def keys(f):
            act.wait_ge(s["khT_ps"], f + 1)
            A.copy(khat[:], p_f[:, 3].rearrange("p (t c) -> p t c", t=T)).then_inc(s["khat_done"], 1)

        def states(f):
            act.wait_ge(s["S_step"], f * NC + NC)
            for h in range(H):
                last = A.copy(Sbd[h * DK:(h + 1) * DK, :, h * DV:(h + 1) * DV], S[h * DK:(h + 1) * DK, 0:NC, :])
            last.then_inc(s["Sbd_done"], 1)

        input(0)
        gate_q_k(0)
        decays(0)
        values_and_gate(0, 0, range(T))
        keys(0)
        states(0)

        def body(n, half, b, b_next, more, more2):
            n1 = n + 1
            if more:
                input(n + 1)
            act.wait_ge(s["o_ps"], n1)
            A.activation(o2[:].rearrange("p t d -> p (t d)"), p_g[:, 0:2].rearrange("p a c -> p (a c)"), ACT.Square, scale=DV ** -0.5).then_inc(s["o2_done"], 1)
            A.copy(o_s[:].rearrange("p t d -> p (t d)"), p_g[:, 0:2].rearrange("p a c -> p (a c)")).then_inc(s["o_s_done"], 1)
            if more:
                gate_q_k(n + 1)
                values_and_gate(n + 1, 1 - half, range(T))
            act.wait_ge(s["ogT_ps"], n1)
            A.mul(ogT[:], p_g[:, 2:4], rmsw_s[:, 0:1]).then_inc(s["ogT_done"], 1)
            if more:
                decays(n + 1)
                keys(n + 1)
            for k in range(2):
                act.wait_ge(s["xrT_ps"], n * 2 + (k + 1))
                A.mul(xrT[:, k], p_g[:, 2 + k], ln1w_s[:, k:k + 1]).then_inc(s["xrT_done"], 1)
            act.wait_ge(s["store_free"], n1)
            for j in range(4):
                act.wait_ge(s["qk2_ps"], n * 4 + (j + 1))
                A.copy(hi[:, j], p_g[:, j]).then_inc(s["hi_done"], 1)
                if j == 1 and more:
                    states(n + 1)
            act.wait_ge(s["v2_ps"], n1)
            for t in range(T):
                last = A.copy(v_s[:, :, t, :].rearrange("p a (h e) -> p a h e", h=2)[:, :, :, 0:16],
                              p_g[:, t // 2, (t % 2) * D:(t % 2 + 1) * D].rearrange("p (a h e) -> p a h e", a=8, h=2))
            last.then_inc(s["v_done"], 1)
        rounds(act, body)

    @block.vector
    def _(dve):
        V_ = nc.vector
        V_.memset(ones[:], 1.0)
        V_.memset(keep[:], 1.0).then_inc(s["consts0"], 1)
        dve.wait_ge(s["consts0"], 2)
        V_.memset(keep[:].rearrange("p (c j) -> p c j", j=C)[:, :, 0:1], 0.0)
        V_.tensor_copy(maski[:], mask[:]).then_inc(s["consts"], 1)
        dve.wait_ge(s["consts"], 1)
        def input_low(f):
            dve.wait_ge(s["xT_done"], f + 1)
            V_.tensor_tensor(xTl[:], p_f[:, 0:2], xT[:].bitcast(f32), ALU.subtract).then_inc(s["xTl_done"], 1)

        def statistics(f, r, b):
            dve.wait_ge(s[f"x_in{r}"], b * 16 + 16)
            for t in range(T):
                last = V_.bn_stats(st6[:, t], xin[:, r, t])
            last.then_inc(s["st_done"], 1)
            dve.wait_ge(s["st_done"], f + 1)
            dve.sem_inc(s["dve_turn"], 1)
            for t in range(T):
                last = V_.bn_aggr(mv[:, t], st6[:, t])
            last.then_inc(s["mv_done"], 1)

        def normalise(f, r):
            dve.wait_ge(s["rstd_done"], f + 1)
            for t in range(T):
                last = V_.tensor_scalar(xn[:, t], xin[:, r, t], mv[:, t, 0:1], rstd[:, t:t + 1], ALU.subtract, ALU.mult)
            last.then_inc(s["xn_done"], 1)

        def gate_minimum(f):
            dve.wait_ge(s["z_ps"], f + 1)
            dve.wait_ge(s["za_done"], f + 1)
            V_.tensor_scalar(zm[:], p_f[:, 2, :], bgk_s[:, 0:1], 0.0, ALU.add, ALU.min).then_inc(s["zm_done"], 1)

        def running_sums(f):
            dve.wait_ge(s["l_z"], f + 1)
            dve.wait_ge(s["zm_done"], f + 1)
            V_.tensor_tensor(zm[:], zm[:], za[:], ALU.subtract).then_inc(s["g0"], 1)
            dve.wait_ge(s["g0"], f + 1)
            V_.tensor_scalar(zm[:], zm[:], 1.0 / 16.0, -3.0, ALU.mult, ALU.max).then_inc(s["g1"], 1)
            dve.wait_ge(s["g1"], f + 1)
            V_.tensor_tensor_scan(cum[:], keep[:], zm[:], 0.0, ALU.mult, ALU.add).then_inc(s["cum_done"], 1)
            dve.wait_ge(s["cum_done"], f + 1)
            cc = cum[:].rearrange("p (c j) -> p c j", j=C)
            V_.tensor_tensor(rel[:].rearrange("p (c j) -> p c j", j=C), cc,
                             cc[:, :, C // 2 - 1:C // 2].to_broadcast([P, NC, C]), ALU.subtract)
            V_.tensor_tensor(tail[:].rearrange("p (c j) -> p c j", j=C),
                             cc[:, :, C - 1:C].to_broadcast([P, NC, C]), cc, ALU.subtract).then_inc(s["tail_done"], 1)

        def decayed(f):
            dve.wait_ge(s["q_done"], f + 1)
            dve.wait_ge(s["k_done"], f + 1)
            dve.wait_ge(s["exps_rel"], f + 1)
            V_.tensor_tensor(kt[:], k_s[:], e_out[:], ALU.mult)
            for h in range(H):
                rows = slice(h * DK, (h + 1) * DK)
                last = V_.tensor_tensor(qz[rows, :, h, :], q_s[rows, :].rearrange("p (t c) -> p t c", t=T),
                                        e_in[rows, :].rearrange("p (t c) -> p t c", t=T), ALU.mult)
            last.then_inc(s["qtkt"], 1)

        def within_chunks(f):
            for t in range(T):
                dve.wait_ge(s["AT_ps"], f * T + (t + 1))
                dve.sem_inc(s["dve_turn"], 1)
                V_.copy_predicated(AT[:, t].rearrange("p h c -> p (h c)"), maski[:], p_f[:, t]).then_inc(s["AT_done"], 1)

        def states(f, half, chunks):
            dve.wait_ge(s["inc_ps"], f + 1)
            for c in chunks:
                if c > 0:
                    dve.wait_ge(s["S_step"], f * NC + c)
                elif half == 1:
                    dve.wait_ge(s["S_carry"], f + 1)
                else:
                    V_.memset(S[:, 0], 0.0).then_inc(s["S_carry"], 1)
                    dve.wait_ge(s["S_carry"], f + 1)
                V_.scalar_tensor_tensor(S[:, c + 1], S[:, c], decay[:, c:c + 1], p_f[:, c % 4, (c // 4) * DV:(c // 4 + 1) * DV],
                                        ALU.mult, ALU.add).then_inc(s["S_step"], 1)

        def carry(f, half):
            if half == 0:
                dve.wait_ge(s["Sbd_done"], f + 1)
                V_.tensor_copy(S[:, 0], S[:, NC]).then_inc(s["S_carry"], 1)

        statistics(0, 0, 0)
        normalise(0, 0)
        for j in range(3):
            dve.wait_ge(s["wT_ps"], j + 1)
            out = [w[:, j].rearrange("p k m -> p (k m)") for w in wT]
            V_.tensor_copy(out[0], p_g[:, j]).then_inc(s["wT_hi"], 1)
            dve.wait_ge(s["wT_hi"], j + 1)
            V_.tensor_tensor(out[1], p_g[:, j], out[0].bitcast(f32), ALU.subtract).then_inc(s["wT_done"], 1)
        dve.wait_ge(s["gk_ps"], 1)
        V_.tensor_copy(Wgk1T[:], p_g[0:16, 3, 0:D]).then_inc(s["gk1T_done"], 1)
        dve.wait_ge(s["gk_ps"], 2)
        V_.tensor_copy(front_raw[:, :, 0:128], p_g[:, 3, 0:D].rearrange("p (k m) -> p k m", k=2)).then_inc(s["raw_done"], 1)
        dve.wait_ge(s["raw_done"], 1)
        V_.tensor_copy(W_f[0][:], front_raw).then_inc(s["front_hi"], 1)
        dve.wait_ge(s["front_hi"], 1)
        V_.tensor_tensor(W_f[1][:], front_raw, W_f[0][:].bitcast(f32), ALU.subtract).then_inc(s["front_done"], 1)
        dve.sem_inc(s["store_free"], 1)
        dve.sem_inc(s["lo_done"], 1)
        dve.sem_inc(s["v_done"], 1)
        input_low(0)
        gate_minimum(0)
        running_sums(0)
        statistics(1, 1, 0)
        dve.wait_ge(s["filled"], 1)
        decayed(0)
        dve.wait_ge(s["front_done"], 1)
        V_.memset(Sbd[:], 0.0)
        within_chunks(0)
        states(0, 0, range(NC))
        normalise(1, 1)
        carry(0, 0)

        def body(n, half, b, b_next, more, more2):
            n1 = n + 1
            if more:
                input_low(n + 1)
            dve.wait_ge(s["o2_done"], n1)
            V_.reduce_sum(ss[:], o2[:].rearrange("p t (h v) -> p (t h) v", h=H), AX.X).then_inc(s["ss_done"], 1)
            if more:
                gate_minimum(n + 1)
            dve.wait_ge(s["rs_done"], n1)
            dve.wait_ge(s["o_s_done"], n1)
            ov = o_s[:].rearrange("p t (h v) -> p (t h) v", h=H)
            V_.tensor_tensor(ov, ov, rs[:].rearrange("p (a o) -> p a o", o=1).to_broadcast([P, T * H, DV]), ALU.mult).then_inc(s["on_done"], 1)
            dve.wait_ge(s["on_done"], n1)
            V_.tensor_tensor(o_s[:], o_s[:], G[half][:], ALU.mult).then_inc(s["og_done"], 1)
            if more:
                running_sums(n + 1)
                decayed(n + 1)
            dve.wait_ge(s["wout_ps"], n1)
            dve.wait_ge(s["store_free"], n1)
            V_.tensor_tensor(x1y[:, :, 0], p_g[:, 0:2].rearrange("p a (e c) -> p (a e) c", e=2), xin[:, half], ALU.add).then_inc(s["x1_done"], 1)
            dve.wait_ge(s["x1_done"], n1)
            for t in range(T):
                last = V_.bn_stats(st6b[:, t], x1y[:, t, 0])
            last.then_inc(s["stb_done"], 1)
            dve.wait_ge(s["stb_done"], n1)
            dve.sem_inc(s["dve_turn"], 1)
            for t in range(T):
                last = V_.bn_aggr(mvb[:, t], st6b[:, t])
            last.then_inc(s["mvb_done"], 1)
            if more:
                within_chunks(n + 1)
            dve.wait_ge(s["roots_done"], n1)
            for t in range(T):
                last = V_.tensor_scalar(xr[:, t], x1y[:, t, 0], mvb[:, t, 0:1], roots[:, 1, t:t + 1], ALU.subtract, ALU.mult)
            last.then_inc(s["xr_done"], 1)
            if more:
                states(n + 1, 1 - half, range(NC // 2))
            for k in range(2):
                dve.wait_ge(s["xrT_done"], n * 2 + (k + 1))
                V_.scalar_tensor_tensor(xrTl[:, k], p_g[:, 2 + k], ln1w_s[:, k:k + 1], xrT[:, k].bitcast(f32), ALU.mult, ALU.subtract).then_inc(s["xrTl_done"], 1)
            if more:
                states(n + 1, 1 - half, range(NC // 2, NC))
            if more2:
                statistics(n + 2, half, b + 1)
            for j in (0, 1):
                dve.wait_ge(s["hi_done"], n * 4 + (j + 1))
                V_.tensor_tensor(lo[:, j], p_g[:, j], hi[:, j].bitcast(f32), ALU.subtract).then_inc(s["lo_done"], 1)
            if more2:
                normalise(n + 2, half)
            for j in (2, 3):
                dve.wait_ge(s["hi_done"], n * 4 + (j + 1))
                V_.tensor_tensor(lo[:, j], p_g[:, j], hi[:, j].bitcast(f32), ALU.subtract).then_inc(s["lo_done"], 1)
            for t in range(T):
                last = V_.tensor_scalar(x1y[:, t, 1], x1y[:, t, 0], mvb[:, t, 0:1], roots[:, 0, t:t + 1], ALU.subtract, ALU.mult)
            last.then_inc(s["y_done"], 1)
            if more:
                carry(n + 1, 1 - half)
        rounds(dve, body)

    @block.gpsimd
    def _(pool):
        g = nc.gpsimd
        g.memset(ident[:], 0.0)
        g.memset(mhalf[:], -0.5)
        g.memset(mask[:], 1.0).then_inc(s["zero"], 1)
        pool.wait_ge(s["zero"], 1)
        g.affine_select(out=ident[:], in_=ident[:], compare_op=ALU.not_equal, fill=1.0, base=0, pattern=[[-1, P]], channel_multiplier=1)
        m4 = mask[:].rearrange("p (t c j) -> p t c j", c=4, j=C)
        g.affine_select(out=m4, in_=m4, compare_op=ALU.is_ge, fill=0.0, base=0, pattern=[[0, T], [-C, 4], [0, C]], channel_multiplier=1).then_inc(s["zero"], 1)
        pool.wait_ge(s["zero"], 2)
        g.affine_select(out=m4, in_=m4, compare_op=ALU.is_ge, fill=0.0, base=0, pattern=[[0, T], [C, 4], [1, C]], channel_multiplier=-1).then_inc(s["consts0"], 1)
        g.memset(qz[:], 0.0)
        g.memset(AT[:], 0.0)
        g.memset(v_s[:], 1.0).then_inc(s["filled"], 1)

        def inverse_root(out, src, width, ready, count, eps_done, done, times):
            pool.wait_ge(s[ready], count)
            pool.sem_inc(s["pool_turn"], 1)
            g.tensor_scalar(out, src, EPS, None, ALU.add).then_inc(s[eps_done], 1)
            pool.wait_ge(s[eps_done], times)
            g.tensor_tensor(out, out, mhalf[:, 0:width], ALU.pow).then_inc(s[done], 1)

        def front_root(f):
            inverse_root(rstd[:], mv[:, :, 1], T, "mv_done", f + 1, "rstd_eps", "rstd_done", f + 1)

        def hats(f):
            pool.wait_ge(s["q_done"], f + 1)
            pool.wait_ge(s["k_done"], f + 1)
            pool.wait_ge(s["exps_tail"], f + 1)
            g.tensor_tensor(kh[:], k_s[:], e_tail[:], ALU.mult).then_inc(s["hats"], 1)
            pool.wait_ge(s["exps"], f + 1)
            g.tensor_tensor(qh[:], q_s[:], e_cum[:], ALU.mult).then_inc(s["hats"], 1)

        front_root(0)
        front_root(1)
        hats(0)

        def body(n, half, b, b_next, more, more2):
            inverse_root(rs[:], ss[:], T * H, "ss_done", n + 1, "rs_eps", "rs_done", n + 1)
            if more:
                hats(n + 1)
            pool.wait_ge(s["mvb_done"], n + 1)
            pool.sem_inc(s["pool_turn"], 1)
            g.tensor_scalar(roots[:, 0], mvb[:, :, 1], EPS, None, ALU.add)
            g.tensor_scalar(roots[:, 1], mvb[:, :, 1], 1.0 + EPS, EPS * EPS, ALU.mult, ALU.add).then_inc(s["roots_eps"], 1)
            pool.wait_ge(s["roots_eps"], n + 1)
            g.tensor_tensor(roots[:].rearrange("p a t -> p (a t)"), roots[:].rearrange("p a t -> p (a t)"), mhalf[:, 0:2 * T], ALU.pow).then_inc(s["roots_done"], 1)
            if more2:
                front_root(n + 2)
        rounds(pool, body)

    @block.tensor
    def _(pe):
        mm, tr = nc.tensor.matmul, nc.tensor.transpose
        pe.wait_ge(s["w_in"], 14 * 16)
        pe.wait_ge(s["consts"], 1)
        for j in range(3):
            for k in range(2):
                for m in range(2):
                    last = tr(p_g[:, j, k * D + m * P:k * D + (m + 1) * P], w_raw[:, j, m, k * P:(k + 1) * P], ident[:])
            last.then_inc(s["wT_ps"], 1)
        pe.wait_ge(s["wT_done"], 3)

        for k in range(2):
            last = tr(p_g[0:16, 3, k * P:(k + 1) * P], Wgk1_s[:, k, :], ident[:])
        last.then_inc(s["gk_ps"], 1)
        pe.wait_ge(s["gk1T_done"], 1)
        for k in range(2):
            last = mm(p_g[:, 3, k * P:(k + 1) * P], Wgk1T[:, k * P:(k + 1) * P], Wgk2_s[:], start=True, stop=True)
        last.then_inc(s["gk_ps"], 1)
        pe.wait_ge(s["front_done"], 1)

        def product(out, wide, x, w, low_ready=None):
            terms = [(0, 0, 0), (0, 0, 1), (0, 1, 0), (0, 1, 1), (1, 0, 0), (1, 0, 1)]
            for i, (px, pw, k) in enumerate(terms):
                if i == 4 and low_ready:
                    pe.wait_ge(*low_ready)
                a, b = (x(px, k), w(pw, k)) if wide else (w(pw, k), x(px, k))
                last = mm(out, a, b, start=(i == 0), stop=(i == 5))
            return last

        def transposes(dst, src, done, each=False):
            for k in range(2):
                for t in range(T):
                    last = tr(dst[:, k, t * P:(t + 1) * P], src[:, t, k * P:(k + 1) * P], ident[:])
                if k or each:
                    last.then_inc(done, 1)

        def input_transposes(f):
            pe.wait_ge(s["xn_done"], f + 1)
            transposes(p_f[:, 0:2], xn, s["xT_ps"])

        def projections(f):
            pe.wait_ge(s["xT_done"], f + 1)
            for bank, name, done in ((2, "z", "z_ps"), (0, "q", "q_ps"), (1, "k", "k_ps")):
                product(p_f[:, bank, :], False, lambda part, k: (xT, xTl)[part][:, k, :], lambda part, k: W_f[part][:, k, COLUMNS[name]],
                        (s["xTl_done"], f + 1) if name == "z" else None).then_inc(s[done], 1)
            for t in range(T):
                if t > 0:
                    pe.wait_ge(s[("zm_done", "q_done", "k_done")[t - 1]], f + 1)
                product(p_f[:, VG_BANK[t], :], True, lambda part, k: (xT, xTl)[part][:, k, t * P:(t + 1) * P],
                        lambda part, k: W_f[part][:, k, COLUMNS["vg"]]).then_inc(s["vg_ps"], 1)

        def key_transposes(f):
            pe.wait_ge(s["vg_taken"], f * T + 1)
            pe.wait_ge(s["hats"], f * 2 + 1)
            for t in range(T):
                last = tr(p_f[:, 3, t * P:(t + 1) * P], kh[:, t * P:(t + 1) * P], ident[:])
            last.then_inc(s["khT_ps"], 1)

        def chunks(f):
            pe.wait_ge(s["vg_taken"], f * T + T)
            pe.wait_ge(s["qtkt"], f + 1)
            for t in range(T):
                if t == 3:
                    pe.wait_ge(s["khat_done"], f + 1)
                mm(p_f[:, t], kt[:, t * P:(t + 1) * P], qz[:, t].rearrange("p h c -> p (h c)"), start=True, stop=True).then_inc(s["AT_ps"], 1)
            for c in range(4):
                pe.wait_ge(s["AT_done"], f * T + (c + 1))
                pe.sem_inc(s["pe_turn"], 1)
                for t in range(T):
                    for h in range(H):
                        rows = slice(c * C, (c + 1) * C)
                        last = mm(p_f[h * DK:(h + 1) * DK, c, t * DV:(t + 1) * DV], khat[rows, t, h * DK:(h + 1) * DK],
                                  V[rows, t, h * DV:(h + 1) * DV], start=True, stop=True)
            last.then_inc(s["inc_ps"], 1)

        input_transposes(0)
        projections(0)
        key_transposes(0)
        chunks(0)

        def body(n, half, b, b_next, more, more2):
            n1 = n + 1
            pe.wait_ge(s["Sbd_done"], n1)
            pe.wait_ge(s["hats"], n * 2 + 2)
            if more:
                input_transposes(n + 1)
            pe.wait_ge(s["v_done"], n1)
            for t in range(T):
                bank, at = t // 2, (t % 2) * D
                for c in range(4):
                    mm(p_g[c * C:(c + 1) * C, bank, at:at + D], qh[:, t * P + c * C:t * P + (c + 1) * C], Sbd[:, t * 4 + c, :],
                       start=True, stop=False, skip_group_check=True)
                for h in range(H):
                    last = mm(p_g[:, bank, at + h * DV:at + (h + 1) * DV], AT[:, t, h, :], V[:, t, h * DV:(h + 1) * DV],
                              start=False, stop=True, skip_group_check=True)
            last.then_inc(s["o_ps"], 1)
            if more:
                projections(n + 1)
            pe.wait_ge(s["og_done"], n1)
            pe.wait_ge(s["lo_done"], n * 4 + 1)
            transposes(p_g[:, 2:4], o_s, s["ogT_ps"])
            pe.wait_ge(s["ogT_done"], n1)
            for t in range(T):
                bank, at = t // 2, (t % 2) * D
                for k in range(2):
                    last = mm(p_g[:, bank, at:at + D], ogT[:, k, t * P:(t + 1) * P], Wout_s[:, k, :], start=(k == 0), stop=(k == 1))
            last.then_inc(s["wout_ps"], 1)
            if more:
                key_transposes(n + 1)
                chunks(n + 1)
            pe.wait_ge(s["xr_done"], n1)
            transposes(p_g[:, 2:4], xr, s["xrT_ps"], each=True)
            for j in range(4):
                if j == 0:
                    pe.wait_ge(s["xrT_done"], n * 2 + 2)
                product(p_g[:, j, :], False, lambda part, k: (xrT, xrTl)[part][:, k, :],
                        lambda part, k: wT[part][:, j // 2, k, (j % 2) * P:(j % 2 + 1) * P],
                        (s["xrTl_done"], n * 2 + 2) if j == 0 else None).then_inc(s["qk2_ps"], 1)
            pe.wait_ge(s["lo_done"], n * 4 + 3)
            for t in range(T):
                bank, at = t // 2, (t % 2) * D
                last = product(p_g[:, bank, at:at + D], True, lambda part, k: (xrT, xrTl)[part][:, k, t * P:(t + 1) * P],
                               lambda part, k: wT[part][:, 2, k, :])
            last.then_inc(s["v2_ps"], 1)
        rounds(pe, body)


def softmax_attention(nc, ctx, qk_d, v_d, o_d, n_batches=8):
    P, N, KT = 128, 1024, 8
    R = 64
    RING = 4
    PAIRS = 8 * n_batches
    f32, f32r = mybir.dt.float32, mybir.dt.float32r
    ALU, ACT, AX = mybir.AluOpType, mybir.ActivationFunctionType, mybir.AxisListType
    SCALE = 0.25

    def sb(name, shape, dt=f32):
        return ctx.enter_context(nc.sbuf_tensor("b_" + name, shape, dt))

    def sem(name):
        return stage_semaphore(nc, ctx, "b_" + name)

    qst = [sb(f"qst{r}", [P, N], f32r) for r in range(RING)]
    kst = [[sb(f"kst{r}_{h}", [P, N], f32r) for h in range(2)] for r in range(RING)]
    vst = [sb(f"vst{r}", [P, KT, 2, 32]) for r in range(RING)]
    ones, zrow = sb("ones", [2, N]), sb("zrow", [2, N])
    ident = sb("ident", [P, P])
    mxq = [sb(f"mxq{r}", [P, 16]) for r in range(2)]
    nm_hi, nm_lo = [sb(f"nm_hi{r}", [16, P], f32r) for r in range(2)], [sb(f"nm_lo{r}", [16, P], f32r) for r in range(2)]
    probs = [sb(f"probs{r}", [P, N]) for r in range(4)]
    oT = sb("oT", [P, 512])
    rden = sb("rden", [P, 4, 4])
    o_s = [sb(f"o_s{r}", [P, KT, 2, 16]) for r in range(2)]
    p_e = [ctx.enter_context(nc.psum_tensor(f"b_p_e{r}", [P, 512], f32)) for r in range(2)]
    p_m = [ctx.enter_context(nc.psum_tensor(f"b_p_m{r}", [P, N], f32)) for r in range(2)]
    p_o = ctx.enter_context(nc.psum_tensor("b_p_o", [P, 512], f32))
    p_t = ctx.enter_context(nc.psum_tensor("b_p_t", [P, 4, P], f32))

    names = ("q_zero", "k_zero", "ident0", "id", *(f"rows{r}" for r in range(RING)), "m_ps", "m_red", "mT_ps", "mT_read", "nm_done",
             "e_ps", "e_done", "pv_done", "oT_done", "oT_ps", "rden_done", "o_done", "o_stored", "o_free",
             *(f"q_in{r}" for r in range(RING)), *(f"m_in{r}" for r in range(RING)), "start")
    s = {n: sem(n) for n in names}
    q_rows = qk_d.rearrange("w c (g r) t -> g w c r t", r=32)
    v_rows = v_d.rearrange("b a p t e -> (b a) p (t e)")
    o_rows = o_d.rearrange("b a p t e -> (b a) p (t e)")
    LOADS = 15
    STEPS = PAIRS // RING
    MT_AT, OT_AT = 1, 2
    NEG_AT = 4 * MT_AT + 3

    def pairs(eng, body):
        with eng.Fori(0, STEPS - 1) as i:
            for r in range(RING):
                body(i * RING + r, i, r, True, True, True)
        for r in range(RING):
            body((STEPS - 1) * RING + r, STEPS - 1, r, r < RING - 1, r < RING - 2, r < RING - 3)

    def ahead(i, r):
        return (i + 1, r - 2) if r >= 2 else (i, r + 2)

    block = ctx.enter_context(nc.Block())

    @block.sync
    def _(sp):
        def load(pair, r):
            for h in range(2):
                at, row = R * h, 16 * h
                sp.dma_start(qst[r][at:at + 16, :].bitcast(f32), q_rows[pair, 0, 0, row:row + 16, :]).then_inc(s[f"q_in{r}"], 16)
                sp.dma_start(qst[r][at + 16:at + 32, :].bitcast(f32), q_rows[pair, 0, 1, row:row + 16, :]).then_inc(s[f"q_in{r}"], 16)
                sp.dma_start(qst[r][at + 32:at + 48, :].bitcast(f32), q_rows[pair, 0, 0, row:row + 16, :]).then_inc(s[f"q_in{r}"], 16)
                sp.dma_start(kst[r][h][at:at + 16, :].bitcast(f32), q_rows[pair, 1, 0, row:row + 16, :]).then_inc(s[f"q_in{r}"], 16)
                sp.dma_start(kst[r][h][at + 16:at + 32, :].bitcast(f32), q_rows[pair, 1, 0, row:row + 16, :]).then_inc(s[f"q_in{r}"], 16)
                sp.dma_start(kst[r][h][at + 32:at + 48, :].bitcast(f32), q_rows[pair, 1, 1, row:row + 16, :]).then_inc(s[f"q_in{r}"], 16)
                sp.dma_start(qst[r][at + 48:at + 50, :].bitcast(f32), zrow[:]).then_inc(s[f"q_in{r}"], 16)
            sp.dma_start(vst[r][:].rearrange("p t h e -> p (t h e)"), v_rows[pair]).then_inc(s[f"q_in{r}"], 16)

        def maxima(pair, half, r):
            sp.wait_ge(s["nm_done"], pair + 1)
            for h in range(2):
                for k, nm in enumerate((nm_hi[half], nm_lo[half])):
                    sp.dma_start(qst[r][R * h + 48 + k:R * h + 49 + k, :].bitcast(f32).rearrange("o (c j) -> o c j", c=8),
                                 nm[8 * h:8 * h + 8, :].bitcast(f32)).then_inc(s[f"m_in{r}"], 16)

        for r in range(RING):
            sp.wait_ge(s["k_zero"], r + 1)
            sp.wait_ge(s["q_zero"], r + 1)
            for h in range(2):
                sp.dma_start(kst[r][h][R * h + 48:R * h + 50, :].bitcast(f32), ones[:]).then_inc(s[f"rows{r}"], 16)
            if r < 3:
                load(r, r)
        maxima(0, 0, 0)

        def body(pair, i, r, more1, more, more3):
            if more1:
                maxima(pair + 1, (r + 1) % 2, (r + 1) % RING)
            if more3:
                sp.wait_ge(s["pv_done"], pair * KT + 2)
                load(pair + 3, (r + 3) % RING)
        pairs(sp, body)

    @block.scalar
    def _(act):
        def negated(pair, half):
            act.wait_ge(s["mT_ps"], pair + 1)
            nc.scalar.mul(nm_hi[half][:], p_t[0:16, 0, :], -1.0).then_inc(s["mT_read"], 1)

        negated(0, 0)

        def body(pair, i, r, more1, more, more3):
            for e in range(4 * KT):
                act.wait_ge(s["e_ps"], pair * 32 + (e + 1))
                if e % 2 == 0:
                    act.wait_ge(s["pv_done"], pair * KT + (e // 4 + 1))
                nc.scalar.activation(probs[e // 2 % 4][:, (e % 2) * 512:(e % 2 + 1) * 512], p_e[e % 2][:], ACT.Exp, scale=SCALE).then_inc(s["e_done"], 1)
                if e == NEG_AT and more1:
                    negated(pair + 1, (r + 1) % 2)
        pairs(act, body)

    @block.gpsimd
    def _(pool):
        g = nc.gpsimd
        for r in range(RING):
            g.memset(qst[r][:].bitcast(f32), 0.0).then_inc(s["q_zero"], 1)
        g.memset(ident[:], 0.0).then_inc(s["ident0"], 1)
        pool.wait_ge(s["ident0"], 1)
        g.affine_select(out=ident[:], in_=ident[:], compare_op=ALU.not_equal, fill=1.0, base=0, pattern=[[-1, P]], channel_multiplier=1).then_inc(s["id"], 1)

        def body(pair, i, r, more1, more, more3):
            pool.wait_ge(s["o_done"], pair + 3)
            g.dma_start(o_rows[pair], o_s[r % 2][:].rearrange("p t h e -> p (t h e)")).then_inc(s["o_stored"], 16)
            pool.wait_ge(s["o_stored"], pair * 16 + 16)
            pool.sem_inc(s["o_free"], 1)
        pairs(pool, body)

    @block.vector
    def _(dve):
        V_ = nc.vector
        V_.memset(ones[:], 1.0)
        V_.memset(zrow[:], 0.0)
        for r in range(RING):
            for h in range(2):
                i = V_.memset(kst[r][h][:].bitcast(f32), 0.0)
            i.then_inc(s["k_zero"], 1)
        V_.memset(vst[RING - 1][:], 1.0)
        V_.memset(probs[2][:], 1.0)
        V_.memset(probs[3][:], 1.0).then_inc(s["start"], 1)
        dve.sem_inc(s["pv_done"], 1)
        dve.sem_inc(s["e_done"], 2)
        dve.sem_inc(s["m_red"], 2)
        dve.sem_inc(s["o_free"], 3)
        dve.sem_inc(s["o_done"], 1)

        def reduce(pair, half, j):
            dve.wait_ge(s["m_ps"], pair * 32 + (2 * j + 2))
            V_.reduce_max(mxq[half][:, j:j + 1], p_m[j % 2][:], AX.X).then_inc(s["m_red"], 1)

        def low_part(pair, half):
            dve.wait_ge(s["mT_read"], pair + 1)
            V_.scalar_tensor_tensor(nm_lo[half][:], p_t[0:16, 0, :], -1.0, nm_hi[half][:].bitcast(f32), ALU.mult, ALU.subtract).then_inc(s["nm_done"], 1)

        for pair in range(2):
            for j in range(16):
                reduce(pair, pair, j)
            if pair == 0:
                low_part(0, 0)

        def evacuate(n):
            dve.wait_ge(s["pv_done"], n * KT + 2)
            V_.tensor_copy(oT[:], p_o[:]).then_inc(s["oT_done"], 1)

        def normalise(n, half):
            dve.wait_ge(s["oT_ps"], n + 1)
            ot = p_t[:].rearrange("p q (h a e) -> p q h a e", h=2, a=2)
            V_.reciprocal(rden[:].rearrange("p q (h a) -> p q h a", h=2), ot[:, :, :, :, 16]).then_inc(s["rden_done"], 1)
            dve.wait_ge(s["rden_done"], n + 1)
            dve.wait_ge(s["o_free"], n + 1)
            for a in range(2):
                last = V_.tensor_tensor(o_s[half][:, a * 4:a * 4 + 4], ot[:, :, :, a, 0:16],
                                        rden[:].rearrange("p q (h a o) -> p q h a o", h=2, o=1)[:, :, :, a].to_broadcast([P, 4, 2, 16]), ALU.mult)
            last.then_inc(s["o_done"], 1)

        def body(pair, i, r, more1, more, more3):
            for j in range(16):
                if j == 0:
                    evacuate(pair)
                if j == 4 and more1:
                    low_part(pair + 1, (r + 1) % 2)
                if j == 8:
                    normalise(pair, (r + 1) % 2)
                if more:
                    reduce(pair + 2, r % 2, j)
        pairs(dve, body)
        evacuate(PAIRS)
        normalise(PAIRS, 1)

    @block.tensor
    def _(pe):
        mm, tr = nc.tensor.matmul, nc.tensor.transpose
        pe.wait_ge(s["id"], 1)
        pe.wait_ge(s["start"], 1)
        def max_half(pair, r, half):
            j, kh = half // 2, half % 2
            h, qt = j // 8, j % 8
            if kh == 0:
                pe.wait_ge(s["m_red"], pair * 16 + (j + 1))
            mm(p_m[j % 2][:, kh * 512:(kh + 1) * 512], qst[r][:, qt * P:(qt + 1) * P], kst[r][h][:, kh * 512:(kh + 1) * 512], start=True, stop=True).then_inc(s["m_ps"], 1)

        def max_scores(pair, r, j):
            for kh in range(2):
                max_half(pair, r, 2 * j + kh)

        def max_transpose(pair, half):
            pe.wait_ge(s["m_red"], pair * 16 + 18)
            if not isinstance(pair, int) or pair > 0:
                pe.wait_ge(s["o_done"], pair)
            tr(p_t[0:16, 0, :], mxq[half][:], ident[:]).then_inc(s["mT_ps"], 1)

        def output_transpose(n):
            pe.wait_ge(s["nm_done"], n + 2 if not isinstance(n, int) else min(n + 2, PAIRS))
            pe.wait_ge(s["oT_done"], n + 1)
            pe.wait_ge(s["o_done"], n + 1)
            for q in range(4):
                last = tr(p_t[:, q, :], oT[:, q * P:(q + 1) * P], ident[:])
            last.then_inc(s["oT_ps"], 1)

        def loaded(r, i):
            pe.wait_ge(s[f"q_in{r}"], i * (16 * LOADS) + 16 * LOADS)

        def values(pair, r, kt):
            pe.wait_ge(s["e_done"], pair * 32 + (4 * kt + 6))
            for h in range(2):
                for a in range(2):
                    last = mm(p_o[32 * (2 * h + a):32 * (2 * h + a) + 32, :], vst[r if kt >= 0 else (r - 1) % RING][:, kt % KT, h, :],
                              probs[(2 * kt + h) % 4][:, a * 512:(a + 1) * 512], start=(kt == 0), stop=(kt == -1))
            last.then_inc(s["pv_done"], 1)

        for pair in range(2):
            loaded(pair, 0)
            for r in range(RING) if pair else (0,):
                pe.wait_ge(s[f"rows{r}"], 32)
            for j in range(16):
                max_scores(pair, pair, j)
            if pair == 0:
                max_transpose(0, 0)

        for g in range(4):
            mm(p_o[32 * g:32 * g + 32, :], vst[RING - 1][:, 0, 0, :], probs[2][:, 0:512], start=True, stop=False)

        def body(pair, i, r, more1, more, more3):
            i2, r2 = ahead(i, r)
            pe.wait_ge(s[f"m_in{r}"], i * 64 + 64)

            if more:
                loaded(r2, i2)
            def scores(kt, e):
                h, a = e // 2, e % 2
                pe.wait_ge(s["e_done"], pair * 32 + (4 * kt + e + 1))
                mm(p_e[a][:], kst[r][h][:, kt * P:(kt + 1) * P], qst[r][:, a * 512:(a + 1) * 512], start=True, stop=True).then_inc(s["e_ps"], 1)

            for kt in range(KT):
                scores(kt, 0)
                if kt > 0 and more:
                    max_half(pair + 2, r2, 4 * kt - 1)
                scores(kt, 1)
                if kt == 0:
                    values(pair, r, -1)
                else:
                    if kt == 1:
                        pe.wait_ge(s["oT_done"], pair + 1)
                    values(pair, r, kt - 1)
                scores(kt, 2)
                scores(kt, 3)
                if more:
                    for m in range(4 * kt, 4 * kt + 3 + (kt == KT - 1)):
                        max_half(pair + 2, r2, m)
                if kt == MT_AT and more1:
                    max_transpose(pair + 1, (r + 1) % 2)
                if kt == OT_AT:
                    output_transpose(pair)
        pairs(pe, body)
        values(PAIRS, 0, -1)
        output_transpose(PAIRS)


def output_projection_and_gate(nc, ctx, o_d, x1y_d, wo, gate_w, ln2_w, base_d, xg_d, chosen, share, n_batches=8):
    P, D, T, NE = 128, 256, 4, 8
    HT = P * T
    EPS = 1e-5
    f32 = mybir.dt.float32
    ALU, ACT, AX = mybir.AluOpType, mybir.ActivationFunctionType, mybir.AxisListType

    def sb(name, shape, dt=f32):
        return ctx.enter_context(nc.sbuf_tensor("c_" + name, shape, dt))

    wo_raw, woT = sb("wo_raw", [P, 2, D]), sb("woT", [P, 2, D])
    gw_raw, gwT = sb("gw_raw", [NE, D]), sb("gwT", [P, 2, NE])
    ln2 = sb("ln2", [P, 2])
    ident, mhalf = sb("ident", [P, P]), sb("mhalf", [P, T])
    oin, xy = [sb(f"oin{r}", [P, 8, T, 32]) for r in range(2)], [sb(f"xy{r}", [P, T, 2, D]) for r in range(2)]
    orow = [sb(f"orow{r}", [P, T, 8, 32]) for r in range(2)]
    oT, xgT = [sb(f"oT{r}", [P, 2, HT]) for r in range(2)], sb("xgT", [P, 2, HT])
    h = sb("h", [P, T, D])
    base, xg = [sb(f"base{r}", [P, T, D]) for r in range(2)], [sb(f"xg{r}", [P, T, D]) for r in range(2)]
    sq, ms, r_s = sb("sq", [P, D]), sb("ms", [P, T]), sb("r_s", [P, T])
    lg, top, tidx = sb("lg", [P, T, NE]), sb("top", [P, T, 8]), sb("tidx", [P, T, 8], mybir.dt.uint32)
    NT = 2 * n_batches * T
    best = sb("best", [P, NT, 2])
    diff, ed, den = sb("diff", [P, NT]), sb("ed", [P, NT]), sb("den", [P, NT])
    p1, p2, p3 = (ctx.enter_context(nc.psum_tensor(f"c_p{i}", [P, 2, 512], f32)) for i in (1, 2, 3))
    p4 = ctx.enter_context(nc.psum_tensor("c_p4", [P, T, NE], f32))
    names = ("w_in", "zero", "consts", "wT_ps", "wT_done", "in0", "in1", "oin0", "oin1", "orow_done", "in_free", "oT_ps", "oT_done", "h_ps", "h_done", "ms_done",
             "ms_eps", "r_done", "xg_done", "base_done", "st0", "st1", "xgT_ps", "xgT_done", "lg_ps", "lg_done", "top_done", "tidx_done",
             "diff_done", "ed_done", "den_done", "rec_done", "copied", "dve_turn", "pool_turn")
    s = {n: stage_semaphore(nc, ctx, "c_" + n) for n in names}
    x1y_v = x1y_d.rearrange("(n t p) e d -> n p t e d", p=P, t=T)
    base_v, xg_v = (d.rearrange("(n t p) d -> n p t d", p=P, t=T) for d in (base_d, xg_d))
    block = ctx.enter_context(nc.Block())

    def halves(eng, body):
        body(0, 0, 0, 0, False, True)
        body(1, 1, 0, 1, True, n_batches > 1)
        if n_batches > 2:
            with eng.Fori(1, n_batches - 1) as b:
                body(b * 2, 0, b, b, True, True)
                body(b * 2 + 1, 1, b, b + 1, True, True)
        if n_batches > 1:
            b = n_batches - 1
            body(b * 2, 0, b, b, True, True)
            body(b * 2 + 1, 1, b, b + 1, True, False)

    @block.sync
    def _(sp):
        sp.dma_start(wo_raw[:], wo.rearrange("(k p) n -> p k n", p=P)).then_inc(s["w_in"], 16)
        sp.dma_start(gw_raw[:], gate_w).then_inc(s["w_in"], 16)
        with nc.allow_non_contiguous_dma("256 weights, once"):
            sp.dma_start(ln2[:], ln2_w.rearrange("(k p) -> p k", p=P)).then_inc(s["w_in"], 16)

        def load_output(n, half, b):
            sp.dma_start(oin[half][:].rearrange("p a t e -> p a (t e)"),
                         o_d[b, :, :, half * T:(half + 1) * T, :].rearrange("a p t e -> p a (t e)")).then_inc(s[f"oin{half}"], 16)

        load_output(0, 0, 0)

        def body(n, half, b, b_next, before, after):
            if after:
                if before:
                    sp.wait_ge(s["orow_done"], n)
                load_output(n + 1, 1 - half, b_next)
            sp.wait_ge(s["in_free"], n + 1)
            sp.dma_start(xy[half][:], x1y_v[n]).then_inc(s[f"in{half}"], 16)
        halves(sp, body)

    @block.gpsimd
    def _(pool):
        g = nc.gpsimd
        g.memset(ident[:], 0.0)
        g.memset(mhalf[:], -0.5).then_inc(s["zero"], 1)
        pool.wait_ge(s["zero"], 1)
        g.affine_select(out=ident[:], in_=ident[:], compare_op=ALU.not_equal, fill=1.0, base=0, pattern=[[-1, P]], channel_multiplier=1).then_inc(s["consts"], 1)

        def body(n, half, b, b_next, before, after):
            n1 = n + 1
            pool.wait_ge(s["ms_done"], n * T + (T + 1))
            pool.sem_inc(s["pool_turn"], 1)
            g.tensor_scalar(r_s[:], ms[:], EPS, None, ALU.add).then_inc(s["ms_eps"], 1)
            pool.wait_ge(s["ms_eps"], n1)
            g.tensor_tensor(r_s[:], r_s[:], mhalf[:], ALU.pow).then_inc(s["r_done"], 1)
        halves(pool, body)

    @block.scalar
    def _(act):
        act.wait_ge(s["w_in"], 48)

        def gather_features(n, half, b):
            act.wait_ge(s[f"oin{half}"], b * 16 + 16)
            nc.scalar.copy(orow[half][:].rearrange("p t a e -> p a t e"), oin[half][:]).then_inc(s["orow_done"], 1)

        def transposed(n, half):
            act.wait_ge(s["oT_ps"], n + 1)
            nc.scalar.copy(oT[half][:], p1[:]).then_inc(s["oT_done"], 1)

        def router_input(n):
            act.wait_ge(s["xgT_ps"], n + 1)
            nc.scalar.mul(xgT[:, 0], p3[:, 0], ln2[:, 0:1])
            nc.scalar.mul(xgT[:, 1], p3[:, 1], ln2[:, 1:2]).then_inc(s["xgT_done"], 1)

        def store(n, half):
            act.wait_ge(s["base_done"], n + 1)
            act.wait_ge(s["xg_done"], n + 1)
            act.dma_start(base_v[n], base[half][:]).then_inc(s[f"st{half}"], 16)
            act.dma_start(xg_v[n], xg[half][:]).then_inc(s[f"st{half}"], 16)

        gather_features(0, 0, 0)
        transposed(0, 0)

        def body(n, half, b, b_next, before, after):
            n1 = n + 1
            if after:
                gather_features(n + 1, 1 - half, b_next)
            if before:
                router_input(n - 1)
                store(n - 1, 1 - half)
            if after:
                transposed(n + 1, 1 - half)
            act.wait_ge(s["h_done"], n1)
            for t in range(T):
                act.wait_ge(s["ms_done"], n * T + (t + 1))
                nc.scalar.activation(sq[:], h[:, t], ACT.Square, scale=D ** -0.5, accum_out=ms[:, t:t + 1]).then_inc(s["ms_done"], 1)
        halves(act, body)
        router_input(2 * n_batches - 1)
        store(2 * n_batches - 1, 1)
        for half in (0, 1):
            act.wait_ge(s[f"st{half}"], 32 * n_batches)
        act.wait_ge(s["diff_done"], 1)
        nc.scalar.activation(ed[:], diff[:], ACT.Exp).then_inc(s["ed_done"], 1)

    @block.vector
    def _(dve):
        V_ = nc.vector
        for n, c in (("in_free", 2), ("ms_done", 1)):
            dve.sem_inc(s[n], c)
        dve.wait_ge(s["wT_ps"], 1)
        V_.tensor_copy(woT[:].rearrange("p k m -> p (k m)"), p1[:, 0])
        V_.tensor_copy(gwT[:].rearrange("p k m -> p (k m)"), p1[:, 1, 0:2 * NE]).then_inc(s["wT_done"], 1)

        def choose(n):
            dve.wait_ge(s["lg_ps"], n + 1)
            V_.tensor_copy(lg[:], p4[:]).then_inc(s["lg_done"], 1)
            dve.wait_ge(s["lg_done"], n + 1)
            dve.sem_inc(s["dve_turn"], 1)
            for t in range(T):
                i = V_.max(top[:, t], lg[:, t])
            i.then_inc(s["top_done"], 1)
            dve.wait_ge(s["top_done"], n + 1)
            dve.sem_inc(s["dve_turn"], 1)
            for t in range(T):
                i = V_.max_index(tidx[:, t], top[:, t], lg[:, t])
            i.then_inc(s["tidx_done"], 1)
            V_.tensor_copy(best[:, bass.ds(n * T, T), :], top[:, :, 0:2])
            dve.wait_ge(s["tidx_done"], n + 1)
            V_.tensor_copy(chosen[:, bass.ds(n * T, T), :], tidx[:, :, 0:2]).then_inc(s["copied"], 1)

        def body(n, half, b, b_next, before, after):
            n1 = n + 1
            dve.wait_ge(s[f"in{half}"], b * 16 + 16)
            dve.wait_ge(s["h_ps"], n1)
            if before:
                dve.wait_ge(s["xg_done"], n)
            V_.tensor_tensor(h[:], p2[:].rearrange("p a (e c) -> p (a e) c", e=2), xy[half][:, :, 1], ALU.add).then_inc(s["h_done"], 1)
            dve.wait_ge(s["h_done"], n1)
            if not isinstance(b, int) or b > 0:
                dve.wait_ge(s[f"st{half}"], b * 32)
            V_.tensor_tensor(base[half][:], h[:], xy[half][:, :, 0], ALU.add).then_inc(s["base_done"], 1)
            dve.wait_ge(s["base_done"], n1)
            dve.sem_inc(s["in_free"], 1)
            if before:
                choose(n - 1)
            dve.wait_ge(s["r_done"], n1)
            for t in range(T):
                i = V_.tensor_scalar(xg[half][:, t], h[:, t], r_s[:, t:t + 1], None, ALU.mult)
            i.then_inc(s["xg_done"], 1)
        halves(dve, body)
        choose(2 * n_batches - 1)
        dve.wait_ge(s["copied"], 2 * n_batches)
        V_.tensor_tensor(diff[:], best[:, :, 1], best[:, :, 0], ALU.subtract).then_inc(s["diff_done"], 1)
        dve.wait_ge(s["ed_done"], 1)
        V_.tensor_scalar(den[:], ed[:], 1.0, None, ALU.add).then_inc(s["den_done"], 1)
        dve.wait_ge(s["den_done"], 1)
        V_.reciprocal(share[:, :, 0], den[:]).then_inc(s["rec_done"], 1)
        dve.wait_ge(s["rec_done"], 1)
        V_.tensor_tensor(share[:, :, 1], ed[:], share[:, :, 0], ALU.mult)

    @block.tensor
    def _(pe):
        mm, tr = nc.tensor.matmul, nc.tensor.transpose
        pe.wait_ge(s["w_in"], 48)
        pe.wait_ge(s["consts"], 1)
        for k in range(2):
            for m in range(2):
                tr(p1[:, 0, k * D + m * P:k * D + (m + 1) * P], wo_raw[:, m, k * P:(k + 1) * P], ident[:])
            i = tr(p1[:, 1, k * NE:(k + 1) * NE], gw_raw[:, k * P:(k + 1) * P], ident[0:NE, 0:NE])
        i.then_inc(s["wT_ps"], 1)
        pe.wait_ge(s["wT_done"], 1)

        def output_transposes(n, half):
            pe.wait_ge(s["orow_done"], n + 1)
            for t in range(T):
                for k in range(2):
                    i = tr(p1[:, k, t * P:(t + 1) * P], orow[half][:, t, 4 * k:4 * k + 4, :].rearrange("p a e -> p (a e)"), ident[:])
            i.then_inc(s["oT_ps"], 1)

        def router_transposes(n, half):
            pe.wait_ge(s["xg_done"], n + 1)
            for t in range(T):
                for k in range(2):
                    i = tr(p3[:, k, t * P:(t + 1) * P], xg[half][:, t, k * P:(k + 1) * P], ident[:])
            i.then_inc(s["xgT_ps"], 1)

        def router(n):
            pe.wait_ge(s["xgT_done"], n + 1)
            for t in range(T):
                for k in range(2):
                    i = mm(p4[:, t, :], xgT[:, k, t * P:(t + 1) * P], gwT[:, k, :], start=(k == 0), stop=(k == 1))
            i.then_inc(s["lg_ps"], 1)

        output_transposes(0, 0)

        def body(n, half, b, b_next, before, after):
            n1 = n + 1
            pe.wait_ge(s["oT_done"], n1)
            if before:
                pe.wait_ge(s["h_done"], n)
            for t in range(T):
                for k in range(2):
                    i = mm(p2[:, t // 2, (t % 2) * D:(t % 2 + 1) * D], oT[half][:, k, t * P:(t + 1) * P], woT[:, k, :], start=(k == 0), stop=(k == 1))
            i.then_inc(s["h_ps"], 1)
            if before:
                router_transposes(n - 1, 1 - half)
            if after:
                output_transposes(n + 1, 1 - half)
            if before:
                router(n - 1)
        halves(pe, body)
        router_transposes(2 * n_batches - 1, 1)
        router(2 * n_batches - 1)


def route_and_transpose_weights(nc, ctx, chosen, token_of, code_of, expert_of, w1, w3, w2, up_hi, up_lo, w2T, NT, TILES):
    P, D, I, NE = 128, 256, 512, 8
    C2 = 2 * NT
    f32, i32 = mybir.dt.float32, mybir.dt.int32
    ALU, AX = mybir.AluOpType, mybir.AxisListType

    def sb(name, shape, dt=f32):
        return ctx.enter_context(nc.sbuf_tensor("r_" + name, shape, dt))

    ones, before = sb("ones", [P, P]), sb("before", [P, P])
    WIDE = max(P, TILES)
    iota_i, iota = sb("iota_i", [P, WIDE], i32), sb("iota", [P, WIDE])
    lane_i, lane = sb("lane_i", [P, 1], i32), sb("lane", [P, 1])
    val_i, val = sb("val_i", [P, C2], i32), sb("val", [P, C2])
    E = sb("E", [P, C2, NE])
    tot_where, cum = sb("tot_where", [P, NE * C2]), sb("cum", [P, NE, C2])
    tot, where = tot_where[:].rearrange("p (e c) -> p e c", e=NE), tot_where[:].rearrange("p (c e) -> p c e", e=NE)
    full, full_i, tiles, end = sb("full", [P, NE]), sb("full_i", [P, NE], i32), sb("tiles", [P, NE]), sb("end", [P, NE])
    begin = sb("begin", [P, NE])
    slot, slot_i = sb("slot", [P, C2]), sb("slot_i", [P, C2], i32)
    lo_i, hi_i, lo, hi = sb("lo_i", [P, C2], i32), sb("hi_i", [P, C2], i32), sb("lo", [P, C2]), sb("hi", [P, C2])
    cmp, ex = sb("cmp", [P, TILES, NE]), sb("ex", [P, TILES])
    is_lo = [sb(f"is_lo{r}", [P, P]) for r in range(4)]
    is_hi = [sb(f"is_hi{r}", [P, TILES]) for r in range(4)]
    inv, invm, empty = sb("inv", [P, TILES]), sb("invm", [P, TILES]), sb("empty", [P, TILES])
    inv_i = sb("inv_i", [P, TILES], i32)
    raw = [sb(f"raw{j}", [P, 1024]) for j in range(3)]
    ident = sb("ident", [P, P])
    W = C2 * NE // 2
    p_before = ctx.enter_context(nc.psum_tensor("r_p_before", [P, 2, 512], f32))
    p_total = ctx.enter_context(nc.psum_tensor("r_p_total", [P, 2, 512], f32))
    p_inv = ctx.enter_context(nc.psum_tensor("r_p_inv", [P, TILES], f32))
    p_w = [ctx.enter_context(nc.psum_tensor(f"r_p_w{r}", [P, 512], f32)) for r in range(2)]
    s = {n: stage_semaphore(nc, ctx, "r_" + n) for n in ("pool0", "pool", "dve", "E_done", "ps", "hot", "inv_ps", "raw_in0", "raw_in1", "raw_in2", "wT_ps", "wT_done")}
    block = ctx.enter_context(nc.Block())

    @block.sync
    def _(sp):
        for e in range(NE):
            for j, src in enumerate((w1[e].rearrange("(a p) d -> p a d", p=P), w3[e].rearrange("(a p) d -> p a d", p=P), w2[e].rearrange("(a p) i -> p a i", p=P))):
                n = e * 3 + j
                if e > 0:
                    sp.wait_ge(s["wT_ps"], 2 * (n - 2))
                sp.dma_start(raw[j][:].rearrange("p (a d) -> p a d", a=src.shape[1]), src).then_inc(s[f"raw_in{j}"], 16)

    @block.scalar
    def _(act):
        for e in range(NE):
            for j in range(6):
                act.wait_ge(s["wT_ps"], e * 6 + j + 1)
                dst = up_hi[:, e, j // 2, j % 2] if j < 4 else w2T[:, e, 2 * j - 8:2 * j - 6].rearrange("p a n -> p (a n)")
                if j < 4:
                    nc.scalar.copy(up_lo[:, e, j // 2, j % 2].bitcast(f32), p_w[j % 2][:])
                nc.scalar.copy(dst, p_w[j % 2][:]).then_inc(s["wT_done"], 1)

    @block.gpsimd
    def _(pool):
        g = nc.gpsimd
        g.memset(before[:], 1.0)
        g.memset(ident[:], 0.0)
        g.iota(iota_i[:], [[1, WIDE]], base=0, channel_multiplier=0)
        g.iota(lane_i[:], [[1, 1]], base=0, channel_multiplier=1)
        g.iota(val_i[:], [[2 * P, NT], [1, 2]], base=1, channel_multiplier=2).then_inc(s["pool0"], 1)
        pool.wait_ge(s["pool0"], 1)
        g.affine_select(out=ident[:], in_=ident[:], compare_op=ALU.not_equal, fill=1.0, base=0, pattern=[[-1, P]], channel_multiplier=1)
        g.affine_select(out=before[:], in_=before[:], compare_op=ALU.is_gt, fill=0.0, base=0, pattern=[[1, P]], channel_multiplier=-1).then_inc(s["pool"], 1)
        for e in range(NE):
            for j in range(4):
                pool.wait_ge(s["wT_done"], e * 6 + j + 1)
                lo = up_lo[:, e, j // 2, j % 2]
                g.tensor_tensor(lo, lo.bitcast(f32), up_hi[:, e, j // 2, j % 2].bitcast(f32), ALU.subtract)

    @block.vector
    def _(dve):
        V_ = nc.vector
        count = [0]

        def then(ins):
            count[0] += 1
            ins.then_inc(s["dve"], 1)
            dve.wait_ge(s["dve"], count[0])

        dve.wait_ge(s["pool"], 1)
        V_.memset(ones[:], 1.0)
        V_.tensor_copy(iota[:], iota_i[:])
        V_.tensor_copy(lane[:], lane_i[:])
        then(V_.tensor_copy(val[:], val_i[:]))
        V_.tensor_tensor(E[:], chosen[:].rearrange("p j (k o) -> p (j k) o", o=1).to_broadcast([P, C2, NE]),
                         iota[:, 0:NE].rearrange("p (o e) -> p o e", o=1).to_broadcast([P, C2, NE]), ALU.is_equal).then_inc(s["E_done"], 1)
        dve.wait_ge(s["ps"], 1)
        for k in range(2):
            i = V_.tensor_copy(tot[:, :, k * NT:(k + 1) * NT], p_total[:, k, 0:W].rearrange("p (c e) -> p e c", e=NE))
        then(i)
        for e in range(NE):
            i = V_.tensor_tensor_scan(cum[:, e, :], ones[:, 0:C2], tot[:, e, :], 0.0, ALU.mult, ALU.add)
        then(i)
        then(V_.tensor_scalar(full[:], cum[:, :, C2 - 1], float(P - 1), None, ALU.add))
        then(V_.tensor_copy(full_i[:], full[:]))
        then(V_.tensor_scalar(full_i[:], full_i[:], 7, None, ALU.arith_shift_right))
        then(V_.tensor_copy(tiles[:], full_i[:]))
        then(V_.tensor_tensor_scan(end[:], ones[:, 0:NE], tiles[:], 0.0, ALU.mult, ALU.add))
        then(V_.tensor_tensor(begin[:], end[:], tiles[:], ALU.subtract))
        then(V_.tensor_scalar(begin[:], begin[:], float(P), None, ALU.mult))
        then(V_.tensor_tensor(cum[:], cum[:], tot[:], ALU.subtract))
        then(V_.tensor_tensor(cum[:], cum[:], begin[:].rearrange("p (e o) -> p e o", o=1).to_broadcast([P, NE, C2]), ALU.add))
        for k in range(2):
            i = V_.tensor_tensor(where[:, k * NT:(k + 1) * NT, :], p_before[:, k, 0:W].rearrange("p (c e) -> p c e", e=NE),
                                 cum[:, :, k * NT:(k + 1) * NT].rearrange("p e c -> p c e"), ALU.add)
        then(i)
        then(V_.tensor_tensor(where[:], where[:], E[:], ALU.mult))
        then(V_.reduce_sum(slot[:], where[:], AX.X))
        then(V_.tensor_copy(slot_i[:], slot[:]))
        V_.tensor_scalar(hi_i[:], slot_i[:], 7, None, ALU.arith_shift_right)
        then(V_.tensor_scalar(lo_i[:], slot_i[:], P - 1, None, ALU.bitwise_and))
        V_.tensor_copy(hi[:], hi_i[:])
        then(V_.tensor_copy(lo[:], lo_i[:]))
        with dve.Fori(0, C2 // 4) as i4:
            for r in range(4):
                c = i4 * 4 + r
                dve.wait_ge(s["inv_ps"], c + 1)
                V_.tensor_scalar(is_lo[r][:], iota[:, 0:P], lo[:, bass.ds(c, 1)], None, ALU.is_equal)
                V_.tensor_scalar(is_hi[r][:], iota[:, 0:TILES], hi[:, bass.ds(c, 1)], val[:, bass.ds(c, 1)], ALU.is_equal, ALU.mult).then_inc(s["hot"], 1)
        V_.tensor_tensor(cmp[:], iota[:, 0:TILES].rearrange("p (m o) -> p m o", o=1).to_broadcast([P, TILES, NE]),
                         end[:].rearrange("p (o e) -> p o e", o=1).to_broadcast([P, TILES, NE]), ALU.is_ge).then_inc(s["dve"], 1)
        count[0] += 1
        dve.wait_ge(s["dve"], count[0])
        then(V_.reduce_sum(ex[:], cmp[:], AX.X))
        then(V_.tensor_scalar(ex[:], ex[:], float(NE - 1), None, ALU.min))
        V_.memset(expert_of[:, 0:1], 0)
        V_.tensor_copy(expert_of[:, 1:TILES + 1], ex[0:1, :])
        dve.wait_ge(s["inv_ps"], C2 + 4)
        then(V_.tensor_copy(inv[:], p_inv[:]))
        V_.tensor_scalar(empty[:], inv[:], 0.0, float(2 * NT * P + 1), ALU.is_equal, ALU.mult)
        then(V_.tensor_scalar(invm[:], inv[:], -1.0, None, ALU.add))
        then(V_.tensor_tensor(inv[:], invm[:], empty[:], ALU.add))
        then(V_.tensor_scalar(empty[:], empty[:], 1.0 / (2 * NT * P + 1), lane[:, 0:1], ALU.mult, ALU.mult))
        then(V_.tensor_tensor(inv[:], inv[:], empty[:], ALU.add))
        V_.tensor_copy(code_of[:], inv[:])
        then(V_.tensor_scalar(invm[:], invm[:], 0.0, None, ALU.max))
        then(V_.tensor_copy(inv_i[:], invm[:]))
        then(V_.tensor_scalar(token_of[:], inv_i[:], 1, None, ALU.arith_shift_right))

    @block.tensor
    def _(pe):
        mm = nc.tensor.matmul
        pe.sem_inc(s["inv_ps"], 4)
        pe.wait_ge(s["E_done"], 1)
        for k in range(2):
            rhs = E[:, k * NT:(k + 1) * NT, :].rearrange("p c e -> p (c e)")
            mm(p_before[:, k, 0:W], before[:], rhs, start=True, stop=True)
            i = mm(p_total[:, k, 0:W], ones[:], rhs, start=True, stop=True)
        i.then_inc(s["ps"], 1)
        def column(c, r, start, stop):
            pe.wait_ge(s["hot"], c + 1)
            mm(p_inv[:], is_lo[r][:], is_hi[r][:], start=start, stop=stop, skip_group_check=True).then_inc(s["inv_ps"], 1)
        def transposes(e, j):
            pe.wait_ge(s[f"raw_in{j}"], e * 16 + 16)
            for half in range(2):
                if j or not isinstance(e, int):
                    pe.wait_ge(s["wT_done"], e * 6 + (2 * j + half - 1))
                for i in range(4):
                    if j < 2:
                        src = raw[j][:].rearrange("p (a d) -> p a d", a=4)[:, i, half * P:(half + 1) * P]
                    else:
                        src = raw[j][:].rearrange("p (a i) -> p a i", a=2)[:, i % 2, (2 * half + i // 2) * P:(2 * half + i // 2 + 1) * P]
                    last = nc.tensor.transpose(p_w[half][:, i * P:(i + 1) * P], src, ident[:])
                last.then_inc(s["wT_ps"], 1)

        per = C2 // NE

        def expert_and_columns(e):
            for j in range(3):
                transposes(e, j)
                for i in range(per * j // 3, per * (j + 1) // 3):
                    column(e * per + i, i % 4, isinstance(e, int) and i == 0, False)
        expert_and_columns(0)
        with pe.Fori(1, NE) as e:
            expert_and_columns(e)


def experts(nc, ctx, xg_d, up_hi, up_lo, w2T, ln2_w, token_of, code_of, expert_of, ys_d, TILES):
    P, D, I, NE = 128, 256, 512, 8
    f32, f32r, i32 = mybir.dt.float32, mybir.dt.float32r, mybir.dt.int32
    ALU, ACT = mybir.AluOpType, mybir.ActivationFunctionType

    def sb(name, shape, dt=f32):
        return ctx.enter_context(nc.sbuf_tensor("d_" + name, shape, dt))

    ln2, ident = sb("ln2", [P, 2]), sb("ident", [P, P])
    tok, code = [sb(f"tok{r}", [P, 1], i32) for r in range(4)], [sb(f"code{r}", [P, 1], i32) for r in range(2)]
    xs = [sb(f"xs{r}", [P, D]) for r in range(4)]
    xh, xl = [sb(f"xh{r}", [P, 2, P], f32r) for r in range(2)], [sb(f"xl{r}", [P, 2, P], f32r) for r in range(2)]
    act_s, h = [sb(f"act{r}", [P, I]) for r in range(2)], [sb(f"h{r}", [P, I]) for r in range(2)]
    hT = [sb(f"hT{r}", [P, 4, P]) for r in range(2)]
    y = [sb(f"y{r}", [P, D]) for r in range(2)]
    p_x = ctx.enter_context(nc.psum_tensor("d_p_x", [P, 4, P], f32))
    p_up = [ctx.enter_context(nc.psum_tensor(f"d_p_up{r}", [P, 2, I], f32)) for r in range(2)]
    p_h = ctx.enter_context(nc.psum_tensor("d_p_h", [P, 4, P], f32))
    p_y = ctx.enter_context(nc.psum_tensor("d_p_y", [P, 512], f32))
    names = ("zero", "id", "tok_done", "turn", *(f"x_in{r}" for r in range(4)), "xT_ps", "xh_done", "xT_done",
             "ln_in", "up_ps", "act_done", "h_done", "hT_ps", "hT_done", "y_ps", "y_done", "code_done", "y_out0", "y_out1", "y_free", "start")
    s = {n: stage_semaphore(nc, ctx, "d_" + n) for n in names}
    block = ctx.enter_context(nc.Block())

    @block.sync
    def _(sp):
        with nc.allow_non_contiguous_dma("256 weights, once"):
            sp.dma_start(ln2[:], ln2_w.rearrange("(k p) -> p k", p=P)).then_inc(s["ln_in"], 16)

    @block.gpsimd
    def _(pool):
        g = nc.gpsimd

        def gather(m, r):
            g.tensor_copy(tok[r][:], token_of[:, bass.ds(m, 1)]).then_inc(s["tok_done"], 1)
            pool.wait_ge(s["tok_done"], m + 1)
            pool.sem_inc(s["turn"], 1)
            g.indirect_dma_start(xs[r][:], None, xg_d, bass.IndirectOffsetOnAxis(ap=tok[r][:, 0:1], axis=0)).then_inc(s[f"x_in{r}"], 16)

        def scatter(m, q, i, previous):
            r = q % 2
            g.tensor_copy(code[r][:], code_of[:, bass.ds(m, 1)]).then_inc(s["code_done"], 1)
            pool.wait_ge(s["code_done"], m + 1)
            if previous:
                pool.wait_ge(s[f"y_out{1 - r}"], i * 32 + (0, 16, 16, 32)[q])
                pool.sem_inc(s["y_free"], 1)
            pool.wait_ge(s["y_done"], m + 3)
            pool.sem_inc(s["turn"], 1)
            g.indirect_dma_start(ys_d, bass.IndirectOffsetOnAxis(ap=code[r][:, 0:1], axis=0), y[r][:], None).then_inc(s[f"y_out{r}"], 16)

        for m in range(3):
            gather(m, m)
        g.memset(ident[:], 0.0).then_inc(s["zero"], 1)
        pool.wait_ge(s["zero"], 1)
        g.affine_select(out=ident[:], in_=ident[:], compare_op=ALU.not_equal, fill=1.0, base=0, pattern=[[-1, P]], channel_multiplier=1).then_inc(s["id"], 1)

        def round(i, first, last):
            for q in range(4):
                m = i * 4 + q
                if not last or q == 0:
                    if not first or q > 0:
                        pool.wait_ge(s["xT_ps"], m)
                    gather(m + 3, (q + 3) % 4)
                scatter(m, q, i, not first or q > 0)
        round(0, True, False)
        with pool.Fori(1, TILES // 4 - 1) as i:
            round(i, False, False)
        round(TILES // 4 - 1, False, True)
        pool.wait_ge(s["y_out1"], 16 * TILES // 2)

    @block.scalar
    def _(act):
        def transposed(m, r):
            act.wait_ge(s["hT_ps"], m + 1)
            nc.scalar.copy(hT[1 - r][:], p_h[:]).then_inc(s["hT_done"], 1)

        with act.Fori(0, TILES // 2) as i:
            for r in (0, 1):
                m = i * 2 + r
                act.wait_ge(s["up_ps"], 2 * m + 1)
                nc.scalar.activation(act_s[r][:], p_up[r][:, 0], ACT.Silu).then_inc(s["act_done"], 1)
                transposed(m, r)
        transposed(TILES, 0)

    @block.vector
    def _(dve):
        V_ = nc.vector
        V_.memset(h[1][:], 0.0).then_inc(s["start"], 1)
        for n, c in (("y_free", 3), ("y_done", 1), ("h_done", 1)):
            dve.sem_inc(s[n], c)
        dve.wait_ge(s["ln_in"], 16)

        def scaled(m, r):
            dve.wait_ge(s["xT_ps"], m + 1)
            for k in range(2):
                last = V_.tensor_scalar(xh[r][:, k], p_x[:, k], ln2[:, k:k + 1], None, ALU.mult)
            last.then_inc(s["xh_done"], 1)
            dve.wait_ge(s["xh_done"], m + 1)
            for k in range(2):
                last = V_.scalar_tensor_tensor(xl[r][:, k], p_x[:, k], ln2[:, k:k + 1], xh[r][:, k].bitcast(f32), ALU.mult, ALU.subtract)
            last.then_inc(s["xT_done"], 1)

        def evacuate(m, r):
            dve.wait_ge(s["y_ps"], m + 1)
            dve.wait_ge(s["y_free"], m + 1)
            V_.tensor_copy(y[1 - r][:], p_y[:, 0:D]).then_inc(s["y_done"], 1)

        scaled(0, 0)

        def tile(m, r, more):
            if more:
                scaled(m + 1, 1 - r)
            dve.wait_ge(s["act_done"], m + 1)
            dve.wait_ge(s["up_ps"], 2 * m + 2)
            V_.tensor_tensor(h[r][:], act_s[r][:], p_up[r][:, 1], ALU.mult).then_inc(s["h_done"], 1)
            evacuate(m, r)
        with dve.Fori(0, TILES // 2 - 1) as i:
            for r in (0, 1):
                tile(i * 2 + r, r, True)
        tile(TILES - 2, 0, True)
        tile(TILES - 1, 1, False)
        evacuate(TILES, 0)

    @block.tensor
    def _(pe):
        mm, tr = nc.tensor.matmul, nc.tensor.transpose
        pe.wait_ge(s["id"], 1)
        pe.wait_ge(s["start"], 1)

        def expert(m):
            return pe.value_load(expert_of[0:1, bass.ds(m + 1, 1)], min_val=0, max_val=NE - 1)

        def input_transposes(q, count):
            pe.wait_ge(s[f"x_in{q}"], count)
            for k in range(2):
                last = tr(p_x[:, k, :], xs[q][:, k * P:(k + 1) * P], ident[:])
            last.then_inc(s["xT_ps"], 1)

        def up(m, r, u, e):
            parts = [(xh, up_hi, 0), (xh, up_lo, 0), (xl, up_hi, 0), (xh, up_hi, 1), (xh, up_lo, 1), (xl, up_hi, 1)]
            for j, (x, w, k) in enumerate(parts):
                last = mm(p_up[r][:, u], x[r][:, k], w[:, bass.ds(e, 1), u, k, :].rearrange("p o n -> p (o n)"), start=(j == 0), stop=(j == 5))
            last.then_inc(s["up_ps"], 1)

        def inner_transposes(m, r):
            pe.wait_ge(s["h_done"], m + 1)
            for k in range(4):
                last = tr(p_h[:, k, :], h[r][:, k * P:(k + 1) * P], ident[:])
            last.then_inc(s["hT_ps"], 1)

        def down(m, r, e):
            pe.wait_ge(s["hT_done"], m + 1)
            pe.wait_ge(s["y_done"], m + 1)
            for k in range(4):
                last = mm(p_y[:, 0:D], hT[r][:, k], w2T[:, bass.ds(e, 1), k, :].rearrange("p o n -> p (o n)"), start=(k == 0), stop=(k == 3))
            last.then_inc(s["y_ps"], 1)

        input_transposes(0, 16)

        def round(i, last):
            for q in range(4):
                m = i * 4 + q
                r = q % 2
                e, e_before = expert(m), expert(m - 1)
                pe.wait_ge(s["xT_done"], m + 1)
                up(m, r, 0, e)
                inner_transposes(m, 1 - r)
                if not last or q < 3:
                    input_transposes((q + 1) % 4, i * 16 + (32 if q == 3 else 16))
                up(m, r, 1, e)
                down(m, 1 - r, e_before)
        with pe.Fori(0, TILES // 4 - 1) as i:
            round(i, False)
        round(TILES // 4 - 1, True)
        inner_transposes(TILES, 1)
        down(TILES, 1, expert(TILES - 1))


def combine(nc, ctx, base_d, ys_d, share, out, NT):
    P, D, T = 128, 256, 4
    RING = 4
    f32 = mybir.dt.float32
    ALU = mybir.AluOpType
    base = [ctx.enter_context(nc.sbuf_tensor(f"e_base{r}", [P, T, D], f32)) for r in range(RING)]
    ys = [ctx.enter_context(nc.sbuf_tensor(f"e_ys{r}", [P, T, 2, D], f32)) for r in range(RING)]
    sh = [ctx.enter_context(nc.sbuf_tensor(f"e_sh{r}", [P, T, 2], f32)) for r in range(RING)]
    names = [f"in{r}" for r in range(RING)] + [f"out{r}" for r in range(RING)] + ["sh_done", "first", "sum"]
    s = {n: stage_semaphore(nc, ctx, "e_" + n) for n in names}
    base_v, out_v = (d.rearrange("(n t p) d -> n p t d", p=P, t=T) for d in (base_d, out))
    ys_v = ys_d[0:2 * NT * P, :].rearrange("(n t p k) d -> n p t k d", p=P, t=T, k=2)
    N = NT // T
    block = ctx.enter_context(nc.Block())

    @block.sync
    def _(sp):
        def load(n, r):
            sp.dma_start(base[r][:], base_v[n]).then_inc(s[f"in{r}"], 16)
            sp.dma_start(ys[r][:], ys_v[n]).then_inc(s[f"in{r}"], 16)
        for r in range(min(RING, N)):
            load(r, r)
        if N > RING:
            with sp.Fori(1, N // RING) as i:
                for r in range(RING):
                    sp.wait_ge(s[f"out{r}"], i * 16)
                    load(i * RING + r, r)

    @block.vector
    def _(dve):
        V_ = nc.vector
        with dve.Fori(0, (N + RING - 1) // RING) as i:
            for r in range(min(RING, N)):
                n = i * RING + r
                V_.tensor_copy(sh[r][:], share[:, bass.ds(n * T, T), :]).then_inc(s["sh_done"], 1)
                dve.wait_ge(s["sh_done"], n + 1)
                dve.wait_ge(s[f"in{r}"], i * 32 + 32)
                for k in range(2):
                    if k:
                        dve.wait_ge(s["first"], n + 1)
                    for t in range(T):
                        last = V_.scalar_tensor_tensor(base[r][:, t], ys[r][:, t, k], sh[r][:, t, k:k + 1], base[r][:, t], ALU.mult, ALU.add)
                    last.then_inc(s["first" if k == 0 else "sum"], 1)

    @block.scalar
    def _(act):
        with act.Fori(0, (N + RING - 1) // RING) as i:
            for r in range(min(RING, N)):
                n = i * RING + r
                act.wait_ge(s["sum"], n + 1)
                act.dma_start(out_v[n], base[r][:]).then_inc(s[f"out{r}"], 16)
        for r in range(min(RING, N)):
            act.wait_ge(s[f"out{r}"], 16 * ((N + RING - 1) // RING))


def layer_kernel(nc, x, Wq, Wk, Wv, Wg, Wgk1, Wgk2, bgk2, Wout, rms_w, ln1_w, ln2_w, wq, wk, wv, wo, gate_w, w1, w2, w3, out):
    B, N, D = x.shape
    P = 128
    NT = B * N // P
    NE = gate_w.shape[0]
    TILES = 2 * NT + NE
    f32, i32 = mybir.dt.float32, mybir.dt.int32
    flat = x.rearrange("b n d -> (b n) d")
    x1y_d = nc.dram_tensor("x1y_d", (B * N, 2, D), f32).ap()
    qk_d = nc.dram_tensor("qk_d", (2, 2, B * D, N), f32).ap()
    v_d = nc.dram_tensor("v_d", (B, 8, P, N // P, 64), f32).ap()
    o_d = nc.dram_tensor("o_d", (B, 8, P, N // P, 32), f32).ap()
    base_d = nc.dram_tensor("base_d", (B * N, D), f32).ap()
    xg_d = nc.dram_tensor("xg_d", (B * N, D), f32).ap()
    ys_d = nc.dram_tensor("ys_d", (2 * B * N + P, D), f32).ap()
    with ExitStack() as ctx:
        def sb(name, shape, dt=f32):
            return ctx.enter_context(nc.sbuf_tensor(name, shape, dt))
        chosen, share = sb("chosen", [P, NT, 2]), sb("share", [P, NT, 2])
        token_of, code_of = sb("token_of", [P, TILES], i32), sb("code_of", [P, TILES], i32)
        expert_of = sb("expert_of", [1, TILES + 1], i32)
        with Stage(nc) as stage:
            gla_and_projections(nc, stage, flat, Wq, Wk, Wv, Wg, Wgk1, Wgk2, bgk2, Wout, rms_w,
                                ln1_w, wq, wk, wv, x1y_d, qk_d, v_d, B)
        with Stage(nc) as stage:
            softmax_attention(nc, stage, qk_d, v_d, o_d, B)
        with Stage(nc) as stage:
            output_projection_and_gate(nc, stage, o_d, x1y_d, wo, gate_w, ln2_w, base_d, xg_d, chosen, share, B)
        with ExitStack() as weights:
            I = w1.shape[1]
            up_hi, up_lo = (weights.enter_context(nc.sbuf_tensor(n, [P, NE, 2, D // P, I], mybir.dt.float32r)) for n in ("up_hi", "up_lo"))
            w2T = weights.enter_context(nc.sbuf_tensor("w2T", [P, NE, I // P, D], f32))
            with Stage(nc) as stage:
                route_and_transpose_weights(nc, stage, chosen, token_of, code_of, expert_of, w1, w3, w2, up_hi, up_lo, w2T, NT, TILES)
            with Stage(nc) as stage:
                experts(nc, stage, xg_d, up_hi, up_lo, w2T, ln2_w, token_of, code_of, expert_of, ys_d, TILES)
        with Stage(nc) as stage:
            combine(nc, stage, base_d, ys_d, share, out.rearrange("b n d -> (b n) d"), NT)


_INS = ["L0_attn_x", "L0_attn_Wq", "L0_attn_Wk", "L0_attn_Wv", "L0_attn_Wg", "L0_attn_Wgk1", "L0_attn_Wgk2",
        "L0_attn_bgk2", "L0_attn_Wout", "L0_attn_rms_w", "L0_ffn_ln1_w", "L0_ffn_ln2_w", "L0_ffn_wq", "L0_ffn_wk",
        "L0_ffn_wv", "L0_ffn_wo", "L0_ffn_gate_w", "L0_ffn_w1", "L0_ffn_w2", "L0_ffn_w3"]
_OUTS = [((8, 1024, 256), "float32")]


def kernel(**inputs):
    import numpy as _np
    import concourse.bacc as _bacc
    from concourse import mybir as _mybir
    from concourse.bass_utils import run_bass_kernel_spmd as _run

    nc = _bacc.Bacc("TRN2", target_bir_lowering=False, num_devices=1)
    arrays, args = {}, []
    for name in _INS:
        a = _np.ascontiguousarray(inputs[name])
        arrays[f"in_{name}_dram"] = a
        args.append(nc.dram_tensor(f"in_{name}_dram", a.shape, _mybir.dt.from_np(a.dtype), kind="ExternalInput").ap())
    for i, (shape, dtype) in enumerate(_OUTS):
        dt = _mybir.dt.from_np(_np.dtype(dtype))
        args.append(nc.dram_tensor(f"out_{i}_dram", shape, dt, kind="ExternalOutput").ap())
    layer_kernel(nc, *args)
    r = _run(nc, [arrays], core_ids=[0])
    got = tuple(r.results[0][f"out_{i}_dram"] for i in range(len(_OUTS)))
    return got[0]
```
